# Optimizing a Trainium2 kernel written in Bass

```python
import numpy as np
import jax
import jax.numpy as jnp

def _softmax(x, axis=-1):
    return jax.nn.softmax(x, axis=axis)

def _gelu(x):
    return jax.nn.gelu(x, approximate=True)

def _silu(x):
    return jax.nn.silu(x)

def _sigmoid(x):
    return jax.nn.sigmoid(x)

def _layernorm(x, axis=-1, eps=1e-05):
    m = jnp.mean(x, axis=axis, keepdims=True)
    v = jnp.var(x, axis=axis, keepdims=True)
    return (x - m) / jnp.sqrt(v + eps)

def _scatter_add(tgt, idx, src, axis=0):
    return tgt.at[idx].add(src)

def _segment_sum(src, seg, n):
    return jax.ops.segment_sum(src, seg, n)
kernel_name = 'mk_adj_resnorm_d2_adj_r2_3f2e95'

def setup_inputs(seed: int=0):
    np.random.seed(seed)
    _w = jnp.asarray

    def _rec_inputs():
        import jax
        import jax.numpy as jnp
        _gk = jax.random.key(seed)
        x = -0.0001538 + 1 * jax.random.normal(jax.random.fold_in(_gk, 1), (64, 128, 384), jnp.float32)
        _a = jax.random.bernoulli(jax.random.fold_in(_gk, 2), 0.03125, (64, 128, 128))
        _af = _a.astype(jnp.float32)
        adj = _af
        return (x, adj)
    x, adj = _rec_inputs()

    def _L0_gnn_setup():
        import jax, jax.numpy as jnp
        import numpy as np
        LN_EPS = 1e-12

        def _digcn_forward(hidden_state, adjacency_matrix, Wl, bl, Ws, bs, Wr, br, ln_w, ln_b):
            B, S, D = hidden_state.shape
            temper = jnp.asarray(D, jnp.float32) ** 0.5
            i = jnp.arange(S)
            upper = (i[None, :] > i[:, None]).astype(hidden_state.dtype)
            lower = (i[None, :] < i[:, None]).astype(hidden_state.dtype)

            def layer(h, params):
                wl, b_l, ws, b_s, wr, b_r, g, beta = params
                u = jnp.einsum('bid,bjd->bij', h, h) / temper
                a = jax.nn.softmax(u, axis=-1)
                delta = a * adjacency_matrix
                attn = delta / (jnp.sum(delta, axis=-1, keepdims=True) + 1e-10)
                hl = h @ wl.T + b_l
                hs = h @ ws.T + b_s
                hr = h @ wr.T + b_r
                diag_a = jnp.diagonal(attn, axis1=1, axis2=2)
                ctx = jnp.einsum('bij,bjd->bid', attn * upper, hl) + diag_a[..., None] * hs + jnp.einsum('bij,bjd->bid', attn * lower, hr)
                mean = ctx.mean(-1, keepdims=True)
                var = ctx.var(-1, keepdims=True)
                o = (ctx - mean) / jnp.sqrt(var + LN_EPS) * g + beta
                return (jax.nn.relu(o), None)
            out, _ = jax.lax.scan(layer, hidden_state, (Wl, bl, Ws, bs, Wr, br, ln_w, ln_b))
            return out
        key = jax.random.key(seed)
        ks = jax.random.split(key, 6)
        B, S, D, L = (8, 512, 384, 2)
        scale = (1.0 / D) ** 0.5
        hidden_state = jax.random.normal(ks[0], (B, S, D), jnp.float32)
        adjacency_matrix = (jax.random.uniform(ks[1], (B, S, S)) < 0.05).astype(jnp.float32)
        Wl = jax.random.normal(ks[2], (L, D, D), jnp.float32) * scale
        Ws = jax.random.normal(ks[3], (L, D, D), jnp.float32) * scale
        Wr = jax.random.normal(ks[4], (L, D, D), jnp.float32) * scale
        bl = jnp.zeros((L, D), jnp.float32)
        bs = jnp.zeros((L, D), jnp.float32)
        br = jnp.zeros((L, D), jnp.float32)
        ln_w = jnp.ones((L, D), jnp.float32)
        ln_b = jnp.zeros((L, D), jnp.float32)
        return dict(hidden_state=hidden_state, adjacency_matrix=adjacency_matrix, Wl=Wl, bl=bl, Ws=Ws, bs=bs, Wr=Wr, br=br, ln_w=ln_w, ln_b=ln_b)
    _L0_gnn_all = _L0_gnn_setup()
    _L0_gnn_in = {k: v for k, v in _L0_gnn_all.items() if k in ('Wl', 'bl', 'Ws', 'bs', 'Wr', 'br', 'ln_w', 'ln_b')}
    del _L0_gnn_all

    def _L1_gnn_setup():
        import jax, jax.numpy as jnp
        import numpy as np
        D_MODEL = 384
        NHEADS = 8
        D_FF = 1536
        B, N = (8, 512)
        EPS = 1e-06

        def _rmsnorm(x, alpha, gamma):
            x = x * jax.lax.rsqrt(jnp.mean(x * x, axis=-1, keepdims=True) + EPS)
            return alpha * x + gamma
        key = jax.random.key(seed)
        ks = jax.random.split(key, 10)
        d, f = (D_MODEL, D_FF)
        s = 1.0 / np.sqrt(d)
        inp = {'x': jax.random.normal(ks[0], (B, N, d), dtype=jnp.float32), 'attn_bias': jax.random.normal(ks[1], (B, N, N), dtype=jnp.float32), 'wq': jax.random.normal(ks[2], (d, d), dtype=jnp.float32) * s, 'bq': jnp.zeros((d,), jnp.float32), 'wk': jax.random.normal(ks[3], (d, d), dtype=jnp.float32) * s, 'bk': jnp.zeros((d,), jnp.float32), 'wv': jax.random.normal(ks[4], (d, d), dtype=jnp.float32) * s, 'bv': jnp.zeros((d,), jnp.float32), 'wo': jax.random.normal(ks[5], (d, d), dtype=jnp.float32) * s, 'bo': jnp.zeros((d,), jnp.float32), 'w1': jax.random.normal(ks[6], (d, f), dtype=jnp.float32) * s, 'b1': jnp.zeros((f,), jnp.float32), 'w2': jax.random.normal(ks[7], (f, d), dtype=jnp.float32) * (1.0 / np.sqrt(f)), 'b2': jnp.zeros((d,), jnp.float32), 'alpha1': jnp.ones((d,), jnp.float32), 'gamma1': jnp.ones((d,), jnp.float32), 'alpha2': jnp.ones((d,), jnp.float32), 'gamma2': jnp.ones((d,), jnp.float32)}
        return inp
    _L1_gnn_all = _L1_gnn_setup()
    _L1_gnn_in = {k: v for k, v in _L1_gnn_all.items() if k in ('wq', 'bq', 'wk', 'bk', 'wv', 'bv', 'wo', 'bo', 'w1', 'b1', 'w2', 'b2', 'alpha1', 'gamma1', 'alpha2', 'gamma2')}
    del _L1_gnn_all
    return {'x': x, 'adj': adj, 'L0_gnn_Wl': _L0_gnn_in['Wl'], 'L0_gnn_bl': _L0_gnn_in['bl'], 'L0_gnn_Ws': _L0_gnn_in['Ws'], 'L0_gnn_bs': _L0_gnn_in['bs'], 'L0_gnn_Wr': _L0_gnn_in['Wr'], 'L0_gnn_br': _L0_gnn_in['br'], 'L0_gnn_ln_w': _L0_gnn_in['ln_w'], 'L0_gnn_ln_b': _L0_gnn_in['ln_b'], 'L1_gnn_wq': _L1_gnn_in['wq'], 'L1_gnn_bq': _L1_gnn_in['bq'], 'L1_gnn_wk': _L1_gnn_in['wk'], 'L1_gnn_bk': _L1_gnn_in['bk'], 'L1_gnn_wv': _L1_gnn_in['wv'], 'L1_gnn_bv': _L1_gnn_in['bv'], 'L1_gnn_wo': _L1_gnn_in['wo'], 'L1_gnn_bo': _L1_gnn_in['bo'], 'L1_gnn_w1': _L1_gnn_in['w1'], 'L1_gnn_b1': _L1_gnn_in['b1'], 'L1_gnn_w2': _L1_gnn_in['w2'], 'L1_gnn_b2': _L1_gnn_in['b2'], 'L1_gnn_alpha1': _L1_gnn_in['alpha1'], 'L1_gnn_gamma1': _L1_gnn_in['gamma1'], 'L1_gnn_alpha2': _L1_gnn_in['alpha2'], 'L1_gnn_gamma2': _L1_gnn_in['gamma2']}

def reference(x, adj, L0_gnn_Wl, L0_gnn_bl, L0_gnn_Ws, L0_gnn_bs, L0_gnn_Wr, L0_gnn_br, L0_gnn_ln_w, L0_gnn_ln_b, L1_gnn_wq, L1_gnn_bq, L1_gnn_wk, L1_gnn_bk, L1_gnn_wv, L1_gnn_bv, L1_gnn_wo, L1_gnn_bo, L1_gnn_w1, L1_gnn_b1, L1_gnn_w2, L1_gnn_b2, L1_gnn_alpha1, L1_gnn_gamma1, L1_gnn_alpha2, L1_gnn_gamma2):
    import jax
    import jax.numpy as jnp

    def _L0_gnn_ref(hidden_state, adjacency_matrix, Wl, bl, Ws, bs, Wr, br, ln_w, ln_b):
        import jax, jax.numpy as jnp
        import numpy as np
        LN_EPS = 1e-12

        def _digcn_forward(hidden_state, adjacency_matrix, Wl, bl, Ws, bs, Wr, br, ln_w, ln_b):
            B, S, D = hidden_state.shape
            temper = jnp.asarray(D, jnp.float32) ** 0.5
            i = jnp.arange(S)
            upper = (i[None, :] > i[:, None]).astype(hidden_state.dtype)
            lower = (i[None, :] < i[:, None]).astype(hidden_state.dtype)

            def layer(h, params):
                wl, b_l, ws, b_s, wr, b_r, g, beta = params
                u = jnp.einsum('bid,bjd->bij', h, h) / temper
                a = jax.nn.softmax(u, axis=-1)
                delta = a * adjacency_matrix
                attn = delta / (jnp.sum(delta, axis=-1, keepdims=True) + 1e-10)
                hl = h @ wl.T + b_l
                hs = h @ ws.T + b_s
                hr = h @ wr.T + b_r
                diag_a = jnp.diagonal(attn, axis1=1, axis2=2)
                ctx = jnp.einsum('bij,bjd->bid', attn * upper, hl) + diag_a[..., None] * hs + jnp.einsum('bij,bjd->bid', attn * lower, hr)
                mean = ctx.mean(-1, keepdims=True)
                var = ctx.var(-1, keepdims=True)
                o = (ctx - mean) / jnp.sqrt(var + LN_EPS) * g + beta
                return (jax.nn.relu(o), None)
            out, _ = jax.lax.scan(layer, hidden_state, (Wl, bl, Ws, bs, Wr, br, ln_w, ln_b))
            return out
        return _digcn_forward(hidden_state, adjacency_matrix, Wl, bl, Ws, bs, Wr, br, ln_w, ln_b)

    def _L1_gnn_ref(x, attn_bias, wq, bq, wk, bk, wv, bv, wo, bo, w1, b1, w2, b2, alpha1, gamma1, alpha2, gamma2):
        import jax, jax.numpy as jnp
        import numpy as np
        D_MODEL = 384
        NHEADS = 8
        D_FF = 1536
        B, N = (8, 512)
        EPS = 1e-06

        def _rmsnorm(x, alpha, gamma):
            x = x * jax.lax.rsqrt(jnp.mean(x * x, axis=-1, keepdims=True) + EPS)
            return alpha * x + gamma
        b, n, d = x.shape
        h = NHEADS
        dh = d // h
        scaling = dh ** (-0.5)

        def split_heads(t):
            return t.reshape(b, n, h, dh).transpose(0, 2, 1, 3)
        q = split_heads(x @ wq + bq)
        k = split_heads(x @ wk + bk)
        v = split_heads(x @ wv + bv)
        scores = jnp.einsum('bhqd,bhkd->bhqk', q, k) * scaling
        scores = scores + attn_bias[:, None, :, :]
        attn = jax.nn.softmax(scores, axis=-1)
        ctx = jnp.einsum('bhij,bhjd->bhid', attn, v)
        ctx = ctx.transpose(0, 2, 1, 3).reshape(b, n, d)
        attn_out = ctx @ wo + bo
        x = _rmsnorm(x + attn_out, alpha1, gamma1)
        ff = jax.nn.silu(x @ w1 + b1) @ w2 + b2
        x = _rmsnorm(x + ff, alpha2, gamma2)
        return x
    x = _layernorm(x + _L0_gnn_ref(x, adj, L0_gnn_Wl, L0_gnn_bl, L0_gnn_Ws, L0_gnn_bs, L0_gnn_Wr, L0_gnn_br, L0_gnn_ln_w, L0_gnn_ln_b), axis=-1)
    x = _layernorm(x + _L1_gnn_ref(x, adj, L1_gnn_wq, L1_gnn_bq, L1_gnn_wk, L1_gnn_bk, L1_gnn_wv, L1_gnn_bv, L1_gnn_wo, L1_gnn_bo, L1_gnn_w1, L1_gnn_b1, L1_gnn_w2, L1_gnn_b2, L1_gnn_alpha1, L1_gnn_gamma1, L1_gnn_alpha2, L1_gnn_gamma2), axis=-1)
    return x

_drawn_inputs = setup_inputs


def setup_inputs(seed=0):
    import zlib

    import numpy as np

    out = dict(_drawn_inputs(seed))
    spreads = {'L0_gnn_bl': (0.0, 0.1),
     'L0_gnn_bs': (0.0, 0.425),
     'L0_gnn_br': (0.0, 0.1),
     'L0_gnn_ln_w': (1.0, 0.2),
     'L0_gnn_ln_b': (0.0, 0.1),
     'L1_gnn_bq': (0.0, 0.8),
     'L1_gnn_bk': (0.0, 0.8),
     'L1_gnn_bv': (0.0, 0.1),
     'L1_gnn_bo': (0.0, 0.1),
     'L1_gnn_b1': (0.0, 0.324),
     'L1_gnn_b2': (0.0, 0.1),
     'L1_gnn_alpha1': (1.0, 0.2),
     'L1_gnn_gamma1': (1.0, 0.2),
     'L1_gnn_alpha2': (1.0, 0.2),
     'L1_gnn_gamma2': (1.0, 0.2)}
    factors = {}
    for name, (base, spread) in spreads.items():
        noise = np.random.default_rng([zlib.crc32(name.encode()), seed]).standard_normal(out[name].shape)
        drawn = base * np.exp(spread * noise) if base else spread * noise
        out[name] = jnp.asarray(drawn.astype(out[name].dtype))
    for name, factor in factors.items():
        out[name] = (out[name] * factor).astype(out[name].dtype)
    return out
```

```python
from contextlib import ExitStack

import concourse.bass as bass
from concourse import mybir

ALU = mybir.AluOpType
ACT = mybir.ActivationFunctionType
AX = mybir.AxisListType
F32 = mybir.dt.float32
F32R = mybir.dt.float32r


def phase_graph_conv(nc, x, adj, w_gcn, b_gcn, ln_gcn, x1, n_batch, S, D):
    KC = D // 128
    N_LAYER = 2
    LN_EPS_GCN = 1e-12
    LN_EPS_OUT = 1e-5
    ATTN_EPS = 1e-10
    TEMPER_INV = float(D) ** -0.5
    RING = 4

    with ExitStack() as ctx:
        def sb(name, shape, dt=F32):
            return ctx.enter_context(nc.sbuf_tensor(name, shape, dt))

        def sem(name):
            return ctx.enter_context(nc.semaphore(name))

        ident = sb("a_ident", [128, 128])
        masks = sb("a_masks", [128, 2, 128])
        neg_row1 = sb("a_neg_row1", [2, 1])
        ones_f = sb("a_ones_f", [128, 128])
        ones = sb("a_ones", [128, 128], F32R)
        exponent = sb("a_exponent", [128, 1])
        w_raw = sb("a_w_raw", [128, KC * 3 * D])
        w_hi = [sb(f"a_w_hi{l}", [128, KC, 3, D], F32R) for l in range(N_LAYER)]
        w_lo = [sb(f"a_w_lo{l}", [128, KC, 3, D], F32R) for l in range(N_LAYER)]
        b_raw = sb("a_b_raw", [2, N_LAYER, 3, D])
        b_hi = sb("a_b_hi", [2, N_LAYER, 3, D], F32R)
        b_rows = sb("a_b_rows", [128, N_LAYER, 3, D], F32R)
        affine = sb("a_affine", [128, N_LAYER, 2, D])
        x_in = [sb(f"a_x_in{s}", [128, D]) for s in range(RING)]
        adj_in = [sb(f"a_adj_in{s}", [128, S]) for s in range(RING)]
        hT_hi = [sb(f"a_hT_hi{l}", [128, KC, 128], F32R) for l in range(N_LAYER)]
        hT_lo = [sb(f"a_hT_lo{l}", [128, KC, 128], F32R) for l in range(N_LAYER)]
        neg_max = sb("a_neg_max", [128, 1])
        exp_bias = sb("a_exp_bias", [128, 1])
        expo = sb("a_expo", [128, S])
        z_sum = sb("a_z_sum", [128, 1])
        e_adj = sb("a_e_adj", [128, S])
        e_sum = sb("a_e_sum", [128, 1])
        denom = sb("a_denom", [128, 1])
        r_den = sb("a_r_den", [128, 1])
        attn = sb("a_attn", [128, 2, S])
        diag_scr = sb("a_diag_scr", [128, S])
        diag = sb("a_diag", [128, 1])
        aT_hi = sb("a_aT_hi", [128, 2, 128], F32R)
        aT_lo = sb("a_aT_lo", [128, 2, 128], F32R)
        hl_hi = sb("a_hl_hi", [128, D], F32R)
        hl_lo = sb("a_hl_lo", [128, D], F32R)
        hr_hi = sb("a_hr_hi", [128, D], F32R)
        hr_lo = sb("a_hr_lo", [128, D], F32R)
        hs_diag = sb("a_hs_diag", [128, D])
        ctx_s = sb("a_ctx_s", [128, D])
        stats = sb("a_stats", [128, 6])
        mv = sb("a_mv", [128, 2])
        var_eps = sb("a_var_eps", [128, 1])
        rstd = sb("a_rstd", [128, 1])
        normed = sb("a_normed", [128, D])
        scaled = sb("a_scaled", [128, D])
        h_nat = sb("a_h_nat", [128, D])
        o_nat = sb("a_o_nat", [128, D])
        y_res = sb("a_y_res", [128, D])
        stats2 = sb("a_stats2", [128, 6])
        mv2 = sb("a_mv2", [128, 2])
        var_eps2 = sb("a_var_eps2", [128, 1])
        rstd2 = sb("a_rstd2", [128, 1])
        filler = sb("a_filler", [128, 1])
        x1_out = [sb(f"a_x1_out{s}", [128, D]) for s in range(2)]

        def bank(name):
            return ctx.enter_context(nc.psum_tensor(name, [128, 512], F32))

        p_u = bank("a_p_u")
        p_aT = bank("a_p_aT")
        p_T = bank("a_p_T")
        p_hl, p_hs, p_hr = bank("a_p_hl"), bank("a_p_hs"), bank("a_p_hr")
        p_ctx = [bank("a_p_ctx0"), bank("a_p_ctx1")]

        s_const = sem("s_const")
        s_wload = sem("s_wload")
        s_wsmall = sem("s_wsmall")
        s_whi = sem("s_whi")
        s_wlo = sem("s_wlo")
        s_bias = sem("s_bias")
        s_in = [sem(f"s_in{s}") for s in range(RING)]
        s_t = sem("s_t")
        s_t_hi = sem("s_t_hi")
        s_t_lo = sem("s_t_lo")
        s_u = sem("s_u")
        s_max = sem("s_max")
        s_bias_exp = sem("s_bias_exp")
        s_exp = sem("s_exp")
        s_ea = sem("s_ea")
        s_den = sem("s_den")
        s_rden = sem("s_rden")
        s_attn = sem("s_attn")
        s_diag = sem("s_diag")
        s_hl = sem("s_hl")
        s_hr = sem("s_hr")
        s_hs = sem("s_hs")
        s_hl_hi = sem("s_hl_hi")
        s_hr_hi = sem("s_hr_hi")
        s_hl_lo = sem("s_hl_lo")
        s_hr_lo = sem("s_hr_lo")
        s_hs_diag = sem("s_hs_diag")
        s_aT = sem("s_aT")
        s_aT_hi = sem("s_aT_hi")
        s_aT_lo = sem("s_aT_lo")
        s_ctx = sem("s_ctx")
        s_ctx_s = sem("s_ctx_s")
        s_stats = sem("s_stats")
        s_mv = sem("s_mv")
        s_var = sem("s_var")
        s_rstd = sem("s_rstd")
        s_normed = sem("s_normed")
        s_scaled = sem("s_scaled")
        s_h = sem("s_h")
        s_o = sem("s_o")
        s_y = sem("s_y")
        s_stats2 = sem("s_stats2")
        s_mv2 = sem("s_mv2")
        s_var2 = sem("s_var2")
        s_rstd2 = sem("s_rstd2")
        s_x1 = sem("s_x1")
        s_store = [sem(f"s_store{s}") for s in range(2)]

        def half_no(i, off, layer):
            if isinstance(i, int) and RING * i + off in (0, n_batch):
                return 0 if i == 0 else 2 * n_batch - 1
            return i * (2 * RING) + (2 * off - 1 + layer)

        def wait(eng, s, value):
            if not isinstance(value, int) or value > 0:
                eng.wait_ge(s, value)

        def steps(eng, half):
            for t in range(RING):
                half(0, t, 0)
                if t > 0:
                    half(0, t, 1)
            with eng.Fori(0, n_batch // RING - 2) as i:
                for off in range(RING, 2 * RING):
                    half(i, off, 0)
                    half(i, off, 1)
            for t in range(n_batch - RING, n_batch):
                half(t // RING, t % RING, 0)
                half(t // RING, t % RING, 1)
            half(n_batch // RING, n_batch % RING, 1)

        def split_products(eng, out, pairs, last_stop=True):
            n = len(pairs)
            for k, ((a_hi, a_lo), (b_hi, b_lo)) in enumerate(pairs):
                eng.matmul(out, a_hi, b_hi, start=(k == 0), stop=False)
                eng.matmul(out, a_hi, b_lo, start=False, stop=False)
                mm = eng.matmul(out, a_lo, b_hi, start=False, stop=(last_stop and k == n - 1))
            return mm

        with nc.Block() as block:

            @block.sync
            def _(sp):
                sp.dma_start(x_in[0][:, :], x[0]).then_inc(s_in[0], 16)
                sp.dma_start(adj_in[0][:, :], adj[0]).then_inc(s_in[0], 16)
                sp.dma_start(w_raw[:, :], w_gcn[0]).then_inc(s_wload, 16)
                sp.dma_start(b_raw[:, :, :, :], b_gcn).then_inc(s_wsmall, 16)
                sp.dma_start(affine[:, :, :, :], ln_gcn).then_inc(s_wsmall, 16)
                for t in range(1, RING):
                    sp.dma_start(x_in[t][:, :], x[t]).then_inc(s_in[t], 16)
                    sp.dma_start(adj_in[t][:, :], adj[t]).then_inc(s_in[t], 16)
                sp.wait_ge(s_wlo, 1)
                sp.dma_start(w_raw[:, :], w_gcn[1]).then_inc(s_wload, 16)
                with sp.Fori(0, n_batch // RING - 1) as i:
                    for slot in range(RING):
                        done = i * RING + slot
                        sp.wait_ge(s_x1, done + 1)
                        sp.dma_start(x1[done], x1_out[slot % 2][:, :]).then_inc(s_store[slot % 2], 16)
                        sp.dma_start(x_in[slot][:, :], x[done + RING]).then_inc(s_in[slot], 16)
                        sp.dma_start(adj_in[slot][:, :], adj[done + RING]).then_inc(s_in[slot], 16)
                for t in range(n_batch - RING, n_batch):
                    sp.wait_ge(s_x1, t + 1)
                    sp.dma_start(x1[t], x1_out[t % 2][:, :]).then_inc(s_store[t % 2], 16)
                for s in range(2):
                    sp.wait_ge(s_store[s], 16 * (n_batch // 2))

            @block.gpsimd
            def _(pool):
                pool.memset(ident[:, :], 0.0).then_inc(s_const, 1)
                pool.memset(masks[:, :, :], 1.0).then_inc(s_const, 1)
                pool.memset(neg_row1[:, :], 0.0).then_inc(s_const, 1)
                pool.memset(ones_f[:, :], 1.0).then_inc(s_const, 1)
                pool.memset(exponent[:, :], -0.5).then_inc(s_const, 1)
                pool.memset(b_rows[:, :, :, :].bitcast(F32), 0.0).then_inc(s_const, 1)
                pool.wait_ge(s_const, 6)
                pool.affine_select(out=ident[:, :], in_=ident[:, :], compare_op=ALU.not_equal, fill=1.0,
                                   base=0, pattern=[[-1, 128]], channel_multiplier=1).then_inc(s_const, 1)
                pool.affine_select(out=masks[:, 0, :], in_=masks[:, 0, :], compare_op=ALU.is_gt, fill=0.0,
                                   base=0, pattern=[[1, 128]], channel_multiplier=-1).then_inc(s_const, 1)
                pool.affine_select(out=masks[:, 1, :], in_=masks[:, 1, :], compare_op=ALU.is_gt, fill=0.0,
                                   base=0, pattern=[[-1, 128]], channel_multiplier=1).then_inc(s_const, 1)
                pool.affine_select(out=neg_row1[:, :], in_=neg_row1[:, :], compare_op=ALU.is_equal, fill=-1.0,
                                   base=0, pattern=[[0, 1]], channel_multiplier=1).then_inc(s_const, 1)

                def norm_tail(q, src, i, off):
                    pool.wait_ge(s_var, q)
                    pool.tensor_tensor(rstd[:, :], var_eps[:, :], exponent[:, :], ALU.pow).then_inc(s_rstd, 1)
                    pool.wait_ge(s_normed, q)
                    pool.tensor_tensor(scaled[:, :], normed[:, :], affine[:, src, 0, :], ALU.mult).then_inc(s_scaled, 1)
                    if src == 0:
                        pool.wait_ge(s_t, q + 1)
                    else:
                        wait(pool, s_y, i * RING + (off - 2))
                    pool.wait_ge(s_scaled, q)
                    dst, done = (h_nat, s_h) if src == 0 else (o_nat, s_o)
                    pool.tensor_tensor(dst[:, :], scaled[:, :], affine[:, src, 1, :], ALU.add).then_inc(done, 1)
                    if src == 1:
                        pool.wait_ge(s_var2, i * RING + (off - 1))
                        pool.tensor_tensor(rstd2[:, :], var_eps2[:, :], exponent[:, :], ALU.pow).then_inc(s_rstd2, 1)

                def half(i, off, layer):
                    q = half_no(i, off, layer)
                    static = isinstance(i, int)
                    if static and q == 0:
                        return
                    last = static and RING * i + off == n_batch
                    src = 0 if static and q == 1 else 1 if last else 1 - layer
                    norm_tail(q, src, i, off)

                pool.wait_ge(s_wsmall, 32)
                steps(pool, half)
                norm_tail(2 * n_batch, 1, n_batch // RING, n_batch % RING + 1)

            @block.scalar
            def _(act):
                act.wait_ge(s_const, 10)
                act.activation(ones[:, :], ones_f[:, :], ACT.Copy).then_inc(s_bias, 1)
                act.wait_ge(s_wsmall, 32)
                act.activation(b_hi[:, :, :, :], b_raw[:, :, :, :], ACT.Copy).then_inc(s_bias, 1)

                def transposed_hi(n, layer_to, relu, free):
                    act.wait_ge(s_t, n + 1)
                    wait(act, s_hs, free)
                    act.activation(hT_hi[layer_to][:, :, :].rearrange("p k n -> p (k n)"), p_T[:, 0:D],
                                   ACT.Relu if relu else ACT.Copy).then_inc(s_t_hi, 1)

                transposed_hi(0, 0, False, 0)
                for l in range(N_LAYER):
                    act.wait_ge(s_wload, 16 * (l + 1))
                    act.activation(w_hi[l][:, :, :, :].rearrange("p k m n -> p (k m n)"), w_raw[:, :],
                                   ACT.Copy).then_inc(s_whi, 1)

                def half(i, off, layer):
                    q = half_no(i, off, layer)
                    first = isinstance(q, int) and q == 0
                    last = isinstance(i, int) and RING * i + off == n_batch
                    no_next = isinstance(i, int) and layer == 1 and RING * i + off == n_batch - 1
                    if last:
                        transposed_hi(q, 1, True, q)
                    act.wait_ge(s_bias_exp, q + 1)
                    wait(act, s_attn, q)
                    act.activation(expo[:, :], p_u[:, 0:S], ACT.Exp, bias=exp_bias[:, 0:1],
                                   scale=TEMPER_INV, accum_out=z_sum[:, 0:1]).then_inc(s_exp, 1)
                    act.wait_ge(s_hl, q + 1)
                    wait(act, s_ctx, q)
                    act.activation(hl_hi[:, :], p_hl[:, 0:D], ACT.Copy).then_inc(s_hl_hi, 1)
                    act.wait_ge(s_hr, q + 1)
                    act.activation(hr_hi[:, :], p_hr[:, 0:D], ACT.Copy).then_inc(s_hr_hi, 1)
                    act.wait_ge(s_aT, q + 1)
                    act.activation(aT_hi[:, :, :].rearrange("p a n -> p (a n)"), p_aT[:, 0:2 * S],
                                   ACT.Copy).then_inc(s_aT_hi, 1)
                    if first:
                        transposed_hi(1, 0, False, 1)
                    elif not (last or no_next):
                        transposed_hi(q + 1, 1 - layer, layer == 0, q)
                    act.wait_ge(s_hs, q + 1)
                    act.wait_ge(s_diag, q + 1)
                    wait(act, s_ctx_s, q)
                    act.activation(hs_diag[:, :], p_hs[:, 0:D], ACT.Copy, scale=diag[:, 0:1]).then_inc(s_hs_diag, 1)

                steps(act, half)

            @block.vector
            def _(dve):
                dve.wait_ge(s_bias, 2)
                dve.scalar_tensor_tensor(out=b_rows[0:2, :, :, :].rearrange("p l m n -> p (l m n)"),
                                         in0=b_hi[:, :, :, :].bitcast(F32).rearrange("p l m n -> p (l m n)"),
                                         scalar=neg_row1[:, 0:1],
                                         in1=b_raw[:, :, :, :].rearrange("p l m n -> p (l m n)"),
                                         op0=ALU.mult, op1=ALU.add).then_inc(s_bias, 1)

                def transposed_lo(n, layer_to, relu):
                    dve.wait_ge(s_t_hi, n + 1)
                    hi = hT_hi[layer_to][:, :, :].bitcast(F32).rearrange("p k n -> p (k n)")
                    lo = hT_lo[layer_to][:, :, :].rearrange("p k n -> p (k n)")
                    if relu:
                        ins = dve.scalar_tensor_tensor(out=lo, in0=p_T[:, 0:D], scalar=0.0, in1=hi,
                                                       op0=ALU.max, op1=ALU.subtract)
                    else:
                        ins = dve.tensor_tensor(lo, p_T[:, 0:D], hi, ALU.subtract)
                    ins.then_inc(s_t_lo, 1)

                transposed_lo(0, 0, False)
                for l in range(N_LAYER):
                    dve.wait_ge(s_whi, l + 1)
                    dve.tensor_tensor(w_lo[l][:, :, :, :].rearrange("p k m n -> p (k m n)"), w_raw[:, :],
                                      w_hi[l][:, :, :, :].bitcast(F32).rearrange("p k m n -> p (k m n)"),
                                      ALU.subtract).then_inc(s_wlo, 1)

                def norm_stats(q, par):
                    dve.wait_ge(s_ctx, q)
                    dve.wait_ge(s_hs_diag, q)
                    dve.tensor_tensor(ctx_s[:, :], p_ctx[par][:, 0:D], hs_diag[:, :], ALU.add).then_inc(s_ctx_s, 1)
                    dve.wait_ge(s_ctx_s, q)
                    dve.bn_stats(stats[:, :], ctx_s[:, :]).then_inc(s_stats, 1)

                def norm_var(q):
                    dve.bn_aggr(mv[:, :], stats[:, :]).then_inc(s_mv, 1)
                    dve.wait_ge(s_mv, q)
                    wait(dve, s_rstd, q - 1)
                    dve.tensor_scalar(var_eps[:, :], mv[:, 1:2], LN_EPS_GCN, None, ALU.add).then_inc(s_var, 1)

                def norm_apply(q):
                    dve.wait_ge(s_rstd, q)
                    wait(dve, s_scaled, q - 1)
                    dve.tensor_scalar(normed[:, :], ctx_s[:, :], mv[:, 0:1], rstd[:, 0:1],
                                      ALU.subtract, ALU.mult).then_inc(s_normed, 1)

                def residual(i, off):
                    n = i * RING + (off - 1)
                    dve.wait_ge(s_o, n)
                    dve.scalar_tensor_tensor(out=y_res[:, :], in0=o_nat[:, :], scalar=0.0,
                                             in1=x_in[(off - 2) % RING][:, :],
                                             op0=ALU.max, op1=ALU.add).then_inc(s_y, 1)
                    dve.wait_ge(s_y, n)
                    dve.bn_stats(stats2[:, :], y_res[:, :]).then_inc(s_stats2, 1)
                    dve.wait_ge(s_stats2, n)
                    dve.memset(filler[:, :], 0.0)
                    dve.bn_aggr(mv2[:, :], stats2[:, :]).then_inc(s_mv2, 1)
                    dve.wait_ge(s_mv2, n)
                    dve.tensor_scalar(var_eps2[:, :], mv2[:, 1:2], LN_EPS_OUT, None, ALU.add).then_inc(s_var2, 1)

                def write_x1(i, off):
                    n = i * RING + (off - 1)
                    dve.wait_ge(s_rstd2, n)
                    slot = off % 2
                    wait(dve, s_store[slot], i * (16 * RING // 2) + 16 * ((off - 2) // 2))
                    dve.tensor_scalar(x1_out[slot][:, :], y_res[:, :], mv2[:, 0:1], rstd2[:, 0:1],
                                      ALU.subtract, ALU.mult).then_inc(s_x1, 1)

                def half(i, off, layer):
                    q = half_no(i, off, layer)
                    static = isinstance(i, int)
                    t = RING * i + off if static else None
                    first = static and t == 0
                    last = static and t == n_batch
                    no_next = static and layer == 1 and t == n_batch - 1
                    slot = (off - layer) % RING
                    if last:
                        transposed_lo(q, 1, True)
                    dve.wait_ge(s_u, q + 1)
                    wait(dve, s_exp, q)
                    dve.tensor_reduce(neg_max[:, :], p_u[:, 0:S], AX.X, ALU.max, negate=True).then_inc(s_max, 1)
                    dve.wait_ge(s_max, q + 1)
                    dve.tensor_scalar(exp_bias[:, :], neg_max[:, :], TEMPER_INV, None, ALU.mult).then_inc(s_bias_exp, 1)
                    if not first:
                        par = 0 if last else layer
                        norm_stats(q, par)
                        dve.wait_ge(s_stats, q)
                    dve.wait_ge(s_exp, q + 1)
                    dve.scalar_tensor_tensor(out=e_adj[:, :], in0=expo[:, :], scalar=1.0, in1=adj_in[slot][:, :],
                                             op0=ALU.mult, op1=ALU.mult, accum_out=e_sum[:, 0:1]).then_inc(s_ea, 1)
                    if not first:
                        norm_var(q)
                    dve.wait_ge(s_ea, q + 1)
                    dve.scalar_tensor_tensor(out=denom[:, :], in0=z_sum[:, :], scalar=ATTN_EPS, in1=e_sum[:, :],
                                             op0=ALU.mult, op1=ALU.add).then_inc(s_den, 1)
                    dve.wait_ge(s_den, q + 1)
                    dve.reciprocal(r_den[:, :], denom[:, :]).then_inc(s_rden, 1)
                    dve.wait_ge(s_rden, q + 1)
                    wait(dve, s_aT, q)
                    dve.scalar_tensor_tensor(out=attn[:, :, :], in0=e_adj[:, :].unsqueeze(1).broadcast_to([128, 2, S]),
                                             scalar=r_den[:, 0:1], in1=masks[:, :, :],
                                             op0=ALU.mult, op1=ALU.mult).then_inc(s_attn, 1)
                    wait(dve, s_hs_diag, q)
                    dve.scalar_tensor_tensor(out=diag_scr[:, :], in0=e_adj[:, :], scalar=r_den[:, 0:1], in1=ident[:, :],
                                             op0=ALU.mult, op1=ALU.mult, accum_out=diag[:, 0:1]).then_inc(s_diag, 1)
                    if not first:
                        norm_apply(q)
                    dve.wait_ge(s_hl_hi, q + 1)
                    dve.tensor_tensor(hl_lo[:, :], p_hl[:, 0:D], hl_hi[:, :].bitcast(F32), ALU.subtract).then_inc(s_hl_lo, 1)
                    dve.wait_ge(s_hr_hi, q + 1)
                    dve.tensor_tensor(hr_lo[:, :], p_hr[:, 0:D], hr_hi[:, :].bitcast(F32), ALU.subtract).then_inc(s_hr_lo, 1)
                    dve.wait_ge(s_aT_hi, q + 1)
                    dve.tensor_tensor(aT_lo[:, :, :].rearrange("p a n -> p (a n)"), p_aT[:, 0:2 * S],
                                      aT_hi[:, :, :].bitcast(F32).rearrange("p a n -> p (a n)"),
                                      ALU.subtract).then_inc(s_aT_lo, 1)
                    if first:
                        transposed_lo(1, 0, False)
                    elif not (last or no_next):
                        transposed_lo(q + 1, 1 - layer, layer == 0)
                    if last or (layer == 0 and not (static and t < 2)):
                        residual(i, off)
                        write_x1(i, off)

                steps(dve, half)
                norm_stats(2 * n_batch, 1)
                dve.wait_ge(s_stats, 2 * n_batch)
                dve.memset(filler[:, :], 0.0)
                norm_var(2 * n_batch)
                norm_apply(2 * n_batch)
                residual(n_batch // RING, n_batch % RING + 1)
                write_x1(n_batch // RING, n_batch % RING + 1)

            @block.tensor
            def _(pe):
                pe.wait_ge(s_const, 10)

                def transposes(n, src):
                    wait(pe, s_t_lo, n)
                    for k in range(KC):
                        mm = pe.transpose(p_T[:, k * 128:(k + 1) * 128], src[:, k * 128:(k + 1) * 128], ident[:, :])
                    mm.then_inc(s_t, 1)

                pe.wait_ge(s_in[0], 32)
                transposes(0, x_in[0])

                def half(i, off, layer):
                    q = half_no(i, off, layer)
                    static = isinstance(i, int)
                    t = RING * i + off if static else None
                    first = static and t == 0
                    last = static and t == n_batch
                    no_next = static and layer == 1 and t == n_batch - 1
                    par = 0 if first else 1 if last else 1 - layer
                    hT = [(hT_hi[layer][:, k, :], hT_lo[layer][:, k, :]) for k in range(KC)]

                    def project(out, m):
                        pe.matmul(out[:, 0:D], ones[:, :], b_rows[:, layer, m, :], start=True, stop=False)
                        for k in range(KC):
                            a_hi, a_lo = hT[k]
                            b_hi_k, b_lo_k = w_hi[layer][:, k, m, :], w_lo[layer][:, k, m, :]
                            pe.matmul(out[:, 0:D], a_hi, b_hi_k, start=False, stop=False)
                            pe.matmul(out[:, 0:D], a_hi, b_lo_k, start=False, stop=False)
                            mm = pe.matmul(out[:, 0:D], a_lo, b_hi_k, start=False, stop=(k == KC - 1))
                        return mm

                    if last:
                        pe.wait_ge(s_h, n_batch)
                        transposes(q, h_nat)
                    pe.wait_ge(s_t_lo, q + 1)
                    wait(pe, s_exp, q)
                    split_products(pe, p_u[:, 0:S], [(a, a) for a in hT]).then_inc(s_u, 1)
                    if static and q <= 2:
                        pe.wait_ge(s_wlo, layer + 1)
                        pe.wait_ge(s_bias, 3)
                    wait(pe, s_hl_lo, q)
                    project(p_hl, 0).then_inc(s_hl, 1)
                    wait(pe, s_hr_lo, q)
                    project(p_hr, 2).then_inc(s_hr, 1)
                    pe.wait_ge(s_attn, q + 1)
                    wait(pe, s_aT_lo, q)
                    for a in range(2):
                        mm = pe.transpose(p_aT[:, a * 128:(a + 1) * 128], attn[:, a, :], ident[:, :])
                    mm.then_inc(s_aT, 1)
                    if first:
                        pe.wait_ge(s_in[1], 32)
                        transposes(1, x_in[1])
                    elif last or no_next:
                        pass
                    elif layer == 0:
                        pe.wait_ge(s_h, i * RING + off)
                        transposes(q + 1, h_nat)
                    else:
                        nxt = off + 1
                        pe.wait_ge(s_in[nxt % RING], i * 32 + 32 * (nxt // RING + 1))
                        transposes(q + 1, x_in[nxt % RING])
                    wait(pe, s_hs_diag, q)
                    project(p_hs, 1).then_inc(s_hs, 1)
                    pe.wait_ge(s_hl_lo, q + 1)
                    pe.wait_ge(s_hr_lo, q + 1)
                    pe.wait_ge(s_aT_lo, q + 1)
                    wait(pe, s_ctx_s, q - 1)
                    split_products(pe, p_ctx[par][:, 0:D],
                                   [((aT_hi[:, 0, :], aT_lo[:, 0, :]), (hl_hi[:, :], hl_lo[:, :])),
                                    ((aT_hi[:, 1, :], aT_lo[:, 1, :]), (hr_hi[:, :], hr_lo[:, :]))]).then_inc(s_ctx, 1)

                steps(pe, half)


def phase_attention(nc, x1, adj, wqk, bqk, wvo, bv_col, rows_at, x2, n_batch, S, D, H):
    KC = D // 128
    DH = D // H
    HP = 64
    NCH = H * HP // 128
    GB = 4
    NT = GB * S
    RMS_EPS = 1e-6
    SCALE = float(DH) ** -0.5
    XR = 4
    PERIOD = 2 * GB

    with ExitStack() as ctx:
        def sb(name, shape, dt=F32):
            return ctx.enter_context(nc.sbuf_tensor(name, shape, dt))

        def sem(name):
            return ctx.enter_context(nc.semaphore(name))

        ident = sb("b_ident", [128, 128])
        exponent = sb("b_exponent", [128, 1])
        ones = sb("b_ones", [128, 128])
        w_raw = sb("b_w_raw", [128, KC, H, HP])
        wv_raw = sb("b_wv_raw", [128, KC * D])
        wq_hi, wk_hi = (sb(f"b_w{a}_hi", [128, KC, NCH * 128], F32R) for a in "qk")
        wq_lo, wk_lo = (sb(f"b_w{a}_lo", [128, KC, NCH * 128], F32R) for a in "qk")
        wv_hi, wo_hi = (sb(f"b_w{a}_hi", [128, KC, D], F32R) for a in "vo")
        wv_lo, wo_lo = (sb(f"b_w{a}_lo", [128, KC, D], F32R) for a in "vo")
        b_qk = sb("b_b_qk", [128, 2, NCH])
        bv = sb("b_bv", [128, KC])
        bv_wide = sb("b_bv_wide", [128, KC, 128])
        bv_hi = sb("b_bv_hi", [128, KC, 128], F32R)
        bv_lo = sb("b_bv_lo", [128, KC, 128], F32R)
        rows = sb("b_rows", [128, 3, D])
        bo_all = sb("b_bo_all", [128, D])
        x_in = [sb(f"b_x_in{s}", [128, D]) for s in range(XR)]
        x_res = [sb(f"b_x_res{s}", [128, D]) for s in range(2)]
        x_bo = [sb(f"b_x_bo{s}", [128, D]) for s in range(2)]
        adj_in = [sb(f"b_adj_in{p}", [128, GB, S]) for p in range(2)]
        xT_hi = [sb(f"b_xT_hi{p}", [128, KC, NT], F32R) for p in range(2)]
        xT_lo = [sb(f"b_xT_lo{p}", [128, KC, NT], F32R) for p in range(2)]
        q_sb, k_sb = ([sb(f"b_{a}{p}", [128, NT]) for p in range(2)] for a in "qk")
        v_sb = [sb(f"b_v{p}", [128, GB, D]) for p in range(2)]
        prob = [sb(f"b_prob{p}", [128, 2, GB, S]) for p in range(2)]
        neg_max = [sb(f"b_neg_max{p}", [128, 2 * GB]) for p in range(2)]
        row_sum = [sb(f"b_row_sum{p}", [128, 2, GB]) for p in range(2)]
        r_sum = [sb(f"b_r_sum{p}", [128, 2, GB]) for p in range(2)]
        pT_sb = sb("b_pT_sb", [128, 2 * GB, S])
        context = [sb(f"b_context{p}", [128, GB, D]) for p in range(2)]
        cT_hi = sb("b_cT_hi", [128, KC * 128], F32R)
        cT_lo = sb("b_cT_lo", [128, KC * 128], F32R)
        y = [sb(f"b_y{s}", [128, D]) for s in range(2)]
        square = sb("b_square", [128, D])
        sum_sq = [sb(f"b_sum_sq{s}", [128, 1]) for s in range(2)]
        mean_sq = sb("b_mean_sq", [128, 1])
        r_rms = sb("b_r_rms", [128, 1])
        z = sb("b_z", [128, D])
        x2_out = [sb(f"b_x2_out{s}", [128, D]) for s in range(2)]

        p_q = ctx.enter_context(nc.psum_tensor("b_p_q", [128, NT], F32))
        p_k = ctx.enter_context(nc.psum_tensor("b_p_k", [128, NT], F32))
        p_s = ctx.enter_context(nc.psum_tensor("b_p_s", [128, 2, GB, S], F32))
        p_pT = ctx.enter_context(nc.psum_tensor("b_p_pT", [128, 2 * GB, S], F32))
        p_c = ctx.enter_context(nc.psum_tensor("b_p_c", [128, 512], F32))
        p_m = ctx.enter_context(nc.psum_tensor("b_p_m", [128, 512], F32))

        s_const = sem("b_s_const")
        s_small = sem("b_s_small")
        s_wload = sem("b_s_wload")
        s_whi = sem("b_s_whi")
        s_wlo = sem("b_s_wlo")
        s_bv = sem("b_s_bv")
        s_x = [sem(f"b_s_xin{s}") for s in range(XR)]
        s_xr = [sem(f"b_s_xr{s}") for s in range(2)]
        s_adj = [sem(f"b_s_adj{p}") for p in range(2)]
        s_t, s_t_hi, s_t_lo = sem("b_s_t"), sem("b_s_t_hi"), sem("b_s_t_lo")
        s_q, s_q_sb = sem("b_s_q"), sem("b_s_q_sb")
        s_k, s_k_sb = sem("b_s_k"), sem("b_s_k_sb")
        s_v, s_v_sb = sem("b_s_v"), sem("b_s_v_sb")
        s_sc = sem("b_s_sc")
        s_logit = sem("b_s_logit")
        s_max = sem("b_s_max")
        s_exp = sem("b_s_exp")
        s_rsum = sem("b_s_rsum")
        s_pT, s_pT_sb = sem("b_s_pT"), sem("b_s_pT_sb")
        s_c = sem("b_s_c")
        s_cn = sem("b_s_cn")
        s_cT, s_cT_hi, s_cT_lo = sem("b_s_cT"), sem("b_s_cT_hi"), sem("b_s_cT_lo")
        s_o = sem("b_s_o")
        s_xbo = sem("b_s_xbo")
        s_y, s_sq, s_ms, s_rms = sem("b_s_y"), sem("b_s_sq"), sem("b_s_ms"), sem("b_s_rms")
        s_z, s_x2 = sem("b_s_z"), sem("b_s_x2")
        s_store = [sem(f"b_s_store{s}") for s in range(2)]

        class Item:
            def __init__(self, i, off):
                self.i, self.off = i, off
                self.static = isinstance(i, int)
                self.no = i * PERIOD + off
                self.exists = not self.static or 0 <= self.no < n_batch
                self.sub = off % GB
                self.par = (off // GB) % 2
                self.odd = off % 2

            def plus(self, d):
                return Item(self.i, self.off + d)

            def over(self, m):
                return self.i * (PERIOD // m) + self.off // m

        def wait(eng, s, value):
            if not isinstance(value, int) or value > 0:
                eng.wait_ge(s, value)

        LEAD, TAIL = 5, 7

        def steps(eng, step):
            for n in range(-LEAD, PERIOD):
                step(Item(0, n))
            with eng.Fori(1, n_batch // PERIOD - 1) as i:
                for off in range(PERIOD):
                    step(Item(i, off))
            for n in range(n_batch - PERIOD, n_batch + TAIL):
                step(Item(0, n))

        def three_passes(eng, out, a, b, start, stop):
            a_hi, a_lo = a
            b_hi, b_lo = b
            eng.matmul(out, a_hi, b_hi, start=start, stop=False)
            eng.matmul(out, a_hi, b_lo, start=False, stop=False)
            return eng.matmul(out, a_lo, b_hi, start=False, stop=stop)

        def flat(ap):
            return ap.rearrange("p a b -> p (a b)")

        with nc.Block() as block:

            @block.sync
            def _(sp):
                for s in range(2):
                    sp.dma_start(x_in[s][:, :], x1[s]).then_inc(s_x[s], 16)
                sp.wait_ge(s_const, 4)
                for a in range(2):
                    for h in range(2):
                        sp.dma_start(b_qk[h * HP:h * HP + DH, a, :], bqk[a, h]).then_inc(s_small, 16)
                sp.dma_start(bv[:, :], bv_col).then_inc(s_small, 16)
                sp.dma_start(rows[:, :, :], rows_at).then_inc(s_small, 16)
                sp.dma_start(wv_raw[:, :], wvo[0]).then_inc(s_wload, 16)
                for a in range(2):
                    wait(sp, s_wlo, 1 if a else 0)
                    for k in range(KC):
                        sp.dma_start(w_raw[:, k, :, 0:DH], wqk[a, k]).then_inc(s_wload, 16)
                    if a == 0:
                        continue
                    sp.wait_ge(s_wlo, 2)
                    sp.dma_start(wv_raw[:, :], wvo[1]).then_inc(s_wload, 16)

                def step(n):
                    j = n.plus(7)
                    if j.exists and not (j.static and j.off < 2):
                        wait(sp, s_t, j.no - XR + 1)
                        sp.dma_start(x_in[j.off % XR][:, :], x1[j.no]).then_inc(s_x[j.off % XR], 16)
                    j = n.plus(5)
                    if j.exists:
                        wait(sp, s_logit, j.no * 2 - 2 * (GB + j.sub))
                        sp.dma_start(adj_in[j.par][:, j.sub, :], adj[j.no]).then_inc(s_adj[j.par], 16)
                    j = n.plus(-4)
                    if j.exists:
                        wait(sp, s_xbo, j.no - 1)
                        sp.dma_start(x_res[j.odd][:, :], x1[j.no]).then_inc(s_xr[j.odd], 16)
                    j = n.plus(-7)
                    if j.exists:
                        sp.wait_ge(s_x2, j.no + 1)
                        sp.dma_start(x2[j.no], x2_out[j.odd][:, :]).then_inc(s_store[j.odd], 16)

                for m in range(-7, -LEAD):
                    step(Item(0, m))
                steps(sp, step)
                for s in range(2):
                    sp.wait_ge(s_store[s], 16 * (n_batch // 2))

            @block.gpsimd
            def _(pool):
                pool.memset(w_raw[:, :, :, :], 0.0).then_inc(s_const, 1)
                pool.memset(b_qk[:, :, :], 0.0).then_inc(s_const, 1)
                pool.memset(ident[:, :], 0.0).then_inc(s_const, 1)
                pool.memset(exponent[:, :], -0.5).then_inc(s_const, 1)
                pool.memset(ones[:, :], 1.0).then_inc(s_const, 1)
                pool.wait_ge(s_const, 5)
                pool.affine_select(out=ident[:, :], in_=ident[:, :], compare_op=ALU.not_equal, fill=1.0,
                                   base=0, pattern=[[-1, 128]], channel_multiplier=1).then_inc(s_const, 1)
                pool.wait_ge(s_bv, KC + 4)

                def step(n):
                    j = n.plus(-5)
                    if j.exists:
                        pool.wait_ge(s_xr[j.odd], j.over(2) * 16 + 16)
                        wait(pool, s_y, j.no - 1)
                        pool.tensor_tensor(x_bo[j.odd][:, :], x_res[j.odd][:, :], bo_all[:, :],
                                           ALU.add).then_inc(s_xbo, 1)
                    j = n.plus(-6)
                    if j.exists:
                        pool.wait_ge(s_ms, j.no + 1)
                        pool.tensor_tensor(r_rms[:, :], mean_sq[:, :], exponent[:, :], ALU.pow).then_inc(s_rms, 1)
                        pool.wait_ge(s_z, j.no + 1)
                        wait(pool, s_store[j.odd], j.over(2) * 16)
                        pool.tensor_tensor(x2_out[j.odd][:, :], z[:, :], rows[:, 2, :], ALU.add).then_inc(s_x2, 1)

                steps(pool, step)

            @block.scalar
            def _(act):
                act.wait_ge(s_wload, 16 * (1 + KC))
                act.activation(flat(wq_hi[:, :, :]), w_raw[:, :, :, :].rearrange("p k h d -> p (k h d)"),
                               ACT.Copy).then_inc(s_whi, 1)
                act.activation(flat(wv_hi[:, :, :]), wv_raw[:, :], ACT.Copy).then_inc(s_whi, 1)
                act.wait_ge(s_wload, 16 * (2 + 2 * KC))
                act.activation(flat(wk_hi[:, :, :]), w_raw[:, :, :, :].rearrange("p k h d -> p (k h d)"),
                               ACT.Copy).then_inc(s_whi, 1)
                act.activation(flat(wo_hi[:, :, :]), wv_raw[:, :], ACT.Copy).then_inc(s_whi, 1)
                act.wait_ge(s_small, 16 * 6)
                act.wait_ge(s_const, 5)
                for k in range(KC):
                    act.activation(bv_wide[:, k, :], ones[:, :], ACT.Copy, scale=bv[:, k:k + 1]).then_inc(s_bv, 1)
                act.wait_ge(s_bv, KC)
                act.activation(flat(bv_hi[:, :, :]), flat(bv_wide[:, :, :]), ACT.Copy).then_inc(s_bv, 1)

                def exps(n, h):
                    act.wait_ge(s_max, n.no * 2 + (h + 1))
                    if h == 0:
                        wait(act, s_rsum, n.no - 1)
                    for b in range(GB):
                        e = act.activation(prob[n.odd][:, h, b, :], prob[n.odd][:, h, b, :], ACT.Exp,
                                           bias=neg_max[n.odd][:, h * GB + b:h * GB + b + 1],
                                           accum_out=row_sum[n.odd][:, h, b:b + 1])
                    return e

                def step(n):
                    j = n.plus(5)
                    if j.exists:
                        act.wait_ge(s_t, j.no + 1)
                        act.activation(xT_hi[j.par][:, :, j.sub * S:(j.sub + 1) * S],
                                       p_m[:, 0:D].rearrange("p (k n) -> p k n", k=KC), ACT.Copy).then_inc(s_t_hi, 1)
                    j = n.plus(-1)
                    if j.exists:
                        act.wait_ge(s_pT, j.no + 1)
                        act.activation(flat(pT_sb[:, :, :]), flat(p_pT[:, :, :]), ACT.Copy).then_inc(s_pT_sb, 1)
                    if n.exists:
                        exps(n, 0)
                    j = n.plus(-5)
                    if j.exists:
                        act.wait_ge(s_cT, j.no + 1)
                        act.activation(cT_hi[:, :], p_m[:, 0:D], ACT.Copy).then_inc(s_cT_hi, 1)
                    j = n.plus(1)
                    if j.exists:
                        act.wait_ge(s_q, j.no + 1)
                        act.activation(q_sb[j.odd][:, :], p_q[:, :], ACT.Identity,
                                       bias=b_qk[:, 0, j.sub:j.sub + 1]).then_inc(s_q_sb, 1)
                    if n.exists:
                        exps(n, 1).then_inc(s_exp, 1)
                    j = n.plus(1)
                    if j.exists:
                        act.wait_ge(s_k, j.no + 1)
                        act.activation(k_sb[j.odd][:, :], p_k[:, :], ACT.Identity,
                                       bias=b_qk[:, 1, j.sub:j.sub + 1]).then_inc(s_k_sb, 1)
                    j = n.plus(-5)
                    if j.exists:
                        act.wait_ge(s_y, j.no + 1)
                        wait(act, s_sq, j.no)
                        act.activation(square[:, :], y[j.odd][:, :], ACT.Square,
                                       accum_out=sum_sq[j.odd][:, 0:1]).then_inc(s_sq, 1)

                steps(act, step)

            @block.vector
            def _(dve):
                splits = [(w_raw[:, :, :, :].rearrange("p k h d -> p (k h d)"), wq_hi, wq_lo), (wv_raw[:, :], wv_hi, wv_lo),
                          (w_raw[:, :, :, :].rearrange("p k h d -> p (k h d)"), wk_hi, wk_lo), (wv_raw[:, :], wo_hi, wo_lo)]
                for m, (raw, hi, lo) in enumerate(splits):
                    dve.wait_ge(s_whi, m + 1)
                    dve.tensor_tensor(flat(lo[:, :, :]), raw, flat(hi[:, :, :].bitcast(F32)), ALU.subtract).then_inc(s_wlo, 1)
                dve.wait_ge(s_bv, KC + 1)
                dve.tensor_tensor(flat(bv_lo[:, :, :]), flat(bv_wide[:, :, :]), flat(bv_hi[:, :, :].bitcast(F32)),
                                  ALU.subtract).then_inc(s_bv, 1)
                dve.wait_ge(s_bv, KC + 3)
                dve.tensor_tensor(bo_all[:, :], p_c[:, 0:D], rows[:, 0, :], ALU.add).then_inc(s_bv, 1)

                def step(n):
                    j = n.plus(2)
                    if j.exists:
                        dve.wait_ge(s_v, j.no + 1)
                        dve.tensor_copy(v_sb[j.par][:, j.sub, :], p_m[:, 0:D]).then_inc(s_v_sb, 1)
                    if n.exists:
                        dve.wait_ge(s_adj[n.par], n.over(PERIOD) * (16 * GB) + 16 * GB)
                        wait(dve, s_pT, n.no - 1)
                        for h in range(2):
                            dve.wait_ge(s_sc, n.no * 2 + (h + 1))
                            dve.scalar_tensor_tensor(out=flat(prob[n.odd][:, h, :, :]), in0=flat(p_s[:, h, :, :]), scalar=SCALE,
                                                     in1=flat(adj_in[n.par][:, :, :]), op0=ALU.mult, op1=ALU.add)\
                               .then_inc(s_logit, 1)
                            dve.wait_ge(s_logit, n.no * 2 + (h + 1))
                            dve.tensor_reduce(neg_max[n.odd][:, h * GB:(h + 1) * GB], prob[n.odd][:, h, :, :], AX.X, ALU.max,
                                              negate=True).then_inc(s_max, 1)
                    j = n.plus(5)
                    if j.exists:
                        dve.wait_ge(s_t_hi, j.no + 1)
                        c = slice(j.sub * S, (j.sub + 1) * S)
                        dve.tensor_tensor(xT_lo[j.par][:, :, c], p_m[:, 0:D].rearrange("p (k n) -> p k n", k=KC),
                                          xT_hi[j.par][:, :, c].bitcast(F32), ALU.subtract).then_inc(s_t_lo, 1)
                    j = n.plus(-1)
                    if j.exists:
                        dve.wait_ge(s_exp, j.no + 1)
                        dve.reciprocal(flat(r_sum[j.odd][:, :, :]), flat(row_sum[j.odd][:, :, :])).then_inc(s_rsum, 1)
                    j = n.plus(-2)
                    if j.exists:
                        dve.wait_ge(s_c, j.no + 1)
                        wait(dve, s_rsum, j.no + 1)
                        for h in range(2):
                            head = 2 * j.sub + h
                            c = dve.tensor_tensor(context[j.par][:, :, head * DH:(head + 1) * DH],
                                                  p_c[:, h * GB * DH:(h + 1) * GB * DH].rearrange("p (b d) -> p b d", b=GB),
                                                  r_sum[j.odd][:, h, :].unsqueeze(2).broadcast_to([128, GB, DH]), ALU.mult)
                        c.then_inc(s_cn, 1)
                    j = n.plus(-5)
                    if j.exists:
                        dve.wait_ge(s_cT_hi, j.no + 1)
                        dve.tensor_tensor(cT_lo[:, :], p_m[:, 0:D], cT_hi[:, :].bitcast(F32), ALU.subtract).then_inc(s_cT_lo, 1)
                    j = n.plus(-6)
                    if j.exists:
                        dve.wait_ge(s_sq, j.no + 1)
                        dve.tensor_scalar(mean_sq[:, :], sum_sq[j.odd][:, :], 1.0 / D, RMS_EPS,
                                          ALU.mult, ALU.add).then_inc(s_ms, 1)
                        dve.wait_ge(s_rms, j.no + 1)
                        wait(dve, s_x2, j.no)
                        dve.scalar_tensor_tensor(out=z[:, :], in0=y[j.odd][:, :], scalar=r_rms[:, 0:1], in1=rows[:, 1, :],
                                                 op0=ALU.mult, op1=ALU.mult).then_inc(s_z, 1)
                    j = n.plus(-5)
                    if j.exists:
                        dve.wait_ge(s_xbo, j.no + 1)
                        dve.wait_ge(s_o, j.no + 1)
                        dve.tensor_tensor(y[j.odd][:, :], p_m[:, 0:D], x_bo[j.odd][:, :], ALU.add).then_inc(s_y, 1)

                steps(dve, step)

            @block.tensor
            def _(pe):
                pe.wait_ge(s_const, 6)
                pe.wait_ge(s_wlo, 4)
                pe.wait_ge(s_bv, KC + 2)
                for k in range(KC):
                    mm = three_passes(pe, p_c[:, 0:D], (bv_hi[:, k, :], bv_lo[:, k, :]),
                                      (wo_hi[:, k, :], wo_lo[:, k, :]), k == 0, k == KC - 1)
                mm.then_inc(s_bv, 1)
                pe.wait_ge(s_bv, KC + 4)

                def project(j, out, hi, lo):
                    c = slice(j.sub * 128, (j.sub + 1) * 128)
                    for k in range(KC):
                        mm = three_passes(pe, out[:, :], (hi[:, k, c], lo[:, k, c]),
                                          (xT_hi[j.par][:, k, :], xT_lo[j.par][:, k, :]), k == 0, k == KC - 1)
                    return mm

                def step(n):
                    if n.exists:
                        pe.wait_ge(s_q_sb, n.no + 1)
                        pe.wait_ge(s_k_sb, n.no + 1)
                        wait(pe, s_logit, n.no * 2)
                        for h in range(2):
                            r = slice(h * HP, h * HP + DH)
                            for b in range(GB):
                                c = slice(b * S, (b + 1) * S)
                                mm = pe.matmul(p_s[:, h, b, :], q_sb[n.odd][r, c], k_sb[n.odd][r, c], start=True, stop=True)
                            if h == 0:
                                mm.then_inc(s_sc, 1)
                        mm.then_inc(s_sc, 1)
                    j = n.plus(5)
                    if j.exists:
                        if n.plus(2).exists:
                            pe.wait_ge(s_v_sb, n.plus(2).no + 1)
                        elif not (j.static and j.no == 0):
                            wait(pe, s_t_lo, j.no)
                        pe.wait_ge(s_x[j.off % XR], j.over(XR) * 16 + 16)
                        for k in range(KC):
                            mm = pe.transpose(p_m[:, k * 128:(k + 1) * 128], x_in[j.off % XR][:, k * 128:(k + 1) * 128],
                                              ident[:, :])
                        mm.then_inc(s_t, 1)
                    j = n.plus(-1)
                    if j.exists:
                        pe.wait_ge(s_exp, j.no + 1)
                        wait(pe, s_pT_sb, j.no)
                        for h in range(2):
                            for b in range(GB):
                                mm = pe.transpose(p_pT[:, h * GB + b, :], prob[j.odd][:, h, b, :], ident[:, :])
                        mm.then_inc(s_pT, 1)
                    j = n.plus(1)
                    if j.exists:
                        pe.wait_ge(s_t_lo, j.no - j.sub + GB)
                        wait(pe, s_q_sb, j.no)
                        project(j, p_q, wq_hi, wq_lo).then_inc(s_q, 1)
                    j = n.plus(-5)
                    if j.exists:
                        pe.wait_ge(s_cn, j.no - j.sub + GB)
                        if n.plus(5).exists:
                            pe.wait_ge(s_t_lo, n.plus(5).no + 1)
                        elif n.plus(2).exists:
                            pe.wait_ge(s_v_sb, n.plus(2).no + 1)
                        wait(pe, s_y, j.no)
                        for k in range(KC):
                            mm = pe.transpose(p_m[:, k * 128:(k + 1) * 128],
                                              context[j.par][:, j.sub, k * 128:(k + 1) * 128], ident[:, :])
                        mm.then_inc(s_cT, 1)
                    j = n.plus(1)
                    if j.exists:
                        wait(pe, s_k_sb, j.no)
                        project(j, p_k, wk_hi, wk_lo).then_inc(s_k, 1)
                    j = n.plus(-5)
                    if j.exists:
                        pe.wait_ge(s_cT_lo, j.no + 1)
                        for k in range(KC):
                            c = slice(k * 128, (k + 1) * 128)
                            mm = three_passes(pe, p_m[:, 0:D], (cT_hi[:, c], cT_lo[:, c]),
                                              (wo_hi[:, k, :], wo_lo[:, k, :]), k == 0, k == KC - 1)
                        mm.then_inc(s_o, 1)
                    j = n.plus(-1)
                    if j.exists:
                        pe.wait_ge(s_pT_sb, j.no + 1)
                        pe.wait_ge(s_v_sb, j.no - j.sub + GB)
                        wait(pe, s_cn, j.no)
                        for h in range(2):
                            head = 2 * j.sub + h
                            d = slice(head * DH, (head + 1) * DH)
                            for b in range(GB):
                                i = h * GB + b
                                mm = pe.matmul(p_c[:, i * DH:(i + 1) * DH], pT_sb[:, i, :], v_sb[j.par][:, b, d],
                                               start=True, stop=True)
                        mm.then_inc(s_c, 1)
                    j = n.plus(3)
                    if j.exists:
                        pe.wait_ge(s_t_lo, j.no + 1)
                        if n.plus(-5).exists:
                            pe.wait_ge(s_y, n.plus(-5).no + 1)
                        elif n.plus(5).exists:
                            pe.wait_ge(s_t_lo, n.plus(5).no + 1)
                        for k in range(KC):
                            c = slice(j.sub * S, (j.sub + 1) * S)
                            mm = three_passes(pe, p_m[:, 0:D], (xT_hi[j.par][:, k, c], xT_lo[j.par][:, k, c]),
                                              (wv_hi[:, k, :], wv_lo[:, k, :]), k == 0, k == KC - 1)
                        mm.then_inc(s_v, 1)

                steps(pe, step)


def phase_feed_forward(nc, x1, x2, w1, b1, w2, rows_ff, out, n_batch, S, D, F):
    KC = D // 128
    FC = F // 128
    GB = 4
    NG = n_batch // GB
    NT = GB * S
    RMS_EPS = 1e-6
    LN_EPS = 1e-5
    T_STEP = {2: 0, 4: 1, 6: 2, 8: 3}

    with ExitStack() as ctx:
        def sb(name, shape, dt=F32):
            return ctx.enter_context(nc.sbuf_tensor(name, shape, dt))

        def sem(name):
            return ctx.enter_context(nc.semaphore(name))

        ident = sb("c_ident", [128, 128])
        exponent = sb("c_exponent", [128, 1])
        w_raw = sb("c_w_raw", [128, F])
        w1_hi = sb("c_w1_hi", [128, KC, F], F32R)
        w1_lo = sb("c_w1_lo", [128, KC, F], F32R)
        w2_hi = sb("c_w2_hi", [128, FC, D], F32R)
        w2_lo = sb("c_w2_lo", [128, FC, D], F32R)
        b1_col = sb("c_b1_col", [128, FC])
        rows = sb("c_rows", [128, 3, D])
        x2_in = [sb(f"c_x2_in{p}", [128, GB, D]) for p in range(2)]
        x1_in = [sb(f"c_x1_in{p}", [128, GB, D]) for p in range(2)]
        xT_hi = [sb(f"c_xT_hi{p}", [128, KC, NT], F32R) for p in range(2)]
        xT_lo = [sb(f"c_xT_lo{p}", [128, KC, NT], F32R) for p in range(2)]
        hid = sb("c_hid", [128, NT])
        hid_hi = [sb(f"c_hid_hi{p}", [128, NT], F32R) for p in range(2)]
        hid_lo = [sb(f"c_hid_lo{p}", [128, NT], F32R) for p in range(2)]
        y = [sb(f"c_y{b}", [128, D]) for b in range(GB)]
        square = sb("c_square", [128, D])
        sum_sq = [sb(f"c_sum_sq{b}", [128, 1]) for b in range(GB)]
        mean_sq = [sb(f"c_mean_sq{b}", [128, 1]) for b in range(GB)]
        r_rms = [sb(f"c_r_rms{b}", [128, 1]) for b in range(GB)]
        z = [sb(f"c_z{b}", [128, D]) for b in range(GB)]
        stats = sb("c_stats", [128, 6])
        mv = [sb(f"c_mv{b}", [128, 2]) for b in range(GB)]
        var_eps = [sb(f"c_var_eps{b}", [128, 1]) for b in range(GB)]
        rstd = [sb(f"c_rstd{b}", [128, 1]) for b in range(GB)]
        filler = sb("c_filler", [128, 1])
        o_out = [sb(f"c_o_out{b}", [128, D]) for b in range(GB)]

        def bank(name):
            return ctx.enter_context(nc.psum_tensor(name, [128, 512], F32))

        p_f1 = [bank("c_p_f1_0"), bank("c_p_f1_1")]
        p_f2 = [bank(f"c_p_f2_{b}") for b in range(GB)]
        p_T = bank("c_p_T")

        s_const = sem("c_s_const")
        s_small = sem("c_s_small")
        s_wload = sem("c_s_wload")
        s_whi = sem("c_s_whi")
        s_wlo = sem("c_s_wlo")
        s_x2 = [sem(f"c_s_x2_{p}") for p in range(2)]
        s_x1 = [sem(f"c_s_x1_{p}") for p in range(2)]
        s_t = sem("c_s_t")
        s_t_hi = sem("c_s_t_hi")
        s_t_lo = sem("c_s_t_lo")
        s_f1 = sem("c_s_f1")
        s_silu = sem("c_s_silu")
        s_hid_hi = sem("c_s_hid_hi")
        s_hid_lo = sem("c_s_hid_lo")
        s_hid_used = sem("c_s_hid_used")
        s_f2 = [sem(f"c_s_f2_{b}") for b in range(GB)]
        s_xb = sem("c_s_xb")
        s_xg = sem("c_s_xg")
        s_y = sem("c_s_y")
        s_sq = sem("c_s_sq")
        s_ms = sem("c_s_ms")
        s_rms = sem("c_s_rms")
        s_z = sem("c_s_z")
        s_sum = sem("c_s_sum")
        s_stats = sem("c_s_stats")
        s_mv = sem("c_s_mv")
        s_var = sem("c_s_var")
        s_rstd = sem("c_s_rstd")
        s_o = sem("c_s_o")
        s_store = [sem(f"c_s_store{b}") for b in range(GB)]

        def wait(eng, s, value):
            if not isinstance(value, int) or value > 0:
                eng.wait_ge(s, value)

        def chunks(i, p, f):
            return i * (2 * FC) + (p * FC + f)

        def batches(i, p, b):
            return i * (2 * GB) + (p * GB + b)

        def groups(i, p):
            return i * 2 + p

        def is_last(i, p):
            return isinstance(i, int) and 2 * i + p == NG - 1

        def is_first(i, p):
            return isinstance(i, int) and 2 * i + p == 0

        def all_groups(eng, group):
            for p in range(2):
                group(0, p)
            with eng.Fori(1, NG // 2 - 1) as i:
                for p in range(2):
                    group(i, p)
            for p in range(2):
                group(NG // 2 - 1, p)

        x1_v = x1.rearrange("(g b) s d -> g s b d", b=GB)
        x2_v = x2.rearrange("(g b) s d -> g s b d", b=GB)
        W_PARTS = [(w1[k], w1_hi[:, k, :], w1_lo[:, k, :], F) for k in range(KC)]
        W_PARTS += [(w2[k], w2_hi[:, k * (FC // KC):(k + 1) * (FC // KC), :].rearrange("p c n -> p (c n)"),
                     w2_lo[:, k * (FC // KC):(k + 1) * (FC // KC), :].rearrange("p c n -> p (c n)"), D * FC // KC)
                    for k in range(KC)]

        with nc.Block() as block:

            @block.sync
            def _(sp):
                sp.dma_start(x2_in[0][:, :, :], x2_v[0]).then_inc(s_x2[0], 16)
                sp.dma_start(b1_col[:, :], b1).then_inc(s_small, 16)
                sp.dma_start(rows[:, :, :], rows_ff).then_inc(s_small, 16)
                for n, (src, _, _, width) in enumerate(W_PARTS):
                    wait(sp, s_wlo, n)
                    sp.dma_start(w_raw[:, 0:width], src).then_inc(s_wload, 16)
                sp.dma_start(x1_in[0][:, :, :], x1_v[0]).then_inc(s_x1[0], 16)

                def group(i, p):
                    if not is_last(i, p):
                        wait(sp, s_y, batches(i, p, 0))
                        wait(sp, s_xb, batches(i, p, 0))
                        sp.dma_start(x2_in[1 - p][:, :, :], x2_v[groups(i, p) + 1]).then_inc(s_x2[1 - p], 16)
                        wait(sp, s_sum, batches(i, p, 0))
                        sp.dma_start(x1_in[1 - p][:, :, :], x1_v[groups(i, p) + 1]).then_inc(s_x1[1 - p], 16)
                    if not is_first(i, p):
                        for b in range(GB):
                            n = i * (2 * GB) + (p * GB + b - GB)
                            sp.wait_ge(s_o, n + 1)
                            sp.dma_start(out[n], o_out[b][:, :]).then_inc(s_store[b], 16)

                all_groups(sp, group)
                for b in range(GB):
                    n = n_batch - GB + b
                    sp.wait_ge(s_o, n + 1)
                    sp.dma_start(out[n], o_out[b][:, :]).then_inc(s_store[b], 16)
                for b in range(GB):
                    sp.wait_ge(s_store[b], 16 * NG)

            @block.gpsimd
            def _(pool):
                pool.memset(ident[:, :], 0.0).then_inc(s_const, 1)
                pool.memset(exponent[:, :], -0.5).then_inc(s_const, 1)
                pool.wait_ge(s_const, 2)
                pool.affine_select(out=ident[:, :], in_=ident[:, :], compare_op=ALU.not_equal, fill=1.0,
                                   base=0, pattern=[[-1, 128]], channel_multiplier=1).then_inc(s_const, 1)
                pool.wait_ge(s_small, 32)

                def finals(i, p):
                    for f in range(FC):
                        if 0 <= f - 1 < GB:
                            b = f - 1
                            pool.wait_ge(s_ms, batches(i, p, b) - GB + 1)
                            pool.tensor_tensor(r_rms[b][:, :], mean_sq[b][:, :], exponent[:, :],
                                               ALU.pow).then_inc(s_rms, 1)
                        if 0 <= f - 2 < GB:
                            b = f - 2
                            pool.wait_ge(s_z, batches(i, p, b) - GB + 1)
                            pool.wait_ge(s_xg, batches(i, p, b) - GB + 1)
                            pool.tensor_tensor(z[b][:, :], z[b][:, :], x1_in[1 - p][:, b, :], ALU.add).then_inc(s_sum, 1)
                        if 0 <= f - 4 < GB:
                            b = f - 4
                            pool.wait_ge(s_var, batches(i, p, b) - GB + 1)
                            pool.tensor_tensor(rstd[b][:, :], var_eps[b][:, :], exponent[:, :],
                                               ALU.pow).then_inc(s_rstd, 1)

                def group(i, p):
                    if not is_first(i, p):
                        finals(i, p)
                    for b in range(GB):
                        pool.wait_ge(s_x2[p], i * 16 + 16)
                        pool.wait_ge(s_t, batches(i, p, b) + 1)
                        pool.tensor_tensor(x2_in[p][:, b, :], x2_in[p][:, b, :], rows[:, 0, :], ALU.add).then_inc(s_xb, 1)
                    for b in range(GB):
                        pool.wait_ge(s_x1[p], i * 16 + 16)
                        pool.tensor_tensor(x1_in[p][:, b, :], x1_in[p][:, b, :], rows[:, 2, :], ALU.add).then_inc(s_xg, 1)

                all_groups(pool, group)
                finals(NG // 2, 0)

            @block.scalar
            def _(act):
                def transposed_hi(i, p, b):
                    act.wait_ge(s_t, batches(i, p, b) + 1)
                    act.activation(xT_hi[p % 2][:, :, b * S:(b + 1) * S],
                                   p_T[:, 0:D].rearrange("p (k n) -> p k n", k=KC), ACT.Copy).then_inc(s_t_hi, 1)

                for b in range(GB):
                    transposed_hi(0, 0, b)
                for n, (_, hi, _, width) in enumerate(W_PARTS):
                    act.wait_ge(s_wload, 16 * (n + 1))
                    act.activation(hi, w_raw[:, 0:width], ACT.Copy).then_inc(s_whi, 1)
                act.wait_ge(s_small, 32)

                def silu(n, par, f):
                    act.wait_ge(s_f1, n + 1)
                    wait(act, s_hid_lo, n)
                    act.activation(hid[:, :], p_f1[par][:, :], ACT.Silu, bias=b1_col[:, f:f + 1]).then_inc(s_silu, 1)

                def squares(i, p):
                    for b in range(GB):
                        n = batches(i, p, b)
                        act.wait_ge(s_y, n + 1)
                        wait(act, s_sq, n)
                        act.activation(square[:, :], y[b][:, :], ACT.Square,
                                       accum_out=sum_sq[b][:, 0:1]).then_inc(s_sq, 1)

                def group(i, p):
                    if is_first(i, p):
                        silu(0, 0, 0)
                    for f in range(FC):
                        if not (is_last(i, p) and f == FC - 1):
                            silu(chunks(i, p, f) + 1, (f + 1) % 2, (f + 1) % FC)
                        if f in T_STEP and not is_last(i, p):
                            transposed_hi(i, p + 1, T_STEP[f])
                        if f == 0 and not is_first(i, p):
                            squares(i, p - 1)

                all_groups(act, group)
                squares(NG // 2, -1)

            @block.vector
            def _(dve):
                def transposed_lo(i, p, b):
                    dve.wait_ge(s_t_hi, batches(i, p, b) + 1)
                    dve.tensor_tensor(xT_lo[p % 2][:, :, b * S:(b + 1) * S],
                                      p_T[:, 0:D].rearrange("p (k n) -> p k n", k=KC),
                                      xT_hi[p % 2][:, :, b * S:(b + 1) * S].bitcast(F32), ALU.subtract).then_inc(s_t_lo, 1)

                for b in range(GB):
                    transposed_lo(0, 0, b)
                for n, (_, hi, lo, width) in enumerate(W_PARTS):
                    dve.wait_ge(s_whi, n + 1)
                    dve.tensor_tensor(lo, w_raw[:, 0:width], hi.bitcast(F32), ALU.subtract).then_inc(s_wlo, 1)
                dve.wait_ge(s_small, 32)

                def hidden(n, par):
                    dve.wait_ge(s_silu, n + 1)
                    wait(dve, s_hid_used, n - 1)
                    dve.tensor_copy(hid_hi[par][:, :], hid[:, :]).then_inc(s_hid_hi, 1)
                    dve.wait_ge(s_hid_hi, n + 1)
                    dve.tensor_tensor(hid_lo[par][:, :], hid[:, :], hid_hi[par][:, :].bitcast(F32),
                                      ALU.subtract).then_inc(s_hid_lo, 1)

                def sums(i, p):
                    for b in range(GB):
                        n = batches(i, p, b)
                        dve.wait_ge(s_xb, n + 1)
                        if b < GB - 1:
                            dve.wait_ge(s_f2[b], groups(i, p) + 1)
                        else:
                            dve.wait_ge(s_hid_used, chunks(i, p, FC))
                        dve.tensor_tensor(y[b][:, :], p_f2[b][:, 0:D], x2_in[p][:, b, :], ALU.add).then_inc(s_y, 1)

                def mean_square(n, b):
                    dve.wait_ge(s_sq, n + 1)
                    dve.tensor_scalar(mean_sq[b][:, :], sum_sq[b][:, :], 1.0 / D, RMS_EPS,
                                      ALU.mult, ALU.add).then_inc(s_ms, 1)

                def scale_rms(n, b):
                    dve.wait_ge(s_rms, n + 1)
                    dve.scalar_tensor_tensor(out=z[b][:, :], in0=y[b][:, :], scalar=r_rms[b][:, 0:1],
                                             in1=rows[:, 1, :], op0=ALU.mult, op1=ALU.mult).then_inc(s_z, 1)

                def statistics(n, b):
                    dve.wait_ge(s_sum, n + 1)
                    dve.bn_stats(stats[:, :], z[b][:, :]).then_inc(s_stats, 1)
                    dve.wait_ge(s_stats, n + 1)
                    dve.memset(filler[:, :], 0.0)
                    dve.bn_aggr(mv[b][:, :], stats[:, :]).then_inc(s_mv, 1)
                    dve.wait_ge(s_mv, n + 1)
                    dve.tensor_scalar(var_eps[b][:, :], mv[b][:, 1:2], LN_EPS, None, ALU.add).then_inc(s_var, 1)

                def normalise(n, b, stores):
                    dve.wait_ge(s_rstd, n + 1)
                    wait(dve, s_store[b], stores)
                    dve.tensor_scalar(o_out[b][:, :], z[b][:, :], mv[b][:, 0:1], rstd[b][:, 0:1],
                                      ALU.subtract, ALU.mult).then_inc(s_o, 1)

                def finals(i, p, f):
                    for piece, lag in ((mean_square, 1), (scale_rms, 2), (statistics, 4)):
                        if 0 <= f - lag < GB:
                            piece(batches(i, p, f - lag) - GB, f - lag)
                    if 0 <= f - 6 < GB:
                        normalise(batches(i, p, f - 6) - GB, f - 6, i * 32 + 16 * (p - 1))

                def group(i, p):
                    if is_first(i, p):
                        hidden(0, 0)
                    for f in range(FC):
                        if not (is_last(i, p) and f == FC - 1):
                            hidden(chunks(i, p, f) + 1, (f + 1) % 2)
                        if f in T_STEP and not is_last(i, p):
                            transposed_lo(i, p + 1, T_STEP[f])
                        if not is_first(i, p):
                            finals(i, p, f)
                    sums(i, p)

                all_groups(dve, group)
                for f in range(FC):
                    finals(NG // 2, 0, f)

            @block.tensor
            def _(pe):
                pe.wait_ge(s_const, 3)

                def transposes(i, p, b):
                    pe.wait_ge(s_x2[p % 2], i * 16 + 16 * (p // 2 + 1))
                    wait(pe, s_t_lo, batches(i, p, b))
                    for k in range(KC):
                        mm = pe.transpose(p_T[:, k * 128:(k + 1) * 128],
                                          x2_in[p % 2][:, b, k * 128:(k + 1) * 128], ident[:, :])
                    mm.then_inc(s_t, 1)

                def hidden_product(n, p, par, f):
                    wait(pe, s_silu, n - 1)
                    c = slice(f * 128, (f + 1) * 128)
                    for k in range(KC):
                        pe.matmul(p_f1[par][:, :], w1_hi[:, k, c], xT_hi[p][:, k, :], start=(k == 0), stop=False)
                        pe.matmul(p_f1[par][:, :], w1_hi[:, k, c], xT_lo[p][:, k, :], start=False, stop=False)
                        mm = pe.matmul(p_f1[par][:, :], w1_lo[:, k, c], xT_hi[p][:, k, :], start=False, stop=(k == KC - 1))
                    mm.then_inc(s_f1, 1)

                def out_product(i, p, f):
                    n = chunks(i, p, f)
                    par = f % 2
                    pe.wait_ge(s_hid_lo, n + 1)
                    for b in range(GB):
                        if f == 0:
                            wait(pe, s_y, batches(i, p, b) - (GB - 1))
                        c = slice(b * S, (b + 1) * S)
                        pe.matmul(p_f2[b][:, 0:D], hid_hi[par][:, c], w2_hi[:, f, :], start=(f == 0), stop=False)
                        pe.matmul(p_f2[b][:, 0:D], hid_hi[par][:, c], w2_lo[:, f, :], start=False, stop=False)
                        mm = pe.matmul(p_f2[b][:, 0:D], hid_lo[par][:, c], w2_hi[:, f, :], start=False, stop=(f == FC - 1))
                        if b == GB - 1:
                            mm.then_inc(s_hid_used, 1)
                        elif f == FC - 1:
                            mm.then_inc(s_f2[b], 1)

                for b in range(GB):
                    transposes(0, 0, b)
                pe.wait_ge(s_wlo, KC)
                pe.wait_ge(s_t_lo, GB)

                def group(i, p):
                    if is_first(i, p):
                        hidden_product(0, 0, 0, 0)
                        pe.wait_ge(s_wlo, 2 * KC)
                    for f in range(FC):
                        if f < FC - 1:
                            hidden_product(chunks(i, p, f) + 1, p, (f + 1) % 2, f + 1)
                        elif not is_last(i, p):
                            pe.wait_ge(s_t_lo, batches(i, p, GB) + GB)
                            hidden_product(chunks(i, p, f) + 1, 1 - p, 0, 0)
                        out_product(i, p, f)
                        if f in T_STEP and not is_last(i, p):
                            transposes(i, p + 1, T_STEP[f])

                all_groups(pe, group)


def graph_stack_kernel(nc, x, adj, w_gcn, b_gcn, ln_gcn, wqk, bqk, wvo, bv_col, rows_at, w1, b1, w2, rows_ff, out):
    n_batch, S, D = x.shape
    F = b1.shape[0] * b1.shape[1]
    H = wqk.shape[3]
    x1 = nc.dram_tensor("x1_scratch", (n_batch, S, D), F32, kind="Internal").ap()
    x2 = nc.dram_tensor("x2_scratch", (n_batch, S, D), F32, kind="Internal").ap()
    phase_graph_conv(nc, x, adj, w_gcn, b_gcn, ln_gcn, x1, n_batch, S, D)
    phase_attention(nc, x1, adj, wqk, bqk, wvo, bv_col, rows_at, x2, n_batch, S, D, H)
    phase_feed_forward(nc, x1, x2, w1, b1, w2, rows_ff, out, n_batch, S, D, F)


_OUTS = [((64, 128, 384), 'float32')]


def _laid_out(t):
    import numpy as _np
    P, D, F, H, L = 128, 384, 1536, 8, 2
    KC, FC = D // P, F // P
    a = {n: _np.asarray(v) for n, v in t.items()}

    def every_partition(*rows):
        stacked = _np.stack(rows)
        return _np.broadcast_to(stacked, (P, *stacked.shape))

    w = _np.stack([a['L0_gnn_Wl'], a['L0_gnn_Ws'], a['L0_gnn_Wr']], 1)
    w_gcn = w.transpose(0, 3, 1, 2).reshape(L, KC, P, 3, D).transpose(0, 2, 1, 3, 4).reshape(L, P, KC * 3 * D)
    b = _np.stack([a['L0_gnn_bl'], a['L0_gnn_bs'], a['L0_gnn_br']], 1)
    return {
        'x': a['x'],
        'adj': a['adj'],
        'w_gcn': w_gcn,
        'b_gcn': _np.stack([b, b], 0),
        'ln_gcn': every_partition(*_np.stack([a['L0_gnn_ln_w'], a['L0_gnn_ln_b']], 1)),
        'wqk': _np.stack([a['L1_gnn_wq'], a['L1_gnn_wk']]).reshape(2, KC, P, H, D // H),
        'bqk': _np.stack([a['L1_gnn_bq'], a['L1_gnn_bk']]).reshape(2, H // 2, 2, D // H).transpose(0, 2, 3, 1),
        'wvo': _np.stack([a['L1_gnn_wv'], a['L1_gnn_wo']]).reshape(2, KC, P, D).transpose(0, 2, 1, 3).reshape(2, P, KC * D),
        'bv_col': a['L1_gnn_bv'].reshape(KC, P).T,
        'rows_at': every_partition(a['L1_gnn_bo'], a['L1_gnn_alpha1'], a['L1_gnn_gamma1']),
        'w1': a['L1_gnn_w1'].reshape(KC, P, F),
        'b1': a['L1_gnn_b1'].reshape(FC, P).T,
        'w2': a['L1_gnn_w2'].reshape(KC, FC // KC, P, D).transpose(0, 2, 1, 3).reshape(KC, P, FC // KC * D),
        'rows_ff': every_partition(a['L1_gnn_b2'], a['L1_gnn_alpha2'], a['L1_gnn_gamma2']),
    }


def kernel(**inputs):
    import numpy as _np
    import concourse.bacc as _bacc
    from concourse import mybir as _mybir
    from concourse.bass_utils import run_bass_kernel_spmd as _run

    nc = _bacc.Bacc("TRN2", target_bir_lowering=False, num_devices=1)
    arrays, args = {}, []
    for name, a in _laid_out(inputs).items():
        a = _np.ascontiguousarray(a)
        arrays[f"in_{name}_dram"] = a
        args.append(nc.dram_tensor(f"in_{name}_dram", a.shape, _mybir.dt.from_np(a.dtype), kind="ExternalInput").ap())
    for i, (shape, dtype) in enumerate(_OUTS):
        dt = _mybir.dt.from_np(_np.dtype(dtype))
        args.append(nc.dram_tensor(f"out_{i}_dram", shape, dt, kind="ExternalOutput").ap())
    graph_stack_kernel(nc, *args)
    r = _run(nc, [arrays], core_ids=[0])
    got = tuple(r.results[0][f"out_{i}_dram"] for i in range(len(_OUTS)))
    return got[0]
```

```python
from contextlib import ExitStack

import concourse.bass as bass
from concourse import mybir

ALU = mybir.AluOpType
ACT = mybir.ActivationFunctionType
AX = mybir.AxisListType
F32 = mybir.dt.float32
F32R = mybir.dt.float32r


def phase_graph_conv(nc, x, adj, w_gcn, rows_gcn, x1, n_batch, S, D):
    KC = D // 128
    N_LAYER = 2
    LN_EPS_GCN = 1e-12
    LN_EPS_OUT = 1e-5
    ATTN_EPS = 1e-10
    TEMPER_INV = float(D) ** -0.5
    RING = 4
    L, R, SELF = 0, 1, 2
    GAIN, SHIFT = 3, 4

    with ExitStack() as ctx:
        def sb(name, shape, dt=F32):
            return ctx.enter_context(nc.sbuf_tensor(name, shape, dt))

        def sem(name):
            return ctx.enter_context(nc.semaphore(name))

        ident = sb("a_ident", [128, 128])
        masks = sb("a_masks", [128, 2, 128])
        exponent = sb("a_exponent", [128, 1])
        w_raw = [sb(f"a_w_raw{m}", [128, KC * D]) for m in range(3)]
        w_hi = [[sb(f"a_w_hi{l}{m}", [128, KC, D], F32R) for m in range(3)] for l in range(N_LAYER)]
        w_lo = [[sb(f"a_w_lo{l}{m}", [128, KC, D], F32R) for m in range(3)] for l in range(N_LAYER)]
        rows = [sb(f"a_rows{l}", [128, 5, D]) for l in range(N_LAYER)]
        x_in = [sb(f"a_x_in{s}", [128, D]) for s in range(RING)]
        adj_in = [sb(f"a_adj_in{s}", [128, S]) for s in range(RING)]
        hT = [sb(f"a_hT{l}", [128, KC, 128]) for l in range(N_LAYER)]
        hT_hi = [sb(f"a_hT_hi{l}", [128, KC, 128], F32R) for l in range(N_LAYER)]
        hT_lo = [sb(f"a_hT_lo{l}", [128, KC, 128], F32R) for l in range(N_LAYER)]
        neg_max = sb("a_neg_max", [128, 1])
        exp_bias = sb("a_exp_bias", [128, 1])
        expo = sb("a_expo", [128, S])
        z_sum = sb("a_z_sum", [128, 1])
        e_adj = sb("a_e_adj", [128, S])
        e_sum = sb("a_e_sum", [128, 1])
        denom = sb("a_denom", [128, 1])
        r_den = sb("a_r_den", [128, 1])
        attn = sb("a_attn", [128, 2, S])
        diag_scr = sb("a_diag_scr", [128, S])
        diag = sb("a_diag", [128, 1])
        aT_hi = sb("a_aT_hi", [128, 2, 128], F32R)
        aT_lo = sb("a_aT_lo", [128, 2, 128], F32R)
        hl, hr, hs = (sb(f"a_h{c}", [128, D]) for c in "lrs")
        hl_hi, hr_hi = (sb(f"a_h{c}_hi", [128, D], F32R) for c in "lr")
        hl_lo, hr_lo = (sb(f"a_h{c}_lo", [128, D], F32R) for c in "lr")
        ctx_s = sb("a_ctx_s", [128, D])
        stats = sb("a_stats", [128, 6])
        mv = sb("a_mv", [128, 2])
        var_eps = sb("a_var_eps", [128, 1])
        neg_mean = sb("a_neg_mean", [128, 1])
        rstd = sb("a_rstd", [128, 1])
        centred = sb("a_centred", [128, D])
        normed = sb("a_normed", [128, D])
        scaled = sb("a_scaled", [128, D])
        h_nat = sb("a_h_nat", [128, D])
        o_nat = sb("a_o_nat", [128, D])
        y_res = sb("a_y_res", [128, D])
        stats2 = sb("a_stats2", [128, 6])
        mv2 = sb("a_mv2", [128, 2])
        var_eps2 = sb("a_var_eps2", [128, 1])
        neg_mean2 = sb("a_neg_mean2", [128, 1])
        rstd2 = sb("a_rstd2", [128, 1])
        centred2 = sb("a_centred2", [128, D])
        filler = sb("a_filler", [128, 1])
        x1_out = [sb(f"a_x1_out{s}", [128, D]) for s in range(2)]

        def bank(name):
            return ctx.enter_context(nc.psum_tensor(name, [128, 512], F32))

        p_u = bank("a_p_u")
        p_aT = bank("a_p_aT")
        p_T = bank("a_p_T")
        p_hl, p_hs, p_hr = bank("a_p_hl"), bank("a_p_hs"), bank("a_p_hr")
        p_ctx = [bank("a_p_ctx0"), bank("a_p_ctx1")]

        s_const = sem("s_const")
        s_wload = [sem(f"s_wload{m}") for m in range(3)]
        s_rows = [sem(f"s_rows{l}") for l in range(N_LAYER)]
        s_whi = sem("s_whi")
        s_wlo = [sem(f"s_wlo{l}") for l in range(N_LAYER)]
        s_in = [sem(f"s_in{s}") for s in range(RING)]
        s_t = sem("s_t")
        s_t_full = sem("s_t_full")
        s_t_hi = sem("s_t_hi")
        s_t_lo = sem("s_t_lo")
        s_u = sem("s_u")
        s_max = sem("s_max")
        s_bias_exp = sem("s_bias_exp")
        s_exp = sem("s_exp")
        s_ea = sem("s_ea")
        s_den = sem("s_den")
        s_rden = sem("s_rden")
        s_attn = sem("s_attn")
        s_diag = sem("s_diag")
        s_p_hl, s_p_hr, s_p_hs = sem("s_p_hl"), sem("s_p_hr"), sem("s_p_hs")
        s_hl, s_hr, s_hs = sem("s_hl"), sem("s_hr"), sem("s_hs")
        s_hl_hi = sem("s_hl_hi")
        s_hr_hi = sem("s_hr_hi")
        s_hl_lo = sem("s_hl_lo")
        s_hr_lo = sem("s_hr_lo")
        s_aT = sem("s_aT")
        s_aT_hi = sem("s_aT_hi")
        s_aT_lo = sem("s_aT_lo")
        s_ctx = sem("s_ctx")
        s_ctx_s = sem("s_ctx_s")
        s_stats = sem("s_stats")
        s_mv = sem("s_mv")
        s_var = sem("s_var")
        s_mean = sem("s_mean")
        s_centred = sem("s_centred")
        s_rstd = sem("s_rstd")
        s_normed = sem("s_normed")
        s_scaled = sem("s_scaled")
        s_h = sem("s_h")
        s_o = sem("s_o")
        s_y = sem("s_y")
        s_stats2 = sem("s_stats2")
        s_mv2 = sem("s_mv2")
        s_var2 = sem("s_var2")
        s_mean2 = sem("s_mean2")
        s_centred2 = sem("s_centred2")
        s_rstd2 = sem("s_rstd2")
        s_x1 = sem("s_x1")
        s_free = [sem(f"s_x1_free{s}") for s in range(2)]

        def half_no(i, off, layer):
            if isinstance(i, int) and RING * i + off in (0, n_batch):
                return 0 if i == 0 else 2 * n_batch - 1
            return i * (2 * RING) + (2 * off - 1 + layer)

        def wait(eng, s, value):
            if not isinstance(value, int) or value > 0:
                eng.wait_ge(s, value)

        def steps(eng, half):
            for t in range(RING):
                half(0, t, 0)
                if t > 0:
                    half(0, t, 1)
            with eng.Fori(0, n_batch // RING - 2) as i:
                for off in range(RING, 2 * RING):
                    half(i, off, 0)
                    half(i, off, 1)
            for t in range(n_batch - RING, n_batch):
                half(t // RING, t % RING, 0)
                half(t // RING, t % RING, 1)
            half(n_batch // RING, n_batch % RING, 1)

        def buffers_free(n):
            return 1 if isinstance(n, int) and n == 1 else n - 1

        def three_passes(eng, out, a, b, start, stop):
            a_hi, a_lo = a
            b_hi, b_lo = b
            eng.matmul(out, a_hi, b_hi, start=start, stop=False)
            eng.matmul(out, a_hi, b_lo, start=False, stop=False)
            return eng.matmul(out, a_lo, b_hi, start=False, stop=stop)

        def flat(ap):
            return ap.rearrange("p a b -> p (a b)")

        with nc.Block() as block:

            @block.sync
            def _(sp):
                sp.dma_start(x_in[0][:, :], x[0]).then_inc(s_in[0], 16)
                sp.dma_start(w_raw[L][:, :], w_gcn[0, L]).then_inc(s_wload[L], 16)
                sp.dma_start(adj_in[0][:, :], adj[0]).then_inc(s_in[0], 16)
                sp.dma_start(w_raw[R][:, :], w_gcn[0, R]).then_inc(s_wload[R], 16)
                sp.dma_start(rows[0][:, :, :], rows_gcn[0]).then_inc(s_rows[0], 16)
                sp.dma_start(w_raw[SELF][:, :], w_gcn[0, SELF]).then_inc(s_wload[SELF], 16)
                for t in range(1, RING):
                    sp.dma_start(x_in[t][:, :], x[t]).then_inc(s_in[t], 16)
                    sp.dma_start(adj_in[t][:, :], adj[t]).then_inc(s_in[t], 16)
                for m in (L, R, SELF):
                    sp.wait_ge(s_wlo[0], m + 1)
                    sp.dma_start(w_raw[m][:, :], w_gcn[1, m]).then_inc(s_wload[m], 16)
                sp.dma_start(rows[1][:, :, :], rows_gcn[1]).then_inc(s_rows[1], 16)

                def store(t, i, slot):
                    sp.wait_ge(s_x1, t + 1)
                    sp.dma_start(x1[t], x1_out[slot % 2][:, :]).then_inc(s_free[slot % 2], 16)

                with sp.Fori(0, n_batch // RING - 1) as i:
                    for slot in range(RING):
                        done = i * RING + slot
                        sp.wait_ge(s_y, done + 1)
                        sp.dma_start(x_in[slot][:, :], x[done + RING]).then_inc(s_in[slot], 16)
                        sp.dma_start(adj_in[slot][:, :], adj[done + RING]).then_inc(s_in[slot], 16)
                        store(done, i, slot)
                for t in range(n_batch - RING, n_batch):
                    store(t, 0, t % RING)
                for s in range(2):
                    sp.wait_ge(s_free[s], 16 * (n_batch // 2 + 1))

            @block.gpsimd
            def _(pool):
                pool.memset(ident[:, :], 0.0).then_inc(s_const, 1)
                pool.memset(masks[:, :, :], 1.0).then_inc(s_const, 1)
                pool.memset(exponent[:, :], -0.5).then_inc(s_const, 1)
                pool.wait_ge(s_const, 3)
                pool.affine_select(out=ident[:, :], in_=ident[:, :], compare_op=ALU.not_equal, fill=1.0,
                                   base=0, pattern=[[-1, 128]], channel_multiplier=1).then_inc(s_const, 1)
                pool.affine_select(out=masks[:, 0, :], in_=masks[:, 0, :], compare_op=ALU.is_gt, fill=0.0,
                                   base=0, pattern=[[1, 128]], channel_multiplier=-1).then_inc(s_const, 1)
                pool.affine_select(out=masks[:, 1, :], in_=masks[:, 1, :], compare_op=ALU.is_gt, fill=0.0,
                                   base=0, pattern=[[-1, 128]], channel_multiplier=1).then_inc(s_const, 1)
                for s in range(2):
                    pool.memset(x1_out[s][:, :], 0.0).then_inc(s_free[s], 16)

                def norm_scale(q):
                    wait(pool, s_normed, q - 1)
                    pool.wait_ge(s_var, q)
                    pool.tensor_tensor(rstd[:, :], var_eps[:, :], exponent[:, :], ALU.pow).then_inc(s_rstd, 1)

                def norm_gain(q, src):
                    pool.wait_ge(s_normed, q)
                    pool.tensor_tensor(scaled[:, :], normed[:, :], rows[src][:, GAIN, :], ALU.mult).then_inc(s_scaled, 1)

                def norm_shift(q, src, i, off):
                    if src == 0:
                        pool.wait_ge(s_t, q + 1)
                    else:
                        wait(pool, s_y, i * RING + (off - 2))
                    pool.wait_ge(s_scaled, q)
                    dst, done = (h_nat, s_h) if src == 0 else (o_nat, s_o)
                    pool.tensor_tensor(dst[:, :], scaled[:, :], rows[src][:, SHIFT, :], ALU.add).then_inc(done, 1)

                def residual_scale(n):
                    wait(pool, s_x1, n - 1)
                    pool.wait_ge(s_var2, n)
                    pool.tensor_tensor(rstd2[:, :], var_eps2[:, :], exponent[:, :], ALU.pow).then_inc(s_rstd2, 1)

                def transposed_lo(n, layer_to):
                    pool.wait_ge(s_t_hi, n + 1)
                    wait(pool, s_p_hs, buffers_free(n))
                    pool.tensor_tensor(flat(hT_lo[layer_to][:, :, :]), flat(hT[layer_to][:, :, :]),
                                       flat(hT_hi[layer_to][:, :, :].bitcast(F32)), ALU.subtract).then_inc(s_t_lo, 1)

                def half(i, off, layer):
                    q = half_no(i, off, layer)
                    static = isinstance(i, int)
                    t = RING * i + off if static else None
                    first = static and t == 0
                    last = static and t == n_batch
                    src = 0 if static and q == 1 else 1 if last else 1 - layer
                    no_next = static and layer == 1 and t == n_batch - 1
                    if last:
                        transposed_lo(q, 1)
                    if last or (layer == 0 and not (static and t < 3)):
                        residual_scale(i * RING + (off - 2))
                    if not first:
                        norm_scale(q)
                    pool.wait_ge(s_hl_hi, q + 1)
                    wait(pool, s_ctx, q)
                    pool.tensor_tensor(hl_lo[:, :], hl[:, :], hl_hi[:, :].bitcast(F32), ALU.subtract).then_inc(s_hl_lo, 1)
                    late = static and q == 1
                    if first:
                        transposed_lo(1, 0)
                    elif not (last or no_next or late):
                        transposed_lo(q + 1, 1 - layer)
                    if not first:
                        norm_gain(q, src)
                    if first:
                        for m in (L, R, SELF):
                            pool.wait_ge(s_whi, 3 + m + 1)
                            pool.tensor_tensor(flat(w_lo[1][m][:, :, :]), w_raw[m][:, :],
                                               flat(w_hi[1][m][:, :, :].bitcast(F32)), ALU.subtract).then_inc(s_wlo[1], 1)
                        pool.wait_ge(s_rows[1], 16)
                    else:
                        norm_shift(q, src, i, off)
                    if late:
                        transposed_lo(2, 1)

                transposed_lo(0, 0)
                pool.wait_ge(s_rows[0], 16)
                steps(pool, half)
                n = 2 * n_batch
                residual_scale(n_batch - 1)
                norm_scale(n)
                norm_gain(n, 1)
                norm_shift(n, 1, n_batch // RING, n_batch % RING + 1)
                residual_scale(n_batch)

            @block.scalar
            def _(act):
                def transposed(n, layer_to, relu):
                    act.wait_ge(s_t, n + 1)
                    wait(act, s_p_hs, buffers_free(n))
                    act.activation(flat(hT[layer_to][:, :, :]), p_T[:, 0:D],
                                   ACT.Relu if relu else ACT.Copy).then_inc(s_t_full, 1)
                    act.wait_ge(s_t_full, n + 1)
                    act.activation(flat(hT_hi[layer_to][:, :, :]), flat(hT[layer_to][:, :, :]), ACT.Copy).then_inc(s_t_hi, 1)

                def weights_hi(l):
                    for m in (L, R, SELF):
                        act.wait_ge(s_wload[m], 16 * (l + 1))
                        act.activation(flat(w_hi[l][m][:, :, :]), w_raw[m][:, :], ACT.Copy).then_inc(s_whi, 1)

                def half(i, off, layer):
                    q = half_no(i, off, layer)
                    static = isinstance(i, int)
                    t = RING * i + off if static else None
                    first = static and t == 0
                    last = static and t == n_batch
                    no_next = static and layer == 1 and t == n_batch - 1
                    if last:
                        transposed(q, 1, True)
                    late = static and q == 1
                    act.wait_ge(s_bias_exp, q + 1)
                    wait(act, s_attn, q)
                    act.activation(expo[:, :], p_u[:, 0:S], ACT.Exp, bias=exp_bias[:, 0:1],
                                   scale=TEMPER_INV, accum_out=z_sum[:, 0:1]).then_inc(s_exp, 1)
                    if first:
                        transposed(1, 0, False)
                    elif not (last or no_next or late):
                        transposed(q + 1, 1 - layer, layer == 0)
                    act.wait_ge(s_hl, q + 1)
                    wait(act, s_ctx, q)
                    act.activation(hl_hi[:, :], hl[:, :], ACT.Copy).then_inc(s_hl_hi, 1)
                    act.wait_ge(s_aT, q + 1)
                    act.activation(flat(aT_hi[:, :, :]), p_aT[:, 0:2 * S], ACT.Copy).then_inc(s_aT_hi, 1)
                    act.wait_ge(s_hr, q + 1)
                    act.activation(hr_hi[:, :], hr[:, :], ACT.Copy).then_inc(s_hr_hi, 1)
                    if first:
                        weights_hi(1)
                    else:
                        norm_apply(q)
                    if late:
                        transposed(2, 1, True)
                    if last or (layer == 0 and not (static and t < 3)):
                        write_x1(i, off - 3)

                def norm_apply(q):
                    act.wait_ge(s_mean, q)
                    wait(act, s_normed, q - 1)
                    act.activation(centred[:, :], ctx_s[:, :], ACT.Identity, bias=neg_mean[:, 0:1]).then_inc(s_centred, 1)
                    act.wait_ge(s_rstd, q)
                    act.wait_ge(s_centred, q)
                    wait(act, s_scaled, q - 1)
                    act.activation(normed[:, :], centred[:, :], ACT.Copy, scale=rstd[:, 0:1]).then_inc(s_normed, 1)

                def write_x1(i, off):
                    n = i * RING + (off + 1)
                    act.wait_ge(s_mean2, n)
                    wait(act, s_x1, n - 1)
                    act.activation(centred2[:, :], y_res[:, :], ACT.Identity, bias=neg_mean2[:, 0:1]).then_inc(s_centred2, 1)
                    act.wait_ge(s_rstd2, n)
                    slot = off % 2
                    act.wait_ge(s_free[slot], i * (16 * RING // 2) + 16 * (off // 2 + 1))
                    act.wait_ge(s_centred2, n)
                    act.activation(x1_out[slot][:, :], centred2[:, :], ACT.Copy, scale=rstd2[:, 0:1]).then_inc(s_x1, 1)

                transposed(0, 0, False)
                weights_hi(0)
                steps(act, half)
                write_x1(n_batch // RING, n_batch % RING - 2)
                norm_apply(2 * n_batch)
                write_x1(n_batch // RING, n_batch % RING - 1)

            @block.vector
            def _(dve):
                def scores_max(q):
                    dve.wait_ge(s_u, q + 1)
                    wait(dve, s_exp, q)
                    dve.tensor_reduce(neg_max[:, :], p_u[:, 0:S], AX.X, ALU.max, negate=True).then_inc(s_max, 1)
                    dve.wait_ge(s_max, q + 1)
                    dve.tensor_scalar(exp_bias[:, :], neg_max[:, :], TEMPER_INV, None, ALU.mult).then_inc(s_bias_exp, 1)

                def context_sum(q, par):
                    dve.wait_ge(s_hs, q)
                    wait(dve, s_centred, q - 1)
                    dve.wait_ge(s_ctx, q)
                    dve.scalar_tensor_tensor(out=ctx_s[:, :], in0=hs[:, :], scalar=diag[:, 0:1], in1=p_ctx[par][:, 0:D],
                                             op0=ALU.mult, op1=ALU.add).then_inc(s_ctx_s, 1)

                def norm_stats(q):
                    dve.wait_ge(s_ctx_s, q)
                    dve.bn_stats(stats[:, :], ctx_s[:, :]).then_inc(s_stats, 1)

                def norm_mean(q):
                    dve.bn_aggr(mv[:, :], stats[:, :]).then_inc(s_mv, 1)

                def norm_var(q):
                    dve.wait_ge(s_mv, q)
                    wait(dve, s_rstd, q - 1)
                    dve.tensor_scalar(var_eps[:, :], mv[:, 1:2], LN_EPS_GCN, None, ALU.add).then_inc(s_var, 1)
                    wait(dve, s_centred, q - 1)
                    dve.tensor_scalar(neg_mean[:, :], mv[:, 0:1], -1.0, None, ALU.mult).then_inc(s_mean, 1)

                def residual(n, slot):
                    wait(dve, s_centred2, n - 1)
                    dve.wait_ge(s_o, n)
                    dve.scalar_tensor_tensor(out=y_res[:, :], in0=o_nat[:, :], scalar=0.0, in1=x_in[slot][:, :],
                                             op0=ALU.max, op1=ALU.add).then_inc(s_y, 1)

                def residual_stats(n):
                    dve.wait_ge(s_y, n)
                    dve.bn_stats(stats2[:, :], y_res[:, :]).then_inc(s_stats2, 1)

                def residual_mean(n):
                    dve.bn_aggr(mv2[:, :], stats2[:, :]).then_inc(s_mv2, 1)

                def residual_var(n):
                    dve.wait_ge(s_mv2, n)
                    wait(dve, s_rstd2, n - 1)
                    dve.tensor_scalar(var_eps2[:, :], mv2[:, 1:2], LN_EPS_OUT, None, ALU.add).then_inc(s_var2, 1)
                    wait(dve, s_centred2, n - 1)
                    dve.tensor_scalar(neg_mean2[:, :], mv2[:, 0:1], -1.0, None, ALU.mult).then_inc(s_mean2, 1)

                def with_bias(q, layer, m, product, product_done, out, read, out_done):
                    dve.wait_ge(product_done, q + 1)
                    wait(dve, read, q)
                    dve.tensor_tensor(out[:, :], product[:, 0:D], rows[layer][:, m, :], ALU.add).then_inc(out_done, 1)

                def half(i, off, layer):
                    q = half_no(i, off, layer)
                    static = isinstance(i, int)
                    t = RING * i + off if static else None
                    first = static and t == 0
                    last = static and t == n_batch
                    no_next = static and layer == 1 and t == n_batch - 1
                    slot = (off - layer) % RING
                    if first:
                        dve.wait_ge(s_rows[0], 16)
                    elif static and q == 2:
                        dve.wait_ge(s_rows[1], 16)
                    outer = last or (layer == 0 and not (static and t < 3))
                    scores_max(q)
                    if outer:
                        residual_stats(i * RING + (off - 2))
                        dve.wait_ge(s_stats2, i * RING + (off - 2))
                    dve.wait_ge(s_exp, q + 1)
                    dve.scalar_tensor_tensor(out=e_adj[:, :], in0=expo[:, :], scalar=1.0, in1=adj_in[slot][:, :],
                                             op0=ALU.mult, op1=ALU.mult, accum_out=e_sum[:, 0:1]).then_inc(s_ea, 1)
                    if outer:
                        residual_mean(i * RING + (off - 2))
                    if not first:
                        context_sum(q, 0 if last else layer)
                    dve.wait_ge(s_ea, q + 1)
                    dve.scalar_tensor_tensor(out=denom[:, :], in0=z_sum[:, :], scalar=ATTN_EPS, in1=e_sum[:, :],
                                             op0=ALU.mult, op1=ALU.add).then_inc(s_den, 1)
                    if outer:
                        residual_var(i * RING + (off - 2))
                    if not first:
                        norm_stats(q)
                    dve.wait_ge(s_den, q + 1)
                    dve.reciprocal(r_den[:, :], denom[:, :]).then_inc(s_rden, 1)
                    if not first:
                        dve.wait_ge(s_stats, q)
                    dve.wait_ge(s_rden, q + 1)
                    wait(dve, s_aT, q)
                    dve.scalar_tensor_tensor(out=attn[:, :, :], in0=e_adj[:, :].unsqueeze(1).broadcast_to([128, 2, S]),
                                             scalar=r_den[:, 0:1], in1=masks[:, :, :],
                                             op0=ALU.mult, op1=ALU.mult).then_inc(s_attn, 1)
                    with_bias(q, layer, L, p_hl, s_p_hl, hl, s_hl_lo, s_hl)
                    if not first:
                        norm_mean(q)
                    wait(dve, s_diag, q)
                    dve.scalar_tensor_tensor(out=diag_scr[:, :], in0=e_adj[:, :], scalar=r_den[:, 0:1], in1=ident[:, :],
                                             op0=ALU.mult, op1=ALU.mult, accum_out=diag[:, 0:1]).then_inc(s_diag, 1)
                    if not first:
                        norm_var(q)
                    with_bias(q, layer, R, p_hr, s_p_hr, hr, s_hr_lo, s_hr)
                    dve.wait_ge(s_aT_hi, q + 1)
                    dve.tensor_tensor(flat(aT_lo[:, :, :]), p_aT[:, 0:2 * S], flat(aT_hi[:, :, :].bitcast(F32)),
                                      ALU.subtract).then_inc(s_aT_lo, 1)
                    dve.wait_ge(s_hr_hi, q + 1)
                    wait(dve, s_ctx, q)
                    dve.tensor_tensor(hr_lo[:, :], hr[:, :], hr_hi[:, :].bitcast(F32), ALU.subtract).then_inc(s_hr_lo, 1)
                    if layer == 1 and not last and not (static and t < 2):
                        residual(i * RING + (off - 1), (off - 2) % RING)
                    with_bias(q, layer, SELF, p_hs, s_p_hs, hs, s_ctx_s, s_hs)
                    if last:
                        residual(n_batch - 1, (n_batch - 2) % RING)

                for m in (L, R, SELF):
                    dve.wait_ge(s_whi, m + 1)
                    dve.tensor_tensor(flat(w_lo[0][m][:, :, :]), w_raw[m][:, :],
                                      flat(w_hi[0][m][:, :, :].bitcast(F32)), ALU.subtract).then_inc(s_wlo[0], 1)
                steps(dve, half)

                def outer_statistics(n):
                    residual_stats(n)
                    dve.wait_ge(s_stats2, n)
                    dve.memset(filler[:, :], 0.0)
                    residual_mean(n)
                    residual_var(n)

                outer_statistics(n_batch - 1)
                context_sum(2 * n_batch, 1)
                norm_stats(2 * n_batch)
                dve.wait_ge(s_stats, 2 * n_batch)
                dve.memset(filler[:, :], 1.0)
                norm_mean(2 * n_batch)
                norm_var(2 * n_batch)
                residual(n_batch, (n_batch - 1) % RING)
                outer_statistics(n_batch)

            @block.tensor
            def _(pe):
                pe.wait_ge(s_const, 6)

                def transposes(n, src):
                    wait(pe, s_t_full, n)
                    for k in range(KC):
                        mm = pe.transpose(p_T[:, k * 128:(k + 1) * 128], src[:, k * 128:(k + 1) * 128], ident[:, :])
                    mm.then_inc(s_t, 1)

                def scores(q, layer):
                    pe.wait_ge(s_t_full, q + 1)
                    wait(pe, s_exp, q)
                    for k in range(KC):
                        mm = pe.matmul(p_u[:, 0:S], hT[layer][:, k, :], hT[layer][:, k, :], start=(k == 0), stop=(k == KC - 1))
                    mm.then_inc(s_u, 1)

                pe.wait_ge(s_in[0], 32)
                transposes(0, x_in[0])
                scores(0, 0)

                def half(i, off, layer):
                    q = half_no(i, off, layer)
                    static = isinstance(i, int)
                    t = RING * i + off if static else None
                    first = static and t == 0
                    last = static and t == n_batch
                    no_next = static and layer == 1 and t == n_batch - 1
                    par = 0 if first else 1 if last else 1 - layer

                    def project(out, m):
                        if static and q in (0, 2):
                            pe.wait_ge(s_wlo[layer], m + 1)
                        for k in range(KC):
                            mm = three_passes(pe, out[:, 0:D], (hT_hi[layer][:, k, :], hT_lo[layer][:, k, :]),
                                              (w_hi[layer][m][:, k, :], w_lo[layer][m][:, k, :]), k == 0, k == KC - 1)
                        return mm

                    if last:
                        pe.wait_ge(s_h, n_batch)
                        transposes(q, h_nat)
                        scores(q, 1)
                    def next_transposes():
                        if first:
                            pe.wait_ge(s_in[1], 32)
                            transposes(1, x_in[1])
                        elif last or no_next:
                            pass
                        elif layer == 0:
                            pe.wait_ge(s_h, i * RING + off)
                            transposes(q + 1, h_nat)
                        else:
                            nxt = off + 1
                            pe.wait_ge(s_in[nxt % RING], i * 32 + 32 * (nxt // RING + 1))
                            transposes(q + 1, x_in[nxt % RING])

                    pe.wait_ge(s_t_lo, q + 1)
                    wait(pe, s_hl, q)
                    project(p_hl, L).then_inc(s_p_hl, 1)
                    late = static and q == 1
                    if not late:
                        next_transposes()
                    wait(pe, s_hr, q)
                    project(p_hr, R).then_inc(s_p_hr, 1)
                    pe.wait_ge(s_attn, q + 1)
                    wait(pe, s_aT_lo, q)
                    for a in range(2):
                        mm = pe.transpose(p_aT[:, a * 128:(a + 1) * 128], attn[:, a, :], ident[:, :])
                    mm.then_inc(s_aT, 1)
                    wait(pe, s_hs, q)
                    project(p_hs, SELF).then_inc(s_p_hs, 1)
                    if late:
                        next_transposes()
                    if first:
                        scores(1, 0)
                    elif not (last or no_next):
                        scores(q + 1, 1 - layer)
                    pe.wait_ge(s_hl_lo, q + 1)
                    pe.wait_ge(s_hr_lo, q + 1)
                    pe.wait_ge(s_aT_lo, q + 1)
                    wait(pe, s_ctx_s, q - 1)
                    three_passes(pe, p_ctx[par][:, 0:D], (aT_hi[:, 0, :], aT_lo[:, 0, :]), (hl_hi[:, :], hl_lo[:, :]),
                                 True, False)
                    three_passes(pe, p_ctx[par][:, 0:D], (aT_hi[:, 1, :], aT_lo[:, 1, :]), (hr_hi[:, :], hr_lo[:, :]),
                                 False, True).then_inc(s_ctx, 1)

                steps(pe, half)


def phase_attention(nc, x1, adj, wqk, bqk, wvo, bv_col, rows_at, x2, n_batch, S, D, H):
    KC = D // 128
    DH = D // H
    HP = 64
    NCH = H * HP // 128
    GB = 4
    NT = GB * S
    RMS_EPS = 1e-6
    SCALE = float(DH) ** -0.5
    XR = 4
    PERIOD = 2 * GB

    with ExitStack() as ctx:
        def sb(name, shape, dt=F32):
            return ctx.enter_context(nc.sbuf_tensor(name, shape, dt))

        def sem(name):
            return ctx.enter_context(nc.semaphore(name))

        ident = sb("b_ident", [128, 128])
        exponent = sb("b_exponent", [128, 1])
        ones = sb("b_ones", [128, 128])
        w_raw = sb("b_w_raw", [128, KC, H, HP])
        wv_raw = sb("b_wv_raw", [128, KC * D])
        wq_hi, wk_hi = (sb(f"b_w{a}_hi", [128, KC, NCH * 128], F32R) for a in "qk")
        wq_lo, wk_lo = (sb(f"b_w{a}_lo", [128, KC, NCH * 128], F32R) for a in "qk")
        wv_hi, wo_hi = (sb(f"b_w{a}_hi", [128, KC, D], F32R) for a in "vo")
        wv_lo, wo_lo = (sb(f"b_w{a}_lo", [128, KC, D], F32R) for a in "vo")
        b_qk = sb("b_b_qk", [128, 2, NCH])
        bv = sb("b_bv", [128, KC])
        bv_wide = sb("b_bv_wide", [128, KC, 128])
        bv_hi = sb("b_bv_hi", [128, KC, 128], F32R)
        bv_lo = sb("b_bv_lo", [128, KC, 128], F32R)
        rows = sb("b_rows", [128, 3, D])
        bo_all = sb("b_bo_all", [128, D])
        x_in = [sb(f"b_x_in{s}", [128, D]) for s in range(XR)]
        x_res = [sb(f"b_x_res{s}", [128, D]) for s in range(2)]
        x_bo = [sb(f"b_x_bo{s}", [128, D]) for s in range(2)]
        adj_in = [sb(f"b_adj_in{p}", [128, GB, S]) for p in range(2)]
        xT_hi = [sb(f"b_xT_hi{p}", [128, KC, NT], F32R) for p in range(2)]
        xT_lo = [sb(f"b_xT_lo{p}", [128, KC, NT], F32R) for p in range(2)]
        q_sb, k_sb = ([sb(f"b_{a}{p}", [128, NT]) for p in range(2)] for a in "qk")
        v_sb = [sb(f"b_v{p}", [128, GB, D]) for p in range(2)]
        prob = [sb(f"b_prob{p}", [128, 2, GB, S]) for p in range(2)]
        neg_max = [sb(f"b_neg_max{p}", [128, 2 * GB]) for p in range(2)]
        row_sum = [sb(f"b_row_sum{p}", [128, 2, GB]) for p in range(2)]
        r_sum = [sb(f"b_r_sum{p}", [128, 2, GB]) for p in range(2)]
        pT_sb = sb("b_pT_sb", [128, 2 * GB, S])
        context = [sb(f"b_context{p}", [128, GB, D]) for p in range(2)]
        cT_hi = sb("b_cT_hi", [128, KC * 128], F32R)
        cT_lo = sb("b_cT_lo", [128, KC * 128], F32R)
        y = [sb(f"b_y{s}", [128, D]) for s in range(2)]
        square = sb("b_square", [128, D])
        sum_sq = [sb(f"b_sum_sq{s}", [128, 1]) for s in range(2)]
        mean_sq = sb("b_mean_sq", [128, 1])
        r_rms = sb("b_r_rms", [128, 1])
        z = sb("b_z", [128, D])
        x2_out = [sb(f"b_x2_out{s}", [128, D]) for s in range(2)]

        p_q = ctx.enter_context(nc.psum_tensor("b_p_q", [128, NT], F32))
        p_k = ctx.enter_context(nc.psum_tensor("b_p_k", [128, NT], F32))
        p_s = ctx.enter_context(nc.psum_tensor("b_p_s", [128, 2, GB, S], F32))
        p_pT = ctx.enter_context(nc.psum_tensor("b_p_pT", [128, 2 * GB, S], F32))
        p_c = ctx.enter_context(nc.psum_tensor("b_p_c", [128, 512], F32))
        p_m = ctx.enter_context(nc.psum_tensor("b_p_m", [128, 512], F32))

        s_const = sem("b_s_const")
        s_small = sem("b_s_small")
        s_wload = sem("b_s_wload")
        s_whi = sem("b_s_whi")
        s_wlo = sem("b_s_wlo")
        s_bv = sem("b_s_bv")
        s_x = [sem(f"b_s_xin{s}") for s in range(XR)]
        s_xr = [sem(f"b_s_xr{s}") for s in range(2)]
        s_adj = [sem(f"b_s_adj{p}") for p in range(2)]
        s_t, s_t_hi, s_t_lo = sem("b_s_t"), sem("b_s_t_hi"), sem("b_s_t_lo")
        s_q, s_q_sb = sem("b_s_q"), sem("b_s_q_sb")
        s_k, s_k_sb = sem("b_s_k"), sem("b_s_k_sb")
        s_v, s_v_sb = sem("b_s_v"), sem("b_s_v_sb")
        s_sc = sem("b_s_sc")
        s_logit = sem("b_s_logit")
        s_max = sem("b_s_max")
        s_exp = sem("b_s_exp")
        s_rsum = sem("b_s_rsum")
        s_pT, s_pT_sb = sem("b_s_pT"), sem("b_s_pT_sb")
        s_c = sem("b_s_c")
        s_cn = sem("b_s_cn")
        s_cT, s_cT_hi, s_cT_lo = sem("b_s_cT"), sem("b_s_cT_hi"), sem("b_s_cT_lo")
        s_o = sem("b_s_o")
        s_xbo = sem("b_s_xbo")
        s_y, s_sq, s_ms, s_rms = sem("b_s_y"), sem("b_s_sq"), sem("b_s_ms"), sem("b_s_rms")
        s_z, s_x2 = sem("b_s_z"), sem("b_s_x2")
        s_store = [sem(f"b_s_store{s}") for s in range(2)]

        class Item:
            def __init__(self, i, off):
                self.i, self.off = i, off
                self.static = isinstance(i, int)
                self.no = i * PERIOD + off
                self.exists = not self.static or 0 <= self.no < n_batch
                self.sub = off % GB
                self.par = (off // GB) % 2
                self.odd = off % 2

            def plus(self, d):
                return Item(self.i, self.off + d)

            def over(self, m):
                return self.i * (PERIOD // m) + self.off // m

        def wait(eng, s, value):
            if not isinstance(value, int) or value > 0:
                eng.wait_ge(s, value)

        LEAD, TAIL = 5, 7

        def steps(eng, step):
            for n in range(-LEAD, PERIOD):
                step(Item(0, n))
            with eng.Fori(1, n_batch // PERIOD - 1) as i:
                for off in range(PERIOD):
                    step(Item(i, off))
            for n in range(n_batch - PERIOD, n_batch + TAIL):
                step(Item(0, n))

        def three_passes(eng, out, a, b, start, stop):
            a_hi, a_lo = a
            b_hi, b_lo = b
            eng.matmul(out, a_hi, b_hi, start=start, stop=False)
            eng.matmul(out, a_hi, b_lo, start=False, stop=False)
            return eng.matmul(out, a_lo, b_hi, start=False, stop=stop)

        def flat(ap):
            return ap.rearrange("p a b -> p (a b)")

        with nc.Block() as block:

            @block.sync
            def _(sp):
                for s in range(2):
                    sp.dma_start(x_in[s][:, :], x1[s]).then_inc(s_x[s], 16)
                sp.wait_ge(s_const, 4)
                for a in range(2):
                    for h in range(2):
                        sp.dma_start(b_qk[h * HP:h * HP + DH, a, :], bqk[a, h]).then_inc(s_small, 16)
                sp.dma_start(bv[:, :], bv_col).then_inc(s_small, 16)
                sp.dma_start(rows[:, :, :], rows_at).then_inc(s_small, 16)
                sp.dma_start(wv_raw[:, :], wvo[0]).then_inc(s_wload, 16)
                for a in range(2):
                    wait(sp, s_wlo, 1 if a else 0)
                    for k in range(KC):
                        sp.dma_start(w_raw[:, k, :, 0:DH], wqk[a, k]).then_inc(s_wload, 16)
                    if a == 0:
                        continue
                    sp.wait_ge(s_wlo, 2)
                    sp.dma_start(wv_raw[:, :], wvo[1]).then_inc(s_wload, 16)

                def step(n):
                    j = n.plus(7)
                    if j.exists and not (j.static and j.off < 2):
                        wait(sp, s_t, j.no - XR + 1)
                        sp.dma_start(x_in[j.off % XR][:, :], x1[j.no]).then_inc(s_x[j.off % XR], 16)
                    j = n.plus(5)
                    if j.exists:
                        wait(sp, s_logit, j.no * 2 - 2 * (GB + j.sub))
                        sp.dma_start(adj_in[j.par][:, j.sub, :], adj[j.no]).then_inc(s_adj[j.par], 16)
                    j = n.plus(-4)
                    if j.exists:
                        wait(sp, s_xbo, j.no - 1)
                        sp.dma_start(x_res[j.odd][:, :], x1[j.no]).then_inc(s_xr[j.odd], 16)
                    j = n.plus(-7)
                    if j.exists:
                        sp.wait_ge(s_x2, j.no + 1)
                        sp.dma_start(x2[j.no], x2_out[j.odd][:, :]).then_inc(s_store[j.odd], 16)

                for m in range(-7, -LEAD):
                    step(Item(0, m))
                steps(sp, step)
                for s in range(2):
                    sp.wait_ge(s_store[s], 16 * (n_batch // 2))

            @block.gpsimd
            def _(pool):
                pool.memset(w_raw[:, :, :, :], 0.0).then_inc(s_const, 1)
                pool.memset(b_qk[:, :, :], 0.0).then_inc(s_const, 1)
                pool.memset(ident[:, :], 0.0).then_inc(s_const, 1)
                pool.memset(exponent[:, :], -0.5).then_inc(s_const, 1)
                pool.memset(ones[:, :], 1.0).then_inc(s_const, 1)
                pool.wait_ge(s_const, 5)
                pool.affine_select(out=ident[:, :], in_=ident[:, :], compare_op=ALU.not_equal, fill=1.0,
                                   base=0, pattern=[[-1, 128]], channel_multiplier=1).then_inc(s_const, 1)
                pool.wait_ge(s_bv, KC + 4)

                def step(n):
                    j = n.plus(-5)
                    if j.exists:
                        pool.wait_ge(s_xr[j.odd], j.over(2) * 16 + 16)
                        wait(pool, s_y, j.no - 1)
                        pool.tensor_tensor(x_bo[j.odd][:, :], x_res[j.odd][:, :], bo_all[:, :],
                                           ALU.add).then_inc(s_xbo, 1)
                    j = n.plus(-6)
                    if j.exists:
                        pool.wait_ge(s_ms, j.no + 1)
                        pool.tensor_tensor(r_rms[:, :], mean_sq[:, :], exponent[:, :], ALU.pow).then_inc(s_rms, 1)
                        pool.wait_ge(s_z, j.no + 1)
                        wait(pool, s_store[j.odd], j.over(2) * 16)
                        pool.tensor_tensor(x2_out[j.odd][:, :], z[:, :], rows[:, 2, :], ALU.add).then_inc(s_x2, 1)

                steps(pool, step)

            @block.scalar
            def _(act):
                act.wait_ge(s_wload, 16 * (1 + KC))
                act.activation(flat(wq_hi[:, :, :]), w_raw[:, :, :, :].rearrange("p k h d -> p (k h d)"),
                               ACT.Copy).then_inc(s_whi, 1)
                act.activation(flat(wv_hi[:, :, :]), wv_raw[:, :], ACT.Copy).then_inc(s_whi, 1)
                act.wait_ge(s_wload, 16 * (2 + 2 * KC))
                act.activation(flat(wk_hi[:, :, :]), w_raw[:, :, :, :].rearrange("p k h d -> p (k h d)"),
                               ACT.Copy).then_inc(s_whi, 1)
                act.activation(flat(wo_hi[:, :, :]), wv_raw[:, :], ACT.Copy).then_inc(s_whi, 1)
                act.wait_ge(s_small, 16 * 6)
                act.wait_ge(s_const, 5)
                for k in range(KC):
                    act.activation(bv_wide[:, k, :], ones[:, :], ACT.Copy, scale=bv[:, k:k + 1]).then_inc(s_bv, 1)
                act.wait_ge(s_bv, KC)
                act.activation(flat(bv_hi[:, :, :]), flat(bv_wide[:, :, :]), ACT.Copy).then_inc(s_bv, 1)

                def exps(n, h):
                    act.wait_ge(s_max, n.no * 2 + (h + 1))
                    if h == 0:
                        wait(act, s_rsum, n.no - 1)
                    for b in range(GB):
                        e = act.activation(prob[n.odd][:, h, b, :], prob[n.odd][:, h, b, :], ACT.Exp,
                                           bias=neg_max[n.odd][:, h * GB + b:h * GB + b + 1],
                                           accum_out=row_sum[n.odd][:, h, b:b + 1])
                    return e

                def step(n):
                    j = n.plus(5)
                    if j.exists:
                        act.wait_ge(s_t, j.no + 1)
                        act.activation(xT_hi[j.par][:, :, j.sub * S:(j.sub + 1) * S],
                                       p_m[:, 0:D].rearrange("p (k n) -> p k n", k=KC), ACT.Copy).then_inc(s_t_hi, 1)
                    j = n.plus(-1)
                    if j.exists:
                        act.wait_ge(s_pT, j.no + 1)
                        act.activation(flat(pT_sb[:, :, :]), flat(p_pT[:, :, :]), ACT.Copy).then_inc(s_pT_sb, 1)
                    if n.exists:
                        exps(n, 0)
                    j = n.plus(-5)
                    if j.exists:
                        act.wait_ge(s_cT, j.no + 1)
                        act.activation(cT_hi[:, :], p_m[:, 0:D], ACT.Copy).then_inc(s_cT_hi, 1)
                    j = n.plus(1)
                    if j.exists:
                        act.wait_ge(s_q, j.no + 1)
                        act.activation(q_sb[j.odd][:, :], p_q[:, :], ACT.Identity,
                                       bias=b_qk[:, 0, j.sub:j.sub + 1]).then_inc(s_q_sb, 1)
                    if n.exists:
                        exps(n, 1).then_inc(s_exp, 1)
                    j = n.plus(1)
                    if j.exists:
                        act.wait_ge(s_k, j.no + 1)
                        act.activation(k_sb[j.odd][:, :], p_k[:, :], ACT.Identity,
                                       bias=b_qk[:, 1, j.sub:j.sub + 1]).then_inc(s_k_sb, 1)
                    j = n.plus(-5)
                    if j.exists:
                        act.wait_ge(s_y, j.no + 1)
                        wait(act, s_sq, j.no)
                        act.activation(square[:, :], y[j.odd][:, :], ACT.Square,
                                       accum_out=sum_sq[j.odd][:, 0:1]).then_inc(s_sq, 1)

                steps(act, step)

            @block.vector
            def _(dve):
                splits = [(w_raw[:, :, :, :].rearrange("p k h d -> p (k h d)"), wq_hi, wq_lo), (wv_raw[:, :], wv_hi, wv_lo),
                          (w_raw[:, :, :, :].rearrange("p k h d -> p (k h d)"), wk_hi, wk_lo), (wv_raw[:, :], wo_hi, wo_lo)]
                for m, (raw, hi, lo) in enumerate(splits):
                    dve.wait_ge(s_whi, m + 1)
                    dve.tensor_tensor(flat(lo[:, :, :]), raw, flat(hi[:, :, :].bitcast(F32)), ALU.subtract).then_inc(s_wlo, 1)
                dve.wait_ge(s_bv, KC + 1)
                dve.tensor_tensor(flat(bv_lo[:, :, :]), flat(bv_wide[:, :, :]), flat(bv_hi[:, :, :].bitcast(F32)),
                                  ALU.subtract).then_inc(s_bv, 1)
                dve.wait_ge(s_bv, KC + 3)
                dve.tensor_tensor(bo_all[:, :], p_c[:, 0:D], rows[:, 0, :], ALU.add).then_inc(s_bv, 1)

                def step(n):
                    j = n.plus(2)
                    if j.exists:
                        dve.wait_ge(s_v, j.no + 1)
                        dve.tensor_copy(v_sb[j.par][:, j.sub, :], p_m[:, 0:D]).then_inc(s_v_sb, 1)
                    if n.exists:
                        dve.wait_ge(s_adj[n.par], n.over(PERIOD) * (16 * GB) + 16 * GB)
                        wait(dve, s_pT, n.no - 1)
                        for h in range(2):
                            dve.wait_ge(s_sc, n.no * 2 + (h + 1))
                            dve.scalar_tensor_tensor(out=flat(prob[n.odd][:, h, :, :]), in0=flat(p_s[:, h, :, :]), scalar=SCALE,
                                                     in1=flat(adj_in[n.par][:, :, :]), op0=ALU.mult, op1=ALU.add)\
                               .then_inc(s_logit, 1)
                            dve.wait_ge(s_logit, n.no * 2 + (h + 1))
                            dve.tensor_reduce(neg_max[n.odd][:, h * GB:(h + 1) * GB], prob[n.odd][:, h, :, :], AX.X, ALU.max,
                                              negate=True).then_inc(s_max, 1)
                    j = n.plus(5)
                    if j.exists:
                        dve.wait_ge(s_t_hi, j.no + 1)
                        c = slice(j.sub * S, (j.sub + 1) * S)
                        dve.tensor_tensor(xT_lo[j.par][:, :, c], p_m[:, 0:D].rearrange("p (k n) -> p k n", k=KC),
                                          xT_hi[j.par][:, :, c].bitcast(F32), ALU.subtract).then_inc(s_t_lo, 1)
                    j = n.plus(-1)
                    if j.exists:
                        dve.wait_ge(s_exp, j.no + 1)
                        dve.reciprocal(flat(r_sum[j.odd][:, :, :]), flat(row_sum[j.odd][:, :, :])).then_inc(s_rsum, 1)
                    j = n.plus(-2)
                    if j.exists:
                        dve.wait_ge(s_c, j.no + 1)
                        wait(dve, s_rsum, j.no + 1)
                        for h in range(2):
                            head = 2 * j.sub + h
                            c = dve.tensor_tensor(context[j.par][:, :, head * DH:(head + 1) * DH],
                                                  p_c[:, h * GB * DH:(h + 1) * GB * DH].rearrange("p (b d) -> p b d", b=GB),
                                                  r_sum[j.odd][:, h, :].unsqueeze(2).broadcast_to([128, GB, DH]), ALU.mult)
                        c.then_inc(s_cn, 1)
                    j = n.plus(-5)
                    if j.exists:
                        dve.wait_ge(s_cT_hi, j.no + 1)
                        dve.tensor_tensor(cT_lo[:, :], p_m[:, 0:D], cT_hi[:, :].bitcast(F32), ALU.subtract).then_inc(s_cT_lo, 1)
                    j = n.plus(-6)
                    if j.exists:
                        dve.wait_ge(s_sq, j.no + 1)
                        dve.tensor_scalar(mean_sq[:, :], sum_sq[j.odd][:, :], 1.0 / D, RMS_EPS,
                                          ALU.mult, ALU.add).then_inc(s_ms, 1)
                        dve.wait_ge(s_rms, j.no + 1)
                        wait(dve, s_x2, j.no)
                        dve.scalar_tensor_tensor(out=z[:, :], in0=y[j.odd][:, :], scalar=r_rms[:, 0:1], in1=rows[:, 1, :],
                                                 op0=ALU.mult, op1=ALU.mult).then_inc(s_z, 1)
                    j = n.plus(-5)
                    if j.exists:
                        dve.wait_ge(s_xbo, j.no + 1)
                        dve.wait_ge(s_o, j.no + 1)
                        dve.tensor_tensor(y[j.odd][:, :], p_m[:, 0:D], x_bo[j.odd][:, :], ALU.add).then_inc(s_y, 1)

                steps(dve, step)

            @block.tensor
            def _(pe):
                pe.wait_ge(s_const, 6)
                pe.wait_ge(s_wlo, 4)
                pe.wait_ge(s_bv, KC + 2)
                for k in range(KC):
                    mm = three_passes(pe, p_c[:, 0:D], (bv_hi[:, k, :], bv_lo[:, k, :]),
                                      (wo_hi[:, k, :], wo_lo[:, k, :]), k == 0, k == KC - 1)
                mm.then_inc(s_bv, 1)
                pe.wait_ge(s_bv, KC + 4)

                def project(j, out, hi, lo):
                    c = slice(j.sub * 128, (j.sub + 1) * 128)
                    for k in range(KC):
                        mm = three_passes(pe, out[:, :], (hi[:, k, c], lo[:, k, c]),
                                          (xT_hi[j.par][:, k, :], xT_lo[j.par][:, k, :]), k == 0, k == KC - 1)
                    return mm

                def step(n):
                    if n.exists:
                        pe.wait_ge(s_q_sb, n.no + 1)
                        pe.wait_ge(s_k_sb, n.no + 1)
                        wait(pe, s_logit, n.no * 2)
                        for h in range(2):
                            r = slice(h * HP, h * HP + DH)
                            for b in range(GB):
                                c = slice(b * S, (b + 1) * S)
                                mm = pe.matmul(p_s[:, h, b, :], q_sb[n.odd][r, c], k_sb[n.odd][r, c], start=True, stop=True)
                            if h == 0:
                                mm.then_inc(s_sc, 1)
                        mm.then_inc(s_sc, 1)
                    j = n.plus(5)
                    if j.exists:
                        if n.plus(2).exists:
                            pe.wait_ge(s_v_sb, n.plus(2).no + 1)
                        elif not (j.static and j.no == 0):
                            wait(pe, s_t_lo, j.no)
                        pe.wait_ge(s_x[j.off % XR], j.over(XR) * 16 + 16)
                        for k in range(KC):
                            mm = pe.transpose(p_m[:, k * 128:(k + 1) * 128], x_in[j.off % XR][:, k * 128:(k + 1) * 128],
                                              ident[:, :])
                        mm.then_inc(s_t, 1)
                    j = n.plus(-1)
                    if j.exists:
                        pe.wait_ge(s_exp, j.no + 1)
                        wait(pe, s_pT_sb, j.no)
                        for h in range(2):
                            for b in range(GB):
                                mm = pe.transpose(p_pT[:, h * GB + b, :], prob[j.odd][:, h, b, :], ident[:, :])
                        mm.then_inc(s_pT, 1)
                    j = n.plus(1)
                    if j.exists:
                        pe.wait_ge(s_t_lo, j.no - j.sub + GB)
                        wait(pe, s_q_sb, j.no)
                        project(j, p_q, wq_hi, wq_lo).then_inc(s_q, 1)
                    j = n.plus(-5)
                    if j.exists:
                        pe.wait_ge(s_cn, j.no - j.sub + GB)
                        if n.plus(5).exists:
                            pe.wait_ge(s_t_lo, n.plus(5).no + 1)
                        elif n.plus(2).exists:
                            pe.wait_ge(s_v_sb, n.plus(2).no + 1)
                        wait(pe, s_y, j.no)
                        for k in range(KC):
                            mm = pe.transpose(p_m[:, k * 128:(k + 1) * 128],
                                              context[j.par][:, j.sub, k * 128:(k + 1) * 128], ident[:, :])
                        mm.then_inc(s_cT, 1)
                    j = n.plus(1)
                    if j.exists:
                        wait(pe, s_k_sb, j.no)
                        project(j, p_k, wk_hi, wk_lo).then_inc(s_k, 1)
                    j = n.plus(-5)
                    if j.exists:
                        pe.wait_ge(s_cT_lo, j.no + 1)
                        for k in range(KC):
                            c = slice(k * 128, (k + 1) * 128)
                            mm = three_passes(pe, p_m[:, 0:D], (cT_hi[:, c], cT_lo[:, c]),
                                              (wo_hi[:, k, :], wo_lo[:, k, :]), k == 0, k == KC - 1)
                        mm.then_inc(s_o, 1)
                    j = n.plus(-1)
                    if j.exists:
                        pe.wait_ge(s_pT_sb, j.no + 1)
                        pe.wait_ge(s_v_sb, j.no - j.sub + GB)
                        wait(pe, s_cn, j.no)
                        for h in range(2):
                            head = 2 * j.sub + h
                            d = slice(head * DH, (head + 1) * DH)
                            for b in range(GB):
                                i = h * GB + b
                                mm = pe.matmul(p_c[:, i * DH:(i + 1) * DH], pT_sb[:, i, :], v_sb[j.par][:, b, d],
                                               start=True, stop=True)
                        mm.then_inc(s_c, 1)
                    j = n.plus(3)
                    if j.exists:
                        pe.wait_ge(s_t_lo, j.no + 1)
                        if n.plus(-5).exists:
                            pe.wait_ge(s_y, n.plus(-5).no + 1)
                        elif n.plus(5).exists:
                            pe.wait_ge(s_t_lo, n.plus(5).no + 1)
                        for k in range(KC):
                            c = slice(j.sub * S, (j.sub + 1) * S)
                            mm = three_passes(pe, p_m[:, 0:D], (xT_hi[j.par][:, k, c], xT_lo[j.par][:, k, c]),
                                              (wv_hi[:, k, :], wv_lo[:, k, :]), k == 0, k == KC - 1)
                        mm.then_inc(s_v, 1)

                steps(pe, step)


def phase_feed_forward(nc, x1, x2, w1, b1, w2, rows_ff, out, n_batch, S, D, F):
    KC = D // 128
    FC = F // 128
    GB = 4
    NG = n_batch // GB
    NT = GB * S
    RMS_EPS = 1e-6
    LN_EPS = 1e-5
    T_STEP = {2: 0, 4: 1, 6: 2, 8: 3}

    with ExitStack() as ctx:
        def sb(name, shape, dt=F32):
            return ctx.enter_context(nc.sbuf_tensor(name, shape, dt))

        def sem(name):
            return ctx.enter_context(nc.semaphore(name))

        ident = sb("c_ident", [128, 128])
        exponent = sb("c_exponent", [128, 1])
        w_raw = sb("c_w_raw", [128, F])
        w1_hi = sb("c_w1_hi", [128, KC, F], F32R)
        w1_lo = sb("c_w1_lo", [128, KC, F], F32R)
        w2_hi = sb("c_w2_hi", [128, FC, D], F32R)
        w2_lo = sb("c_w2_lo", [128, FC, D], F32R)
        b1_col = sb("c_b1_col", [128, FC])
        rows = sb("c_rows", [128, 3, D])
        x2_in = [sb(f"c_x2_in{p}", [128, GB, D]) for p in range(2)]
        x1_in = [sb(f"c_x1_in{p}", [128, GB, D]) for p in range(2)]
        xT_hi = [sb(f"c_xT_hi{p}", [128, KC, NT], F32R) for p in range(2)]
        xT_lo = [sb(f"c_xT_lo{p}", [128, KC, NT], F32R) for p in range(2)]
        hid = sb("c_hid", [128, NT])
        hid_hi = [sb(f"c_hid_hi{p}", [128, NT], F32R) for p in range(2)]
        hid_lo = [sb(f"c_hid_lo{p}", [128, NT], F32R) for p in range(2)]
        y = [sb(f"c_y{b}", [128, D]) for b in range(GB)]
        square = sb("c_square", [128, D])
        sum_sq = [sb(f"c_sum_sq{b}", [128, 1]) for b in range(GB)]
        mean_sq = [sb(f"c_mean_sq{b}", [128, 1]) for b in range(GB)]
        r_rms = [sb(f"c_r_rms{b}", [128, 1]) for b in range(GB)]
        z = [sb(f"c_z{b}", [128, D]) for b in range(GB)]
        stats = sb("c_stats", [128, 6])
        mv = [sb(f"c_mv{b}", [128, 2]) for b in range(GB)]
        var_eps = [sb(f"c_var_eps{b}", [128, 1]) for b in range(GB)]
        rstd = [sb(f"c_rstd{b}", [128, 1]) for b in range(GB)]
        filler = sb("c_filler", [128, 1])
        o_out = [sb(f"c_o_out{b}", [128, D]) for b in range(GB)]

        def bank(name):
            return ctx.enter_context(nc.psum_tensor(name, [128, 512], F32))

        p_f1 = [bank("c_p_f1_0"), bank("c_p_f1_1")]
        p_f2 = [bank(f"c_p_f2_{b}") for b in range(GB)]
        p_T = bank("c_p_T")

        s_const = sem("c_s_const")
        s_small = sem("c_s_small")
        s_wload = sem("c_s_wload")
        s_whi = sem("c_s_whi")
        s_wlo = sem("c_s_wlo")
        s_x2 = [sem(f"c_s_x2_{p}") for p in range(2)]
        s_x1 = [sem(f"c_s_x1_{p}") for p in range(2)]
        s_t = sem("c_s_t")
        s_t_hi = sem("c_s_t_hi")
        s_t_lo = sem("c_s_t_lo")
        s_f1 = sem("c_s_f1")
        s_silu = sem("c_s_silu")
        s_hid_hi = sem("c_s_hid_hi")
        s_hid_lo = sem("c_s_hid_lo")
        s_hid_used = sem("c_s_hid_used")
        s_f2 = [sem(f"c_s_f2_{b}") for b in range(GB)]
        s_xb = sem("c_s_xb")
        s_xg = sem("c_s_xg")
        s_y = sem("c_s_y")
        s_sq = sem("c_s_sq")
        s_ms = sem("c_s_ms")
        s_rms = sem("c_s_rms")
        s_z = sem("c_s_z")
        s_sum = sem("c_s_sum")
        s_stats = sem("c_s_stats")
        s_mv = sem("c_s_mv")
        s_var = sem("c_s_var")
        s_rstd = sem("c_s_rstd")
        s_o = sem("c_s_o")
        s_store = [sem(f"c_s_store{b}") for b in range(GB)]

        def wait(eng, s, value):
            if not isinstance(value, int) or value > 0:
                eng.wait_ge(s, value)

        def chunks(i, p, f):
            return i * (2 * FC) + (p * FC + f)

        def batches(i, p, b):
            return i * (2 * GB) + (p * GB + b)

        def groups(i, p):
            return i * 2 + p

        def is_last(i, p):
            return isinstance(i, int) and 2 * i + p == NG - 1

        def is_first(i, p):
            return isinstance(i, int) and 2 * i + p == 0

        def all_groups(eng, group):
            for p in range(2):
                group(0, p)
            with eng.Fori(1, NG // 2 - 1) as i:
                for p in range(2):
                    group(i, p)
            for p in range(2):
                group(NG // 2 - 1, p)

        x1_v = x1.rearrange("(g b) s d -> g s b d", b=GB)
        x2_v = x2.rearrange("(g b) s d -> g s b d", b=GB)
        W_PARTS = [(w1[k], w1_hi[:, k, :], w1_lo[:, k, :], F) for k in range(KC)]
        W_PARTS += [(w2[k], w2_hi[:, k * (FC // KC):(k + 1) * (FC // KC), :].rearrange("p c n -> p (c n)"),
                     w2_lo[:, k * (FC // KC):(k + 1) * (FC // KC), :].rearrange("p c n -> p (c n)"), D * FC // KC)
                    for k in range(KC)]

        with nc.Block() as block:

            @block.sync
            def _(sp):
                sp.dma_start(x2_in[0][:, :, :], x2_v[0]).then_inc(s_x2[0], 16)
                sp.dma_start(b1_col[:, :], b1).then_inc(s_small, 16)
                sp.dma_start(rows[:, :, :], rows_ff).then_inc(s_small, 16)
                for n, (src, _, _, width) in enumerate(W_PARTS):
                    wait(sp, s_wlo, n)
                    sp.dma_start(w_raw[:, 0:width], src).then_inc(s_wload, 16)
                sp.dma_start(x1_in[0][:, :, :], x1_v[0]).then_inc(s_x1[0], 16)

                def group(i, p):
                    if not is_last(i, p):
                        wait(sp, s_y, batches(i, p, 0))
                        wait(sp, s_xb, batches(i, p, 0))
                        sp.dma_start(x2_in[1 - p][:, :, :], x2_v[groups(i, p) + 1]).then_inc(s_x2[1 - p], 16)
                        wait(sp, s_sum, batches(i, p, 0))
                        sp.dma_start(x1_in[1 - p][:, :, :], x1_v[groups(i, p) + 1]).then_inc(s_x1[1 - p], 16)
                    if not is_first(i, p):
                        for b in range(GB):
                            n = i * (2 * GB) + (p * GB + b - GB)
                            sp.wait_ge(s_o, n + 1)
                            sp.dma_start(out[n], o_out[b][:, :]).then_inc(s_store[b], 16)

                all_groups(sp, group)
                for b in range(GB):
                    n = n_batch - GB + b
                    sp.wait_ge(s_o, n + 1)
                    sp.dma_start(out[n], o_out[b][:, :]).then_inc(s_store[b], 16)
                for b in range(GB):
                    sp.wait_ge(s_store[b], 16 * NG)

            @block.gpsimd
            def _(pool):
                pool.memset(ident[:, :], 0.0).then_inc(s_const, 1)
                pool.memset(exponent[:, :], -0.5).then_inc(s_const, 1)
                pool.wait_ge(s_const, 2)
                pool.affine_select(out=ident[:, :], in_=ident[:, :], compare_op=ALU.not_equal, fill=1.0,
                                   base=0, pattern=[[-1, 128]], channel_multiplier=1).then_inc(s_const, 1)
                pool.wait_ge(s_small, 32)

                def finals(i, p):
                    for f in range(FC):
                        if 0 <= f - 1 < GB:
                            b = f - 1
                            pool.wait_ge(s_ms, batches(i, p, b) - GB + 1)
                            pool.tensor_tensor(r_rms[b][:, :], mean_sq[b][:, :], exponent[:, :],
                                               ALU.pow).then_inc(s_rms, 1)
                        if 0 <= f - 2 < GB:
                            b = f - 2
                            pool.wait_ge(s_z, batches(i, p, b) - GB + 1)
                            pool.wait_ge(s_xg, batches(i, p, b) - GB + 1)
                            pool.tensor_tensor(z[b][:, :], z[b][:, :], x1_in[1 - p][:, b, :], ALU.add).then_inc(s_sum, 1)
                        if 0 <= f - 4 < GB:
                            b = f - 4
                            pool.wait_ge(s_var, batches(i, p, b) - GB + 1)
                            pool.tensor_tensor(rstd[b][:, :], var_eps[b][:, :], exponent[:, :],
                                               ALU.pow).then_inc(s_rstd, 1)

                def group(i, p):
                    if not is_first(i, p):
                        finals(i, p)
                    for b in range(GB):
                        pool.wait_ge(s_x2[p], i * 16 + 16)
                        pool.wait_ge(s_t, batches(i, p, b) + 1)
                        pool.tensor_tensor(x2_in[p][:, b, :], x2_in[p][:, b, :], rows[:, 0, :], ALU.add).then_inc(s_xb, 1)
                    for b in range(GB):
                        pool.wait_ge(s_x1[p], i * 16 + 16)
                        pool.tensor_tensor(x1_in[p][:, b, :], x1_in[p][:, b, :], rows[:, 2, :], ALU.add).then_inc(s_xg, 1)

                all_groups(pool, group)
                finals(NG // 2, 0)

            @block.scalar
            def _(act):
                def transposed_hi(i, p, b):
                    act.wait_ge(s_t, batches(i, p, b) + 1)
                    act.activation(xT_hi[p % 2][:, :, b * S:(b + 1) * S],
                                   p_T[:, 0:D].rearrange("p (k n) -> p k n", k=KC), ACT.Copy).then_inc(s_t_hi, 1)

                for b in range(GB):
                    transposed_hi(0, 0, b)
                for n, (_, hi, _, width) in enumerate(W_PARTS):
                    act.wait_ge(s_wload, 16 * (n + 1))
                    act.activation(hi, w_raw[:, 0:width], ACT.Copy).then_inc(s_whi, 1)
                act.wait_ge(s_small, 32)

                def silu(n, par, f):
                    act.wait_ge(s_f1, n + 1)
                    wait(act, s_hid_lo, n)
                    act.activation(hid[:, :], p_f1[par][:, :], ACT.Silu, bias=b1_col[:, f:f + 1]).then_inc(s_silu, 1)

                def squares(i, p):
                    for b in range(GB):
                        n = batches(i, p, b)
                        act.wait_ge(s_y, n + 1)
                        wait(act, s_sq, n)
                        act.activation(square[:, :], y[b][:, :], ACT.Square,
                                       accum_out=sum_sq[b][:, 0:1]).then_inc(s_sq, 1)

                def group(i, p):
                    if is_first(i, p):
                        silu(0, 0, 0)
                    for f in range(FC):
                        if not (is_last(i, p) and f == FC - 1):
                            silu(chunks(i, p, f) + 1, (f + 1) % 2, (f + 1) % FC)
                        if f in T_STEP and not is_last(i, p):
                            transposed_hi(i, p + 1, T_STEP[f])
                        if f == 0 and not is_first(i, p):
                            squares(i, p - 1)

                all_groups(act, group)
                squares(NG // 2, -1)

            @block.vector
            def _(dve):
                def transposed_lo(i, p, b):
                    dve.wait_ge(s_t_hi, batches(i, p, b) + 1)
                    dve.tensor_tensor(xT_lo[p % 2][:, :, b * S:(b + 1) * S],
                                      p_T[:, 0:D].rearrange("p (k n) -> p k n", k=KC),
                                      xT_hi[p % 2][:, :, b * S:(b + 1) * S].bitcast(F32), ALU.subtract).then_inc(s_t_lo, 1)

                for b in range(GB):
                    transposed_lo(0, 0, b)
                for n, (_, hi, lo, width) in enumerate(W_PARTS):
                    dve.wait_ge(s_whi, n + 1)
                    dve.tensor_tensor(lo, w_raw[:, 0:width], hi.bitcast(F32), ALU.subtract).then_inc(s_wlo, 1)
                dve.wait_ge(s_small, 32)

                def hidden(n, par):
                    dve.wait_ge(s_silu, n + 1)
                    wait(dve, s_hid_used, n - 1)
                    dve.tensor_copy(hid_hi[par][:, :], hid[:, :]).then_inc(s_hid_hi, 1)
                    dve.wait_ge(s_hid_hi, n + 1)
                    dve.tensor_tensor(hid_lo[par][:, :], hid[:, :], hid_hi[par][:, :].bitcast(F32),
                                      ALU.subtract).then_inc(s_hid_lo, 1)

                def sums(i, p):
                    for b in range(GB):
                        n = batches(i, p, b)
                        dve.wait_ge(s_xb, n + 1)
                        if b < GB - 1:
                            dve.wait_ge(s_f2[b], groups(i, p) + 1)
                        else:
                            dve.wait_ge(s_hid_used, chunks(i, p, FC))
                        dve.tensor_tensor(y[b][:, :], p_f2[b][:, 0:D], x2_in[p][:, b, :], ALU.add).then_inc(s_y, 1)

                def mean_square(n, b):
                    dve.wait_ge(s_sq, n + 1)
                    dve.tensor_scalar(mean_sq[b][:, :], sum_sq[b][:, :], 1.0 / D, RMS_EPS,
                                      ALU.mult, ALU.add).then_inc(s_ms, 1)

                def scale_rms(n, b):
                    dve.wait_ge(s_rms, n + 1)
                    dve.scalar_tensor_tensor(out=z[b][:, :], in0=y[b][:, :], scalar=r_rms[b][:, 0:1],
                                             in1=rows[:, 1, :], op0=ALU.mult, op1=ALU.mult).then_inc(s_z, 1)

                def statistics(n, b):
                    dve.wait_ge(s_sum, n + 1)
                    dve.bn_stats(stats[:, :], z[b][:, :]).then_inc(s_stats, 1)
                    dve.wait_ge(s_stats, n + 1)
                    dve.memset(filler[:, :], 0.0)
                    dve.bn_aggr(mv[b][:, :], stats[:, :]).then_inc(s_mv, 1)
                    dve.wait_ge(s_mv, n + 1)
                    dve.tensor_scalar(var_eps[b][:, :], mv[b][:, 1:2], LN_EPS, None, ALU.add).then_inc(s_var, 1)

                def normalise(n, b, stores):
                    dve.wait_ge(s_rstd, n + 1)
                    wait(dve, s_store[b], stores)
                    dve.tensor_scalar(o_out[b][:, :], z[b][:, :], mv[b][:, 0:1], rstd[b][:, 0:1],
                                      ALU.subtract, ALU.mult).then_inc(s_o, 1)

                def finals(i, p, f):
                    for piece, lag in ((mean_square, 1), (scale_rms, 2), (statistics, 4)):
                        if 0 <= f - lag < GB:
                            piece(batches(i, p, f - lag) - GB, f - lag)
                    if 0 <= f - 6 < GB:
                        normalise(batches(i, p, f - 6) - GB, f - 6, i * 32 + 16 * (p - 1))

                def group(i, p):
                    if is_first(i, p):
                        hidden(0, 0)
                    for f in range(FC):
                        if not (is_last(i, p) and f == FC - 1):
                            hidden(chunks(i, p, f) + 1, (f + 1) % 2)
                        if f in T_STEP and not is_last(i, p):
                            transposed_lo(i, p + 1, T_STEP[f])
                        if not is_first(i, p):
                            finals(i, p, f)
                    sums(i, p)

                all_groups(dve, group)
                for f in range(FC):
                    finals(NG // 2, 0, f)

            @block.tensor
            def _(pe):
                pe.wait_ge(s_const, 3)

                def transposes(i, p, b):
                    pe.wait_ge(s_x2[p % 2], i * 16 + 16 * (p // 2 + 1))
                    wait(pe, s_t_lo, batches(i, p, b))
                    for k in range(KC):
                        mm = pe.transpose(p_T[:, k * 128:(k + 1) * 128],
                                          x2_in[p % 2][:, b, k * 128:(k + 1) * 128], ident[:, :])
                    mm.then_inc(s_t, 1)

                def hidden_product(n, p, par, f):
                    wait(pe, s_silu, n - 1)
                    c = slice(f * 128, (f + 1) * 128)
                    for k in range(KC):
                        pe.matmul(p_f1[par][:, :], w1_hi[:, k, c], xT_hi[p][:, k, :], start=(k == 0), stop=False)
                        pe.matmul(p_f1[par][:, :], w1_hi[:, k, c], xT_lo[p][:, k, :], start=False, stop=False)
                        mm = pe.matmul(p_f1[par][:, :], w1_lo[:, k, c], xT_hi[p][:, k, :], start=False, stop=(k == KC - 1))
                    mm.then_inc(s_f1, 1)

                def out_product(i, p, f):
                    n = chunks(i, p, f)
                    par = f % 2
                    pe.wait_ge(s_hid_lo, n + 1)
                    for b in range(GB):
                        if f == 0:
                            wait(pe, s_y, batches(i, p, b) - (GB - 1))
                        c = slice(b * S, (b + 1) * S)
                        pe.matmul(p_f2[b][:, 0:D], hid_hi[par][:, c], w2_hi[:, f, :], start=(f == 0), stop=False)
                        pe.matmul(p_f2[b][:, 0:D], hid_hi[par][:, c], w2_lo[:, f, :], start=False, stop=False)
                        mm = pe.matmul(p_f2[b][:, 0:D], hid_lo[par][:, c], w2_hi[:, f, :], start=False, stop=(f == FC - 1))
                        if b == GB - 1:
                            mm.then_inc(s_hid_used, 1)
                        elif f == FC - 1:
                            mm.then_inc(s_f2[b], 1)

                for b in range(GB):
                    transposes(0, 0, b)
                pe.wait_ge(s_wlo, KC)
                pe.wait_ge(s_t_lo, GB)

                def group(i, p):
                    if is_first(i, p):
                        hidden_product(0, 0, 0, 0)
                        pe.wait_ge(s_wlo, 2 * KC)
                    for f in range(FC):
                        if f < FC - 1:
                            hidden_product(chunks(i, p, f) + 1, p, (f + 1) % 2, f + 1)
                        elif not is_last(i, p):
                            pe.wait_ge(s_t_lo, batches(i, p, GB) + GB)
                            hidden_product(chunks(i, p, f) + 1, 1 - p, 0, 0)
                        out_product(i, p, f)
                        if f in T_STEP and not is_last(i, p):
                            transposes(i, p + 1, T_STEP[f])

                all_groups(pe, group)


def graph_stack_kernel(nc, x, adj, w_gcn, rows_gcn, wqk, bqk, wvo, bv_col, rows_at, w1, b1, w2, rows_ff, out):
    n_batch, S, D = x.shape
    F = b1.shape[0] * b1.shape[1]
    H = wqk.shape[3]
    x1 = nc.dram_tensor("x1_scratch", (n_batch, S, D), F32, kind="Internal").ap()
    x2 = nc.dram_tensor("x2_scratch", (n_batch, S, D), F32, kind="Internal").ap()
    phase_graph_conv(nc, x, adj, w_gcn, rows_gcn, x1, n_batch, S, D)
    phase_attention(nc, x1, adj, wqk, bqk, wvo, bv_col, rows_at, x2, n_batch, S, D, H)
    phase_feed_forward(nc, x1, x2, w1, b1, w2, rows_ff, out, n_batch, S, D, F)


_OUTS = [((64, 128, 384), 'float32')]


def _laid_out(t):
    import numpy as _np
    P, D, F, H, L = 128, 384, 1536, 8, 2
    KC, FC = D // P, F // P
    a = {n: _np.asarray(v) for n, v in t.items()}

    def every_partition(*rows):
        stacked = _np.stack(rows)
        return _np.broadcast_to(stacked, (P, *stacked.shape))

    w = _np.stack([a['L0_gnn_Wl'], a['L0_gnn_Wr'], a['L0_gnn_Ws']], 1)
    w_gcn = w.transpose(0, 1, 3, 2).reshape(L, 3, KC, P, D).transpose(0, 1, 3, 2, 4).reshape(L, 3, P, KC * D)
    rows_gcn = _np.stack([a['L0_gnn_bl'], a['L0_gnn_br'], a['L0_gnn_bs'], a['L0_gnn_ln_w'], a['L0_gnn_ln_b']], 1)
    return {
        'x': a['x'],
        'adj': a['adj'],
        'w_gcn': w_gcn,
        'rows_gcn': _np.broadcast_to(rows_gcn[:, None], (L, P, 5, D)),
        'wqk': _np.stack([a['L1_gnn_wq'], a['L1_gnn_wk']]).reshape(2, KC, P, H, D // H),
        'bqk': _np.stack([a['L1_gnn_bq'], a['L1_gnn_bk']]).reshape(2, H // 2, 2, D // H).transpose(0, 2, 3, 1),
        'wvo': _np.stack([a['L1_gnn_wv'], a['L1_gnn_wo']]).reshape(2, KC, P, D).transpose(0, 2, 1, 3).reshape(2, P, KC * D),
        'bv_col': a['L1_gnn_bv'].reshape(KC, P).T,
        'rows_at': every_partition(a['L1_gnn_bo'], a['L1_gnn_alpha1'], a['L1_gnn_gamma1']),
        'w1': a['L1_gnn_w1'].reshape(KC, P, F),
        'b1': a['L1_gnn_b1'].reshape(FC, P).T,
        'w2': a['L1_gnn_w2'].reshape(KC, FC // KC, P, D).transpose(0, 2, 1, 3).reshape(KC, P, FC // KC * D),
        'rows_ff': every_partition(a['L1_gnn_b2'], a['L1_gnn_alpha2'], a['L1_gnn_gamma2']),
    }


def kernel(**inputs):
    import numpy as _np
    import concourse.bacc as _bacc
    from concourse import mybir as _mybir
    from concourse.bass_utils import run_bass_kernel_spmd as _run

    nc = _bacc.Bacc("TRN2", target_bir_lowering=False, num_devices=1)
    arrays, args = {}, []
    for name, a in _laid_out(inputs).items():
        a = _np.ascontiguousarray(a)
        arrays[f"in_{name}_dram"] = a
        args.append(nc.dram_tensor(f"in_{name}_dram", a.shape, _mybir.dt.from_np(a.dtype), kind="ExternalInput").ap())
    for i, (shape, dtype) in enumerate(_OUTS):
        dt = _mybir.dt.from_np(_np.dtype(dtype))
        args.append(nc.dram_tensor(f"out_{i}_dram", shape, dt, kind="ExternalOutput").ap())
    graph_stack_kernel(nc, *args)
    r = _run(nc, [arrays], core_ids=[0])
    got = tuple(r.results[0][f"out_{i}_dram"] for i in range(len(_OUTS)))
    return got[0]
```

```python
from contextlib import ExitStack

import concourse.bass as bass
from concourse import mybir

ALU = mybir.AluOpType
ACT = mybir.ActivationFunctionType
AX = mybir.AxisListType
F32 = mybir.dt.float32
F32R = mybir.dt.float32r


def phase_graph_conv(nc, ident, exponent, x_ring, x1_out, s_free, s_x1_in, x, x_T, adj, w_gcn, rows_gcn, x1,
                     w_attn, w_split, n_batch, S, D, H):
    KC = D // 128
    N_LAYER = 2
    LN_EPS_GCN = 1e-12
    LN_EPS_OUT = 1e-5
    ATTN_EPS = 1e-10
    TEMPER_INV = float(D) ** -0.5
    RING = 4
    L, R, SELF = 0, 1, 2
    GAIN, SHIFT = 3, 4

    with ExitStack() as ctx:
        def sb(name, shape, dt=F32):
            return ctx.enter_context(nc.sbuf_tensor(name, shape, dt))

        def sem(name):
            return ctx.enter_context(nc.semaphore(name))

        masks = sb("a_masks", [128, 2, 128])
        w_raw = [sb(f"a_w_raw{m}", [128, KC * D]) for m in range(3)]
        w_hi = [[sb(f"a_w_hi{l}{m}", [128, KC, D], F32R) for m in range(3)] for l in range(N_LAYER)]
        w_lo = [[sb(f"a_w_lo{l}{m}", [128, KC, D], F32R) for m in range(3)] for l in range(N_LAYER)]
        rows = [sb(f"a_rows{l}", [128, 5, D]) for l in range(N_LAYER)]
        x_in = x_ring
        adj_in = [sb(f"a_adj_in{s}", [128, S]) for s in range(RING)]
        xT_in = [sb(f"a_xT_in{p}", [128, KC, 128]) for p in range(2)]
        hT = sb("a_hT", [128, KC, 128])
        hT_hi = [sb(f"a_hT_hi{l}", [128, KC, 128], F32R) for l in range(N_LAYER)]
        hT_lo = [sb(f"a_hT_lo{l}", [128, KC, 128], F32R) for l in range(N_LAYER)]
        neg_max = sb("a_neg_max", [128, 1])
        exp_bias = sb("a_exp_bias", [128, 1])
        expo = sb("a_expo", [128, S])
        z_sum = sb("a_z_sum", [128, 1])
        e_adj = sb("a_e_adj", [128, S])
        e_sum = sb("a_e_sum", [128, 1])
        denom = sb("a_denom", [128, 1])
        r_den = sb("a_r_den", [128, 1])
        attn = sb("a_attn", [128, 2, S])
        diag_scr = sb("a_diag_scr", [128, S])
        diag = sb("a_diag", [128, 1])
        aT_hi = sb("a_aT_hi", [128, 2, 128], F32R)
        aT_lo = sb("a_aT_lo", [128, 2, 128], F32R)
        hl, hr, hs = (sb(f"a_h{c}", [128, D]) for c in "lrs")
        hl_hi, hr_hi = (sb(f"a_h{c}_hi", [128, D], F32R) for c in "lr")
        hl_lo, hr_lo = (sb(f"a_h{c}_lo", [128, D], F32R) for c in "lr")
        ctx_s = sb("a_ctx_s", [128, D])
        stats = sb("a_stats", [128, 6])
        mv = sb("a_mv", [128, 2])
        var_eps = sb("a_var_eps", [128, 1])
        neg_mean = sb("a_neg_mean", [128, 1])
        rstd = sb("a_rstd", [128, 1])
        normed = sb("a_normed", [128, D])
        h_nat = sb("a_h_nat", [128, D])
        o_nat = sb("a_o_nat", [128, D])
        y_res = sb("a_y_res", [128, D])
        stats2 = sb("a_stats2", [128, 6])
        mv2 = sb("a_mv2", [128, 2])
        var_eps2 = sb("a_var_eps2", [128, 1])
        neg_mean2 = sb("a_neg_mean2", [128, 1])
        rstd2 = sb("a_rstd2", [128, 1])
        filler = sb("a_filler", [128, 1])

        def bank(name):
            return ctx.enter_context(nc.psum_tensor(name, [128, 512], F32))

        p_u = bank("a_p_u")
        p_aT = bank("a_p_aT")
        p_T = bank("a_p_T")
        p_hl, p_hs, p_hr = bank("a_p_hl"), bank("a_p_hs"), bank("a_p_hr")
        p_ctx = [bank("a_p_ctx0"), bank("a_p_ctx1")]

        s_const = sem("s_const")
        s_wload = [sem(f"s_wload{m}") for m in range(3)]
        s_rows = [sem(f"s_rows{l}") for l in range(N_LAYER)]
        s_whi = sem("s_whi")
        s_wlo = [[sem(f"s_wlo{l}{m}") for m in range(3)] for l in range(N_LAYER)]
        s_in = [sem(f"s_in{s}") for s in range(RING)]
        s_t = sem("s_t")
        s_t_full = sem("s_t_full")
        s_xT = [sem(f"s_xT{p}") for p in range(2)]
        s_t_hi = sem("s_t_hi")
        s_t_lo = sem("s_t_lo")
        s_u = sem("s_u")
        s_max = sem("s_max")
        s_bias_exp = sem("s_bias_exp")
        s_exp = sem("s_exp")
        s_ea = sem("s_ea")
        s_den = sem("s_den")
        s_rden = sem("s_rden")
        s_attn = sem("s_attn")
        s_diag = sem("s_diag")
        s_p_hl, s_p_hr, s_p_hs = sem("s_p_hl"), sem("s_p_hr"), sem("s_p_hs")
        s_hl, s_hr, s_hs = sem("s_hl"), sem("s_hr"), sem("s_hs")
        s_hl_hi = sem("s_hl_hi")
        s_hr_hi = sem("s_hr_hi")
        s_hl_lo = sem("s_hl_lo")
        s_hr_lo = sem("s_hr_lo")
        s_aT = sem("s_aT")
        s_aT_hi = sem("s_aT_hi")
        s_aT_lo = sem("s_aT_lo")
        s_ctx = sem("s_ctx")
        s_ctx_s = sem("s_ctx_s")
        s_stats = sem("s_stats")
        s_mv = sem("s_mv")
        s_var = sem("s_var")
        s_mean = sem("s_mean")
        s_centred = sem("s_centred")
        s_rstd = sem("s_rstd")
        s_normed = sem("s_normed")
        s_scaled = sem("s_scaled")
        s_h = sem("s_h")
        s_o = sem("s_o")
        s_y = sem("s_y")
        s_stats2 = sem("s_stats2")
        s_mv2 = sem("s_mv2")
        s_var2 = sem("s_var2")
        s_mean2 = sem("s_mean2")
        s_centred2 = sem("s_centred2")
        s_rstd2 = sem("s_rstd2")
        s_x1 = sem("s_x1")
        s_ahi = sem("s_ahi")
        s_alo = sem("s_alo")

        def half_no(i, off, layer):
            if isinstance(i, int) and RING * i + off in (0, n_batch):
                return 0 if i == 0 else 2 * n_batch - 1
            return i * (2 * RING) + (2 * off - 1 + layer)

        def wait(eng, s, value):
            if not isinstance(value, int) or value > 0:
                eng.wait_ge(s, value)

        def steps(eng, half):
            for t in range(RING):
                half(0, t, 0)
                if t > 0:
                    half(0, t, 1)
            with eng.Fori(0, n_batch // RING - 2) as i:
                for off in range(RING, 2 * RING):
                    half(i, off, 0)
                    half(i, off, 1)
            for t in range(n_batch - RING, n_batch):
                half(t // RING, t % RING, 0)
                half(t // RING, t % RING, 1)
            half(n_batch // RING, n_batch % RING, 1)

        def buffers_free(n):
            return 1 if isinstance(n, int) and n == 1 else n - 1

        def three_passes(eng, out, a, b, start, stop):
            a_hi, a_lo = a
            b_hi, b_lo = b
            eng.matmul(out, a_hi, b_hi, start=start, stop=False)
            eng.matmul(out, a_hi, b_lo, start=False, stop=False)
            return eng.matmul(out, a_lo, b_hi, start=False, stop=stop)

        def flat(ap):
            return ap.rearrange("p a b -> p (a b)")

        LOOP_END = 2 * (n_batch - RING) - 1
        PIECES_AT = {3: (0,), 4: (1,), 5: (2,), 6: (3,)}
        PIECES_AT.update({LOOP_END + n: (4 + n,) for n in range(5)})
        PIECES_AT.update({LOOP_END + 6: (9,), LOOP_END + 7: (10, 11)})

        def pieces_of(i, off, layer):
            if not isinstance(i, int):
                return ()
            return PIECES_AT.get(half_no(i, off, layer), ())

        def piece(j):
            m, k = divmod(j, KC)
            hi, lo = (part[:, k, :] for part in w_split[m])
            raw = w_raw[m % 3][:, k * D:(k + 1) * D]
            if m < 2:
                DH = D // H
                hi, lo = (part.rearrange("p (h d) -> p h d", h=H)[:, :, 0:DH] for part in (hi, lo))
                raw = raw.rearrange("p (h d) -> p h d", h=H)
            return raw, hi, lo

        def weights_lo(eng, l, m):
            eng.wait_ge(s_whi, 3 * l + m + 1)
            eng.tensor_tensor(flat(w_lo[l][m][:, :, :]), w_raw[m][:, :],
                              flat(w_hi[l][m][:, :, :].bitcast(F32)), ALU.subtract).then_inc(s_wlo[l][m], 1)

        def xT_loads(i, off):
            return off % 2, i * (RING // 2 * 16) + 16 * (off // 2 + 1)

        def transposed_lo(eng, n, layer_to, full):
            eng.wait_ge(s_t_hi, n + 1)
            wait(eng, s_p_hs, buffers_free(n))
            eng.tensor_tensor(flat(hT_lo[layer_to][:, :, :]), flat(full[:, :, :]),
                              flat(hT_hi[layer_to][:, :, :].bitcast(F32)), ALU.subtract).then_inc(s_t_lo, 1)

        with nc.Block() as block:

            @block.sync
            def _(sp):
                sp.dma_start(xT_in[0][:, :, :], x_T[0]).then_inc(s_xT[0], 16)
                sp.dma_start(adj_in[0][:, :], adj[0]).then_inc(s_in[0], 16)
                sp.dma_start(w_raw[L][:, :], w_gcn[0, L]).then_inc(s_wload[L], 16)
                sp.dma_start(w_raw[R][:, :], w_gcn[0, R]).then_inc(s_wload[R], 16)
                sp.dma_start(w_raw[SELF][:, :], w_gcn[0, SELF]).then_inc(s_wload[SELF], 16)
                sp.dma_start(rows[0][:, :, :], rows_gcn[0]).then_inc(s_rows[0], 16)
                sp.dma_start(xT_in[1][:, :, :], x_T[1]).then_inc(s_xT[1], 16)
                for t in range(RING):
                    sp.dma_start(x_in[t][:, :], x[t]).then_inc(s_in[t], 16)
                    if t > 0:
                        sp.dma_start(adj_in[t][:, :], adj[t]).then_inc(s_in[t], 16)
                for m in (L, R, SELF):
                    sp.wait_ge(s_wlo[0][m], 1)
                    sp.dma_start(w_raw[m][:, :], w_gcn[1, m]).then_inc(s_wload[m], 16)
                sp.dma_start(rows[1][:, :, :], rows_gcn[1]).then_inc(s_rows[1], 16)
                for t in range(2):
                    sp.wait_ge(s_u, t + 1)
                    sp.wait_ge(s_t_lo, t + 1)
                    sp.dma_start(xT_in[t][:, :, :], x_T[2 + t]).then_inc(s_xT[t], 16)
                for m in range(3):
                    sp.wait_ge(s_wlo[1][m], 1)
                    sp.dma_start(w_raw[m][:, :], w_attn[m]).then_inc(s_wload[m], 16)

                def store(t, slot):
                    sp.wait_ge(s_x1, t + 1)
                    sp.dma_start(x1[t], x1_out[slot % 2][:, :]).then_inc(s_free[slot % 2], 16)

                with sp.Fori(0, n_batch // RING - 1) as i:
                    for slot in range(RING):
                        done = i * RING + slot
                        sp.wait_ge(s_y, done + 1)
                        sp.dma_start(x_in[slot][:, :], x[done + RING]).then_inc(s_in[slot], 16)
                        sp.dma_start(adj_in[slot][:, :], adj[done + RING]).then_inc(s_in[slot], 16)
                        sp.wait_ge(s_u, i * (2 * RING) + 2 * slot + 4)
                        sp.wait_ge(s_t_lo, i * (2 * RING) + 2 * slot + 4)
                        sp.dma_start(xT_in[slot % 2][:, :, :], x_T[done + RING]).then_inc(s_xT[slot % 2], 16)
                        store(done, slot)
                sp.wait_ge(s_alo, KC)
                sp.dma_start(w_raw[0][:, :], w_attn[3]).then_inc(s_wload[0], 16)
                for t in range(n_batch - RING, n_batch):
                    store(t, t % RING)
                    sp.wait_ge(s_y, t + 1)
                    sp.dma_start(x_in[t % RING][:, :], x1[t % RING]).then_inc(s_x1_in[t % RING], 16)

            @block.gpsimd
            def _(pool):
                pool.memset(masks[:, :, :], 1.0).then_inc(s_const, 1)
                pool.wait_ge(s_const, 1)
                pool.affine_select(out=masks[:, 0, :], in_=masks[:, 0, :], compare_op=ALU.is_gt, fill=0.0,
                                   base=0, pattern=[[1, 128]], channel_multiplier=-1).then_inc(s_const, 1)
                pool.affine_select(out=masks[:, 1, :], in_=masks[:, 1, :], compare_op=ALU.is_gt, fill=0.0,
                                   base=0, pattern=[[-1, 128]], channel_multiplier=1).then_inc(s_const, 1)
                for s in range(2):
                    pool.memset(x1_out[s][:, :], 0.0).then_inc(s_free[s], 16)
                for parts in w_split[0:2]:
                    for part in parts:
                        pool.memset(part[:, :, :].bitcast(F32), 0.0).then_inc(s_const, 1)

                def norm_scale(q):
                    wait(pool, s_normed, q - 1)
                    pool.wait_ge(s_var, q)
                    pool.tensor_tensor(rstd[:, :], var_eps[:, :], exponent[:, :], ALU.pow).then_inc(s_rstd, 1)

                def norm_gain(q, src, i, off):
                    if src == 0:
                        if not (isinstance(q, int) and q == 1):
                            wait(pool, s_t, i * RING + off)
                    else:
                        wait(pool, s_y, i * RING + (off - 2))
                    pool.wait_ge(s_normed, q)
                    dst = h_nat if src == 0 else o_nat
                    pool.tensor_tensor(dst[:, :], normed[:, :], rows[src][:, GAIN, :], ALU.mult).then_inc(s_scaled, 1)

                def norm_shift(q, src):
                    pool.wait_ge(s_scaled, q)
                    dst, done = (h_nat, s_h) if src == 0 else (o_nat, s_o)
                    pool.tensor_tensor(dst[:, :], dst[:, :], rows[src][:, SHIFT, :], ALU.add).then_inc(done, 1)

                def residual_scale(n):
                    wait(pool, s_x1, n - 1)
                    pool.wait_ge(s_var2, n)
                    pool.tensor_tensor(rstd2[:, :], var_eps2[:, :], exponent[:, :], ALU.pow).then_inc(s_rstd2, 1)

                def low_piece(j):
                    pool.wait_ge(s_ahi, j + 1)
                    raw, hi, lo = piece(j)
                    pool.tensor_tensor(lo, raw, hi.bitcast(F32), ALU.subtract).then_inc(s_alo, 1)

                def half(i, off, layer):
                    q = half_no(i, off, layer)
                    static = isinstance(i, int)
                    t = RING * i + off if static else None
                    first = static and t == 0
                    last = static and t == n_batch
                    src = 0 if static and q == 1 else 1 if last else 1 - layer
                    if last or (layer == 0 and not (static and t < 3)):
                        residual_scale(i * RING + (off - 2))
                    if not first:
                        norm_scale(q)
                    pool.wait_ge(s_hl_hi, q + 1)
                    wait(pool, s_ctx, q)
                    pool.tensor_tensor(hl_lo[:, :], hl[:, :], hl_hi[:, :].bitcast(F32), ALU.subtract).then_inc(s_hl_lo, 1)
                    late = static and q == 1
                    if layer == 0 and not late:
                        if first:
                            transposed_lo(pool, 1, 0, xT_in[1])
                        else:
                            transposed_lo(pool, q + 1, 1, hT)
                    if not first:
                        norm_gain(q, src, i, off)
                    if first:
                        weights_lo(pool, 1, SELF)
                        pool.wait_ge(s_rows[1], 16)
                    else:
                        norm_shift(q, src)
                    if late:
                        transposed_lo(pool, 2, 1, hT)
                    for j in pieces_of(i, off, layer):
                        low_piece(j)

                pool.wait_ge(s_rows[0], 16)
                steps(pool, half)
                n = 2 * n_batch
                norm_scale(n)
                norm_gain(n, 1, n_batch // RING, n_batch % RING + 1)
                residual_scale(n_batch - 1)
                norm_shift(n, 1)
                residual_scale(n_batch)

            @block.scalar
            def _(act):
                def input_hi(n, i, off):
                    p, landed = xT_loads(i, off)
                    act.wait_ge(s_xT[p], landed)
                    wait(act, s_p_hs, buffers_free(n))
                    act.activation(flat(hT_hi[0][:, :, :]), flat(xT_in[p][:, :, :]), ACT.Copy).then_inc(s_t_hi, 1)

                def transposed(n, count):
                    act.wait_ge(s_t, count)
                    wait(act, s_p_hs, buffers_free(n))
                    act.activation(flat(hT[:, :, :]), p_T[:, 0:D], ACT.Relu).then_inc(s_t_full, 1)
                    act.wait_ge(s_t_full, count)
                    act.activation(flat(hT_hi[1][:, :, :]), flat(hT[:, :, :]), ACT.Copy).then_inc(s_t_hi, 1)

                def weights_hi(l, which):
                    for m in which:
                        act.wait_ge(s_wload[m], 16 * (l + 1))
                        act.activation(flat(w_hi[l][m][:, :, :]), w_raw[m][:, :], ACT.Copy).then_inc(s_whi, 1)

                def half(i, off, layer):
                    q = half_no(i, off, layer)
                    static = isinstance(i, int)
                    t = RING * i + off if static else None
                    first = static and t == 0
                    last = static and t == n_batch
                    no_next = static and layer == 1 and t == n_batch - 1
                    if last:
                        transposed(q, n_batch)
                    late = static and q == 1
                    act.wait_ge(s_bias_exp, q + 1)
                    wait(act, s_attn, q)
                    act.activation(expo[:, :], p_u[:, 0:S], ACT.Exp, bias=exp_bias[:, 0:1],
                                   scale=TEMPER_INV, accum_out=z_sum[:, 0:1]).then_inc(s_exp, 1)
                    if not (first or last or no_next or late):
                        if layer == 0:
                            transposed(q + 1, i * RING + off)
                        else:
                            input_hi(q + 1, i, off + 1)
                    if not (last or (static and t < 3)):
                        if layer == 0:
                            outer_centre(i, off - 3)
                        else:
                            outer_scale(i * RING + (off - 2), (off - 3) % 2)
                    act.wait_ge(s_hl, q + 1)
                    wait(act, s_ctx, q)
                    act.activation(hl_hi[:, :], hl[:, :], ACT.Copy).then_inc(s_hl_hi, 1)
                    act.wait_ge(s_aT, q + 1)
                    act.activation(flat(aT_hi[:, :, :]), p_aT[:, 0:2 * S], ACT.Copy).then_inc(s_aT_hi, 1)
                    act.wait_ge(s_hr, q + 1)
                    act.activation(hr_hi[:, :], hr[:, :], ACT.Copy).then_inc(s_hr_hi, 1)
                    if first:
                        input_hi(1, 0, 1)
                        weights_hi(1, (L, R, SELF))
                    else:
                        norm_apply(q)
                    if late:
                        transposed(2, 1)
                    if last:
                        outer_centre(i, off - 3)
                        outer_scale(i * RING + (off - 2), (off - 3) % 2)
                    for j in pieces_of(i, off, layer):
                        act.wait_ge(s_wload[j // KC % 3], 16 * (N_LAYER + 1 + j // (3 * KC)))
                        act.wait_ge(s_const, 7)
                        raw, hi, _ = piece(j)
                        act.activation(hi, raw, ACT.Copy).then_inc(s_ahi, 1)

                def norm_apply(q):
                    act.wait_ge(s_mean, q)
                    wait(act, s_scaled, q - 1)
                    act.activation(normed[:, :], ctx_s[:, :], ACT.Identity, bias=neg_mean[:, 0:1]).then_inc(s_centred, 1)
                    act.wait_ge(s_rstd, q)
                    act.wait_ge(s_centred, q)
                    act.activation(normed[:, :], normed[:, :], ACT.Copy, scale=rstd[:, 0:1]).then_inc(s_normed, 1)

                def outer_centre(i, off):
                    act.wait_ge(s_mean2, i * RING + (off + 1))
                    slot = off % 2
                    act.wait_ge(s_free[slot], i * (16 * RING // 2) + 16 * (off // 2 + 1))
                    act.activation(x1_out[slot][:, :], y_res[:, :], ACT.Identity, bias=neg_mean2[:, 0:1]).then_inc(s_centred2, 1)

                def outer_scale(n, slot):
                    act.wait_ge(s_centred2, n)
                    act.wait_ge(s_rstd2, n)
                    act.activation(x1_out[slot][:, :], x1_out[slot][:, :], ACT.Copy, scale=rstd2[:, 0:1]).then_inc(s_x1, 1)

                input_hi(0, 0, 0)
                weights_hi(0, (L, R, SELF))
                steps(act, half)
                norm_apply(2 * n_batch)
                outer_centre(n_batch // RING, n_batch % RING - 2)
                outer_scale(n_batch - 1, (n_batch - 2) % 2)
                outer_centre(n_batch // RING, n_batch % RING - 1)
                outer_scale(n_batch, (n_batch - 1) % 2)

            @block.vector
            def _(dve):
                def scores_max(q):
                    dve.wait_ge(s_u, q + 1)
                    wait(dve, s_exp, q)
                    dve.tensor_reduce(neg_max[:, :], p_u[:, 0:S], AX.X, ALU.max, negate=True).then_inc(s_max, 1)
                    dve.wait_ge(s_max, q + 1)
                    dve.tensor_scalar(exp_bias[:, :], neg_max[:, :], TEMPER_INV, None, ALU.mult).then_inc(s_bias_exp, 1)

                def context_sum(q, par):
                    dve.wait_ge(s_hs, q)
                    wait(dve, s_centred, q - 1)
                    dve.wait_ge(s_ctx, q)
                    dve.scalar_tensor_tensor(out=ctx_s[:, :], in0=hs[:, :], scalar=diag[:, 0:1], in1=p_ctx[par][:, 0:D],
                                             op0=ALU.mult, op1=ALU.add).then_inc(s_ctx_s, 1)

                def norm_stats(q):
                    dve.wait_ge(s_ctx_s, q)
                    dve.bn_stats(stats[:, :], ctx_s[:, :]).then_inc(s_stats, 1)

                def norm_mean(q):
                    dve.bn_aggr(mv[:, :], stats[:, :]).then_inc(s_mv, 1)

                def norm_var(q):
                    dve.wait_ge(s_mv, q)
                    wait(dve, s_rstd, q - 1)
                    dve.tensor_scalar(var_eps[:, :], mv[:, 1:2], LN_EPS_GCN, None, ALU.add).then_inc(s_var, 1)

                def norm_neg_mean(q):
                    wait(dve, s_centred, q - 1)
                    dve.tensor_scalar(neg_mean[:, :], mv[:, 0:1], -1.0, None, ALU.mult).then_inc(s_mean, 1)

                def residual(n, slot):
                    wait(dve, s_centred2, n - 1)
                    dve.wait_ge(s_o, n)
                    dve.scalar_tensor_tensor(out=y_res[:, :], in0=o_nat[:, :], scalar=0.0, in1=x_in[slot][:, :],
                                             op0=ALU.max, op1=ALU.add).then_inc(s_y, 1)

                def residual_stats(n):
                    dve.wait_ge(s_y, n)
                    dve.bn_stats(stats2[:, :], y_res[:, :]).then_inc(s_stats2, 1)

                def residual_mean(n):
                    dve.bn_aggr(mv2[:, :], stats2[:, :]).then_inc(s_mv2, 1)

                def residual_var(n):
                    dve.wait_ge(s_mv2, n)
                    wait(dve, s_rstd2, n - 1)
                    dve.tensor_scalar(var_eps2[:, :], mv2[:, 1:2], LN_EPS_OUT, None, ALU.add).then_inc(s_var2, 1)
                    wait(dve, s_centred2, n - 1)
                    dve.tensor_scalar(neg_mean2[:, :], mv2[:, 0:1], -1.0, None, ALU.mult).then_inc(s_mean2, 1)

                def with_bias(q, layer, m, product, product_done, out, read, out_done):
                    dve.wait_ge(product_done, q + 1)
                    wait(dve, read, q)
                    dve.tensor_tensor(out[:, :], product[:, 0:D], rows[layer][:, m, :], ALU.add).then_inc(out_done, 1)

                def half(i, off, layer):
                    q = half_no(i, off, layer)
                    static = isinstance(i, int)
                    t = RING * i + off if static else None
                    first = static and t == 0
                    last = static and t == n_batch
                    no_next = static and layer == 1 and t == n_batch - 1
                    slot = (off - layer) % RING
                    if static and q == 2:
                        dve.wait_ge(s_rows[1], 16)
                    outer = last or (layer == 0 and not (static and t < 3))
                    if last:
                        transposed_lo(dve, q, 1, hT)
                    if first:
                        dve.wait_ge(s_const, 3)
                    scores_max(q)
                    if first:
                        weights_lo(dve, 0, SELF)
                        dve.wait_ge(s_rows[0], 16)
                    if outer:
                        residual_stats(i * RING + (off - 2))
                        dve.wait_ge(s_stats2, i * RING + (off - 2))
                    if layer == 0:
                        dve.wait_ge(s_in[off % RING], i * 32 + 32 * (off // RING + 1))
                    dve.wait_ge(s_exp, q + 1)
                    dve.scalar_tensor_tensor(out=e_adj[:, :], in0=expo[:, :], scalar=1.0, in1=adj_in[slot][:, :],
                                             op0=ALU.mult, op1=ALU.mult, accum_out=e_sum[:, 0:1]).then_inc(s_ea, 1)
                    if outer:
                        residual_mean(i * RING + (off - 2))
                    if not first:
                        context_sum(q, 0 if last else layer)
                    dve.wait_ge(s_ea, q + 1)
                    dve.scalar_tensor_tensor(out=denom[:, :], in0=z_sum[:, :], scalar=ATTN_EPS, in1=e_sum[:, :],
                                             op0=ALU.mult, op1=ALU.add).then_inc(s_den, 1)
                    if outer:
                        residual_var(i * RING + (off - 2))
                    if not first:
                        norm_stats(q)
                    dve.wait_ge(s_den, q + 1)
                    dve.reciprocal(r_den[:, :], denom[:, :]).then_inc(s_rden, 1)
                    if not first:
                        dve.wait_ge(s_stats, q)
                    dve.wait_ge(s_rden, q + 1)
                    wait(dve, s_aT, q)
                    dve.scalar_tensor_tensor(out=attn[:, :, :], in0=e_adj[:, :].unsqueeze(1).broadcast_to([128, 2, S]),
                                             scalar=r_den[:, 0:1], in1=masks[:, :, :],
                                             op0=ALU.mult, op1=ALU.mult).then_inc(s_attn, 1)
                    if not first:
                        norm_mean(q)
                    with_bias(q, layer, L, p_hl, s_p_hl, hl, s_hl_lo, s_hl)
                    if not first:
                        norm_var(q)
                    with_bias(q, layer, R, p_hr, s_p_hr, hr, s_hr_lo, s_hr)
                    wait(dve, s_diag, q)
                    dve.scalar_tensor_tensor(out=diag_scr[:, :], in0=e_adj[:, :], scalar=r_den[:, 0:1], in1=ident[:, :],
                                             op0=ALU.mult, op1=ALU.mult, accum_out=diag[:, 0:1]).then_inc(s_diag, 1)
                    if not first:
                        norm_neg_mean(q)
                    dve.wait_ge(s_aT_hi, q + 1)
                    dve.tensor_tensor(flat(aT_lo[:, :, :]), p_aT[:, 0:2 * S], flat(aT_hi[:, :, :].bitcast(F32)),
                                      ALU.subtract).then_inc(s_aT_lo, 1)
                    dve.wait_ge(s_hr_hi, q + 1)
                    wait(dve, s_ctx, q)
                    dve.tensor_tensor(hr_lo[:, :], hr[:, :], hr_hi[:, :].bitcast(F32), ALU.subtract).then_inc(s_hr_lo, 1)
                    if layer == 1 and not (last or no_next):
                        transposed_lo(dve, q + 1, 0, xT_in[(off + 1) % 2])
                    if layer == 1 and not last and not (static and t < 2):
                        residual(i * RING + (off - 1), (off - 2) % RING)
                    with_bias(q, layer, SELF, p_hs, s_p_hs, hs, s_ctx_s, s_hs)
                    if first:
                        weights_lo(dve, 1, L)
                        weights_lo(dve, 1, R)

                transposed_lo(dve, 0, 0, xT_in[0])
                weights_lo(dve, 0, L)
                weights_lo(dve, 0, R)
                steps(dve, half)

                def outer_statistics(n):
                    residual_stats(n)
                    dve.wait_ge(s_stats2, n)
                    dve.memset(filler[:, :], 0.0)
                    residual_mean(n)
                    residual_var(n)

                context_sum(2 * n_batch, 1)
                norm_stats(2 * n_batch)
                dve.wait_ge(s_stats, 2 * n_batch)
                dve.memset(filler[:, :], 1.0)
                norm_mean(2 * n_batch)
                norm_var(2 * n_batch)
                norm_neg_mean(2 * n_batch)
                residual(n_batch - 1, (n_batch - 2) % RING)
                outer_statistics(n_batch - 1)
                residual(n_batch, (n_batch - 1) % RING)
                outer_statistics(n_batch)

            @block.tensor
            def _(pe):

                def transposes(count):
                    wait(pe, s_t_full, count - 1)
                    for k in range(KC):
                        mm = pe.transpose(p_T[:, k * 128:(k + 1) * 128], h_nat[:, k * 128:(k + 1) * 128], ident[:, :])
                    mm.then_inc(s_t, 1)

                def scores(q, full):
                    wait(pe, s_exp, q)
                    for k in range(KC):
                        mm = pe.matmul(p_u[:, 0:S], full[:, k, :], full[:, k, :], start=(k == 0), stop=(k == KC - 1))
                    mm.then_inc(s_u, 1)

                def input_scores(q, i, off):
                    p, landed = xT_loads(i, off)
                    pe.wait_ge(s_xT[p], landed)
                    scores(q, xT_in[p])

                def hidden_scores(q, count):
                    pe.wait_ge(s_t_full, count)
                    scores(q, hT)

                input_scores(0, 0, 0)

                def half(i, off, layer):
                    q = half_no(i, off, layer)
                    static = isinstance(i, int)
                    t = RING * i + off if static else None
                    first = static and t == 0
                    last = static and t == n_batch
                    no_next = static and layer == 1 and t == n_batch - 1
                    par = 0 if first else 1 if last else 1 - layer

                    def project(out, m):
                        if static and q in (0, 2):
                            pe.wait_ge(s_wlo[layer][m], 1)
                        for k in range(KC):
                            mm = three_passes(pe, out[:, 0:D], (hT_hi[layer][:, k, :], hT_lo[layer][:, k, :]),
                                              (w_hi[layer][m][:, k, :], w_lo[layer][m][:, k, :]), k == 0, k == KC - 1)
                        return mm

                    if last:
                        pe.wait_ge(s_h, n_batch)
                        transposes(n_batch)
                        hidden_scores(q, n_batch)
                    def next_transposes():
                        pe.wait_ge(s_h, i * RING + off)
                        transposes(i * RING + off)

                    pe.wait_ge(s_t_lo, q + 1)
                    wait(pe, s_hl, q)
                    project(p_hl, L).then_inc(s_p_hl, 1)
                    late = static and q == 1
                    if layer == 0 and not (first or late):
                        next_transposes()
                    wait(pe, s_hr, q)
                    project(p_hr, R).then_inc(s_p_hr, 1)
                    pe.wait_ge(s_attn, q + 1)
                    wait(pe, s_aT_lo, q)
                    for a in range(2):
                        mm = pe.transpose(p_aT[:, a * 128:(a + 1) * 128], attn[:, a, :], ident[:, :])
                    mm.then_inc(s_aT, 1)
                    wait(pe, s_hs, q)
                    project(p_hs, SELF).then_inc(s_p_hs, 1)

                    def context_product():
                        pe.wait_ge(s_hl_lo, q + 1)
                        pe.wait_ge(s_hr_lo, q + 1)
                        pe.wait_ge(s_aT_lo, q + 1)
                        wait(pe, s_ctx_s, q - 1)
                        three_passes(pe, p_ctx[par][:, 0:D], (aT_hi[:, 0, :], aT_lo[:, 0, :]), (hl_hi[:, :], hl_lo[:, :]),
                                     True, False)
                        three_passes(pe, p_ctx[par][:, 0:D], (aT_hi[:, 1, :], aT_lo[:, 1, :]), (hr_hi[:, :], hr_lo[:, :]),
                                     False, True).then_inc(s_ctx, 1)

                    if late:
                        context_product()
                        next_transposes()
                    if first:
                        input_scores(1, 0, 1)
                    elif layer == 0:
                        hidden_scores(q + 1, i * RING + off)
                    elif not (last or no_next):
                        input_scores(q + 1, i, off + 1)
                    if not late:
                        context_product()

                steps(pe, half)


def phase_attention(nc, ident, exponent, x_ring, x2_out, s_x1_in, x1_stores, s_x2_in, s_store, x1, adj, w_split,
                    bqk, rows_at, x2, w1, w1_split, n_batch, S, D, H):
    KC = D // 128
    DH = D // H
    HP = 64
    NCH = H * HP // 128
    GB = 4
    NT = GB * S
    RMS_EPS = 1e-6
    SCALE = float(DH) ** -0.5
    XR = 4
    PERIOD = 2 * GB

    with ExitStack() as ctx:
        def sb(name, shape, dt=F32):
            return ctx.enter_context(nc.sbuf_tensor(name, shape, dt))

        def sem(name):
            return ctx.enter_context(nc.semaphore(name))

        (wq_hi, wq_lo), (wk_hi, wk_lo), (wv_hi, wv_lo), (wo_hi, wo_lo) = w_split
        w1_hi, w1_lo = w1_split
        b_qk = sb("b_b_qk", [128, 2, NCH])
        rows = sb("b_rows", [128, 4, D])
        w1_raw = [sb(f"b_w1_raw{s}", [128, NT]) for s in range(2)]
        x_in = x_ring
        x_res = [sb(f"b_x_res{s}", [128, D]) for s in range(2)]
        x_bo = [sb(f"b_x_bo{s}", [128, D]) for s in range(2)]
        adj_in = [sb(f"b_adj_in{p}", [128, GB, S]) for p in range(2)]
        xT_hi = [sb(f"b_xT_hi{p}", [128, KC, NT], F32R) for p in range(2)]
        xT_lo = [sb(f"b_xT_lo{p}", [128, KC, NT], F32R) for p in range(2)]
        q_sb, k_sb = ([sb(f"b_{a}{p}", [128, NT]) for p in range(2)] for a in "qk")
        v_sb = [sb(f"b_v{p}", [128, GB, D]) for p in range(2)]
        prob = [sb(f"b_prob{p}", [128, 2, GB, S]) for p in range(2)]
        neg_max = [sb(f"b_neg_max{p}", [128, 2 * GB]) for p in range(2)]
        row_sum = [sb(f"b_row_sum{p}", [128, 2, GB]) for p in range(2)]
        r_sum = [sb(f"b_r_sum{p}", [128, 2, GB]) for p in range(2)]
        pT_sb = sb("b_pT_sb", [128, 2 * GB, S])
        context = [sb(f"b_context{p}", [128, GB, D]) for p in range(2)]
        cT_hi = sb("b_cT_hi", [128, KC * 128], F32R)
        cT_lo = sb("b_cT_lo", [128, KC * 128], F32R)
        y = [sb(f"b_y{s}", [128, D]) for s in range(2)]
        square = sb("b_square", [128, D])
        sum_sq = [sb(f"b_sum_sq{s}", [128, 1]) for s in range(2)]
        mean_sq = sb("b_mean_sq", [128, 1])
        r_rms = sb("b_r_rms", [128, 1])
        z = sb("b_z", [128, D])

        p_q = ctx.enter_context(nc.psum_tensor("b_p_q", [128, NT], F32))
        p_k = ctx.enter_context(nc.psum_tensor("b_p_k", [128, NT], F32))
        p_s = ctx.enter_context(nc.psum_tensor("b_p_s", [128, 2, GB, S], F32))
        p_pT = ctx.enter_context(nc.psum_tensor("b_p_pT", [128, 2 * GB, S], F32))
        p_c = ctx.enter_context(nc.psum_tensor("b_p_c", [128, 512], F32))
        p_m = ctx.enter_context(nc.psum_tensor("b_p_m", [128, 512], F32))

        s_const = sem("b_s_const")
        s_small = sem("b_s_small")
        s_wload = [sem(f"b_s_wload{s}") for s in range(2)]
        s_whi, s_wlo = sem("b_s_whi"), sem("b_s_wlo")
        s_x = s_x1_in
        s_xr = [sem(f"b_s_xr{s}") for s in range(2)]
        s_adj = [sem(f"b_s_adj{p}") for p in range(2)]
        s_t, s_t_hi, s_t_lo = sem("b_s_t"), sem("b_s_t_hi"), sem("b_s_t_lo")
        s_q, s_q_sb = sem("b_s_q"), sem("b_s_q_sb")
        s_k, s_k_sb = sem("b_s_k"), sem("b_s_k_sb")
        s_v, s_v_sb = sem("b_s_v"), sem("b_s_v_sb")
        s_sc = sem("b_s_sc")
        s_logit = sem("b_s_logit")
        s_max = sem("b_s_max")
        s_exp = sem("b_s_exp")
        s_rsum = sem("b_s_rsum")
        s_pT, s_pT_sb = sem("b_s_pT"), sem("b_s_pT_sb")
        s_c = sem("b_s_c")
        s_cn = sem("b_s_cn")
        s_cT, s_cT_hi, s_cT_lo = sem("b_s_cT"), sem("b_s_cT_hi"), sem("b_s_cT_lo")
        s_o = sem("b_s_o")
        s_xbo = sem("b_s_xbo")
        s_y, s_sq, s_ms, s_rms = sem("b_s_y"), sem("b_s_sq"), sem("b_s_ms"), sem("b_s_rms")
        s_z, s_x2 = sem("b_s_z"), sem("b_s_x2")

        class Item:
            def __init__(self, i, off):
                self.i, self.off = i, off
                self.static = isinstance(i, int)
                self.no = i * PERIOD + off
                self.exists = not self.static or 0 <= self.no < n_batch
                self.sub = off % GB
                self.par = (off // GB) % 2
                self.odd = off % 2

            def plus(self, d):
                return Item(self.i, self.off + d)

            def over(self, m):
                return self.i * (PERIOD // m) + self.off // m

        def wait(eng, s, value):
            if not isinstance(value, int) or value > 0:
                eng.wait_ge(s, value)

        def flat(ap):
            return ap.rearrange("p a b -> p (a b)")

        def t_bank(j):
            if j.static and j.no < 5:
                return (p_c, flat(p_pT[:, 0:GB, :]), flat(p_pT[:, GB:2 * GB, :]), flat(p_s[:, 0, :, :]), p_c)[j.no]
            return p_m

        LEAD, TAIL = 5, 7

        last_group = [n_batch - GB + b for b in range(GB)]
        cT_banks = (p_m, p_q, p_k, flat(p_s[:, 0, :, :]))
        o_banks = (flat(p_s[:, 1, :, :]), flat(p_pT[:, 0:GB, :]), flat(p_pT[:, GB:2 * GB, :]), p_c)
        cT_par = n_batch // GB % 2
        last_cT = [(xT_hi[cT_par][:, :, b * S:(b + 1) * S], xT_lo[cT_par][:, :, b * S:(b + 1) * S]) for b in range(GB)]

        def steps(eng, step, tail=1):
            for n in range(-LEAD, PERIOD):
                step(Item(0, n))
            with eng.Fori(1, n_batch // PERIOD - 1) as i:
                for off in range(PERIOD):
                    step(Item(i, off))
            for n in range(n_batch - PERIOD, n_batch + tail):
                step(Item(0, n))

        def three_passes(eng, out, a, b, start, stop):
            a_hi, a_lo = a
            b_hi, b_lo = b
            eng.matmul(out, a_hi, b_hi, start=start, stop=False)
            eng.matmul(out, a_hi, b_lo, start=False, stop=False)
            return eng.matmul(out, a_lo, b_hi, start=False, stop=stop)

        COLS = w1.shape[2] // NT
        N_PIECE = KC * COLS

        def w1_piece(j):
            k, c = divmod(j, COLS)
            c = slice(c * NT, (c + 1) * NT)
            return w1[k][:, c], w1_hi[:, k, c], w1_lo[:, k, c]

        def piece_at(n):
            j = n.no - (n_batch - PERIOD) if n.static else -1
            return j if 0 <= j < N_PIECE else None

        with nc.Block() as block:

            @block.sync
            def _(sp):
                sp.dma_start(rows[:, :, :], rows_at).then_inc(s_small, 16)
                sp.wait_ge(s_const, 1)
                for a in range(2):
                    for h in range(2):
                        sp.dma_start(b_qk[h * HP:h * HP + DH, a, :], bqk[a, h]).then_inc(s_small, 16)
                for b in range(GB):
                    sp.dma_start(adj_in[0][:, b, :], adj[b]).then_inc(s_adj[0], 16)
                for s, value in x1_stores:
                    sp.wait_ge(s, value)

                def step(n):
                    j = n.plus(7)
                    if j.exists and not (j.static and j.no < XR):
                        wait(sp, s_t, j.no - XR + 1)
                        sp.dma_start(x_in[j.off % XR][:, :], x1[j.no]).then_inc(s_x[j.off % XR], 16)
                    j = n.plus(5)
                    if j.exists and not (j.static and j.no < GB):
                        wait(sp, s_logit, j.no * 2 - 2 * (GB + j.sub))
                        sp.dma_start(adj_in[j.par][:, j.sub, :], adj[j.no]).then_inc(s_adj[j.par], 16)
                    j = n.plus(-4)
                    if j.exists:
                        wait(sp, s_xbo, j.no - 1)
                        sp.dma_start(x_res[j.odd][:, :], x1[j.no]).then_inc(s_xr[j.odd], 16)
                    j = n.plus(-7)
                    if j.exists:
                        sp.wait_ge(s_x2, j.no + 1)
                        sp.dma_start(x2[j.no], x2_out[j.odd][:, :]).then_inc(s_store[j.odd], 16)
                    if n.static and 0 <= n.no - n_batch < XR:
                        sp.wait_ge(s_store[n.odd], 16)
                        sp.wait_ge(s_t, n_batch)
                        sp.dma_start(x_in[n.no % XR][:, :], x2[n.no % XR]).then_inc(s_x2_in, 16)
                    pieces = (0, 1) if piece_at(n) == 0 else (piece_at(n.plus(1)),)
                    for j in pieces:
                        if j is not None:
                            wait(sp, s_wlo, j - 1)
                            sp.dma_start(w1_raw[j % 2][:, :], w1_piece(j)[0]).then_inc(s_wload[j % 2], 16)

                for m in range(-7, -LEAD):
                    step(Item(0, m))
                steps(sp, step, TAIL)

            @block.gpsimd
            def _(pool):
                pool.memset(b_qk[:, :, :], 0.0).then_inc(s_const, 1)
                pool.wait_ge(s_small, 16 * 5)

                def step(n):
                    j = n.plus(-5)
                    if j.exists:
                        pool.wait_ge(s_xr[j.odd], j.over(2) * 16 + 16)
                        wait(pool, s_y, j.no - 1)
                        pool.tensor_tensor(x_bo[j.odd][:, :], x_res[j.odd][:, :], rows[:, 0, :],
                                           ALU.add).then_inc(s_xbo, 1)
                    j = n.plus(-6)
                    if j.exists:
                        pool.wait_ge(s_ms, j.no + 1)
                        pool.tensor_tensor(r_rms[:, :], mean_sq[:, :], exponent[:, :], ALU.pow).then_inc(s_rms, 1)
                    if j.exists and not (j.static and j.no >= n_batch - GB):
                        pool.wait_ge(s_z, j.no + 1)
                        wait(pool, s_store[j.odd], j.over(2) * 16)
                        pool.tensor_tensor(x2_out[j.odd][:, :], z[:, :], rows[:, 2, :], ALU.add).then_inc(s_x2, 1)

                steps(pool, step, TAIL)

            @block.scalar
            def _(act):
                def exps(n, h):
                    act.wait_ge(s_max, n.no * 2 + (h + 1))
                    if h == 0:
                        wait(act, s_rsum, n.no - 1)
                    for b in range(GB):
                        e = act.activation(prob[n.odd][:, h, b, :], prob[n.odd][:, h, b, :], ACT.Exp,
                                           bias=neg_max[n.odd][:, h * GB + b:h * GB + b + 1],
                                           accum_out=row_sum[n.odd][:, h, b:b + 1])
                    return e

                def squares(j):
                    act.wait_ge(s_y, j.no + 1)
                    wait(act, s_sq, j.no)
                    act.activation(square[:, :], y[j.odd][:, :], ACT.Square,
                                   accum_out=sum_sq[j.odd][:, 0:1]).then_inc(s_sq, 1)

                def step(n):
                    j = n.plus(5)
                    if j.exists:
                        act.wait_ge(s_t, j.no + 1)
                        act.activation(xT_hi[j.par][:, :, j.sub * S:(j.sub + 1) * S],
                                       t_bank(j)[:, 0:D].rearrange("p (k n) -> p k n", k=KC), ACT.Copy).then_inc(s_t_hi, 1)
                    j = n.plus(-1)
                    if j.exists:
                        act.wait_ge(s_pT, j.no + 1)
                        act.activation(flat(pT_sb[:, :, :]), flat(p_pT[:, :, :]), ACT.Copy).then_inc(s_pT_sb, 1)
                    context_first = n.static and n.no >= n_batch - 1
                    if n.exists and not context_first:
                        exps(n, 0)
                    j = n.plus(-5)
                    if j.exists:
                        act.wait_ge(s_cT, j.no + 1)
                        act.activation(cT_hi[:, :], p_m[:, 0:D], ACT.Copy).then_inc(s_cT_hi, 1)
                    if n.exists and context_first:
                        exps(n, 0)
                    j = n.plus(1)
                    if j.exists:
                        if j.static and j.no == 0:
                            act.wait_ge(s_small, 16 * 5)
                        act.wait_ge(s_q, j.no + 1)
                        act.activation(q_sb[j.odd][:, :], p_q[:, :], ACT.Identity,
                                       bias=b_qk[:, 0, j.sub:j.sub + 1]).then_inc(s_q_sb, 1)
                    if n.exists:
                        exps(n, 1).then_inc(s_exp, 1)
                    j = n.plus(1)
                    if j.exists:
                        act.wait_ge(s_k, j.no + 1)
                        act.activation(k_sb[j.odd][:, :], p_k[:, :], ACT.Identity,
                                       bias=b_qk[:, 1, j.sub:j.sub + 1]).then_inc(s_k_sb, 1)
                    j = n.plus(-5)
                    if j.exists:
                        squares(j)
                    j = piece_at(n)
                    if j is not None:
                        act.wait_ge(s_wload[j % 2], 16 * (j // 2 + 1))
                        act.activation(w1_piece(j)[1], w1_raw[j % 2][:, :], ACT.Copy).then_inc(s_whi, 1)

                steps(act, step)
                for b, j in enumerate(last_group):
                    act.wait_ge(s_cT, j + 1)
                    act.activation(last_cT[b][0], cT_banks[b][:, 0:D].rearrange("p (k n) -> p k n", k=KC),
                                   ACT.Copy).then_inc(s_cT_hi, 1)
                for j in last_group:
                    squares(Item(0, j))

            @block.vector
            def _(dve):
                def divide_context(j):
                    dve.wait_ge(s_c, j.no + 1)
                    wait(dve, s_rsum, j.no + 1)
                    for h in range(2):
                        head = 2 * j.sub + h
                        c = dve.tensor_tensor(context[j.par][:, :, head * DH:(head + 1) * DH],
                                              p_c[:, h * GB * DH:(h + 1) * GB * DH].rearrange("p (b d) -> p b d", b=GB),
                                              r_sum[j.odd][:, h, :].unsqueeze(2).broadcast_to([128, GB, DH]), ALU.mult)
                    c.then_inc(s_cn, 1)

                def mean_square(j):
                    dve.wait_ge(s_sq, j.no + 1)
                    dve.tensor_scalar(mean_sq[:, :], sum_sq[j.odd][:, :], 1.0 / D, RMS_EPS,
                                      ALU.mult, ALU.add).then_inc(s_ms, 1)

                def scale_rms(j):
                    dve.wait_ge(s_rms, j.no + 1)
                    wait(dve, s_x2, j.no)
                    dve.scalar_tensor_tensor(out=z[:, :], in0=y[j.odd][:, :], scalar=r_rms[:, 0:1], in1=rows[:, 1, :],
                                             op0=ALU.mult, op1=ALU.mult).then_inc(s_z, 1)

                def residual_sum(j, product):
                    dve.wait_ge(s_xbo, j.no + 1)
                    wait(dve, s_z, j.no - 1)
                    dve.wait_ge(s_o, j.no + 1)
                    dve.tensor_tensor(y[j.odd][:, :], product[:, 0:D], x_bo[j.odd][:, :], ALU.add).then_inc(s_y, 1)

                def shift_rms(j):
                    dve.wait_ge(s_z, j.no + 1)
                    dve.wait_ge(s_store[j.odd], j.over(2) * 16)
                    dve.tensor_tensor(x2_out[j.odd][:, :], z[:, :], rows[:, 2, :], ALU.add).then_inc(s_x2, 1)

                def w1_low(j):
                    dve.wait_ge(s_whi, j + 1)
                    _, hi, lo = w1_piece(j)
                    dve.tensor_tensor(lo, w1_raw[j % 2][:, :], hi.bitcast(F32), ALU.subtract).then_inc(s_wlo, 1)

                def step(n):
                    j = n.plus(2)
                    if j.exists:
                        if j.static and j.no == 0:
                            dve.wait_ge(s_small, 16 * 5)
                        dve.wait_ge(s_v, j.no + 1)
                        dve.tensor_tensor(v_sb[j.par][:, j.sub, :], p_m[:, 0:D], rows[:, 3, :], ALU.add).then_inc(s_v_sb, 1)
                    if n.exists:
                        dve.wait_ge(s_adj[n.par], n.over(PERIOD) * (16 * GB) + 16 * GB)
                        wait(dve, s_pT, n.no - 1)
                        for h in range(2):
                            dve.wait_ge(s_sc, n.no * 2 + (h + 1))
                            dve.scalar_tensor_tensor(out=flat(prob[n.odd][:, h, :, :]), in0=flat(p_s[:, h, :, :]), scalar=SCALE,
                                                     in1=flat(adj_in[n.par][:, :, :]), op0=ALU.mult, op1=ALU.add)\
                               .then_inc(s_logit, 1)
                            dve.wait_ge(s_logit, n.no * 2 + (h + 1))
                            dve.tensor_reduce(neg_max[n.odd][:, h * GB:(h + 1) * GB], prob[n.odd][:, h, :, :], AX.X, ALU.max,
                                              negate=True).then_inc(s_max, 1)
                    j = n.plus(5)
                    if j.exists:
                        dve.wait_ge(s_t_hi, j.no + 1)
                        c = slice(j.sub * S, (j.sub + 1) * S)
                        dve.tensor_tensor(xT_lo[j.par][:, :, c], t_bank(j)[:, 0:D].rearrange("p (k n) -> p k n", k=KC),
                                          xT_hi[j.par][:, :, c].bitcast(F32), ALU.subtract).then_inc(s_t_lo, 1)
                    j = n.plus(-1)
                    if j.exists:
                        dve.wait_ge(s_exp, j.no + 1)
                        dve.reciprocal(flat(r_sum[j.odd][:, :, :]), flat(row_sum[j.odd][:, :, :])).then_inc(s_rsum, 1)
                    j = n.plus(-2)
                    if j.exists:
                        divide_context(j)
                    j = n.plus(-5)
                    if j.exists:
                        dve.wait_ge(s_cT_hi, j.no + 1)
                        dve.tensor_tensor(cT_lo[:, :], p_m[:, 0:D], cT_hi[:, :].bitcast(F32), ALU.subtract).then_inc(s_cT_lo, 1)
                    j = n.plus(-6)
                    if j.exists:
                        mean_square(j)
                        scale_rms(j)
                    j = n.plus(-5)
                    if j.exists:
                        residual_sum(j, p_m)
                    j = piece_at(n.plus(-1))
                    if j is not None:
                        w1_low(j)

                steps(dve, step)
                divide_context(Item(0, n_batch - 1))
                before = Item(0, n_batch - GB - 1)
                mean_square(before)
                for b, j in enumerate(last_group):
                    dve.wait_ge(s_cT_hi, j + 1)
                    hi, lo = last_cT[b]
                    dve.tensor_tensor(lo, cT_banks[b][:, 0:D].rearrange("p (k n) -> p k n", k=KC), hi.bitcast(F32),
                                      ALU.subtract).then_inc(s_cT_lo, 1)
                scale_rms(before)
                w1_low(N_PIECE - 1)
                for b, j in enumerate(last_group):
                    residual_sum(Item(0, j), o_banks[b])
                    if b > 0:
                        scale_rms(Item(0, j - 1))
                    mean_square(Item(0, j))
                    if b > 0:
                        shift_rms(Item(0, j - 1))
                scale_rms(Item(0, n_batch - 1))
                shift_rms(Item(0, n_batch - 1))

            @block.tensor
            def _(pe):
                def project(j, out, hi, lo):
                    c = slice(j.sub * 128, (j.sub + 1) * 128)
                    for k in range(KC):
                        mm = three_passes(pe, out[:, :], (hi[:, k, c], lo[:, k, c]),
                                          (xT_hi[j.par][:, k, :], xT_lo[j.par][:, k, :]), k == 0, k == KC - 1)
                    return mm

                def step(n):
                    if n.exists:
                        pe.wait_ge(s_q_sb, n.no + 1)
                        pe.wait_ge(s_k_sb, n.no + 1)
                        wait(pe, s_logit, n.no * 2)
                        for h in range(2):
                            r = slice(h * HP, h * HP + DH)
                            for b in range(GB):
                                c = slice(b * S, (b + 1) * S)
                                mm = pe.matmul(p_s[:, h, b, :], q_sb[n.odd][r, c], k_sb[n.odd][r, c], start=True, stop=True)
                            if h == 0:
                                mm.then_inc(s_sc, 1)
                        mm.then_inc(s_sc, 1)
                    j = n.plus(5)
                    if j.exists:
                        if j.static and j.no < 5:
                            wait(pe, s_t_lo, 1 if j.no == 4 else 0)
                        else:
                            pe.wait_ge(s_v_sb, n.plus(2).no + 1)
                        pe.wait_ge(s_x[j.off % XR], j.over(XR) * 16 + 16)
                        for k in range(KC):
                            mm = pe.transpose(t_bank(j)[:, k * 128:(k + 1) * 128], x_in[j.off % XR][:, k * 128:(k + 1) * 128],
                                              ident[:, :])
                        mm.then_inc(s_t, 1)
                    j = n.plus(-1)
                    if j.exists:
                        pe.wait_ge(s_exp, j.no + 1)
                        wait(pe, s_pT_sb, j.no)
                        for h in range(2):
                            for b in range(GB):
                                mm = pe.transpose(p_pT[:, h * GB + b, :], prob[j.odd][:, h, b, :], ident[:, :])
                        mm.then_inc(s_pT, 1)
                    j = n.plus(1)
                    if j.exists:
                        pe.wait_ge(s_t_lo, j.no - j.sub + GB)
                        wait(pe, s_q_sb, j.no)
                        project(j, p_q, wq_hi, wq_lo).then_inc(s_q, 1)
                    j = n.plus(-5)
                    if j.exists:
                        pe.wait_ge(s_cn, j.no - j.sub + GB)
                        if n.plus(5).exists:
                            pe.wait_ge(s_t_lo, n.plus(5).no + 1)
                        elif n.plus(2).exists:
                            pe.wait_ge(s_v_sb, n.plus(2).no + 1)
                        wait(pe, s_y, j.no)
                        for k in range(KC):
                            mm = pe.transpose(p_m[:, k * 128:(k + 1) * 128],
                                              context[j.par][:, j.sub, k * 128:(k + 1) * 128], ident[:, :])
                        mm.then_inc(s_cT, 1)
                    j = n.plus(1)
                    if j.exists:
                        wait(pe, s_k_sb, j.no)
                        project(j, p_k, wk_hi, wk_lo).then_inc(s_k, 1)
                    j = n.plus(-5)
                    if j.exists:
                        pe.wait_ge(s_cT_lo, j.no + 1)
                        for k in range(KC):
                            c = slice(k * 128, (k + 1) * 128)
                            mm = three_passes(pe, p_m[:, 0:D], (cT_hi[:, c], cT_lo[:, c]),
                                              (wo_hi[:, k, :], wo_lo[:, k, :]), k == 0, k == KC - 1)
                        mm.then_inc(s_o, 1)
                    j = n.plus(-1)
                    if j.exists:
                        pe.wait_ge(s_pT_sb, j.no + 1)
                        pe.wait_ge(s_v_sb, j.no - j.sub + GB)
                        wait(pe, s_cn, j.no)
                        for h in range(2):
                            head = 2 * j.sub + h
                            d = slice(head * DH, (head + 1) * DH)
                            for b in range(GB):
                                i = h * GB + b
                                mm = pe.matmul(p_c[:, i * DH:(i + 1) * DH], pT_sb[:, i, :], v_sb[j.par][:, b, d],
                                               start=True, stop=True)
                        mm.then_inc(s_c, 1)
                    j = n.plus(3)
                    if j.exists:
                        pe.wait_ge(s_t_lo, j.no + 1)
                        if n.plus(-5).exists:
                            pe.wait_ge(s_y, n.plus(-5).no + 1)
                        elif n.plus(5).static and n.plus(5).no < 5:
                            wait(pe, s_v_sb, j.no)
                        elif n.plus(5).exists:
                            pe.wait_ge(s_t_lo, n.plus(5).no + 1)
                        for k in range(KC):
                            c = slice(j.sub * S, (j.sub + 1) * S)
                            mm = three_passes(pe, p_m[:, 0:D], (xT_hi[j.par][:, k, c], xT_lo[j.par][:, k, c]),
                                              (wv_hi[:, k, :], wv_lo[:, k, :]), k == 0, k == KC - 1)
                        mm.then_inc(s_v, 1)

                steps(pe, step)
                pe.wait_ge(s_cn, n_batch)
                for b, j in enumerate(last_group):
                    read, value = ((s_y, n_batch - GB), (s_q_sb, n_batch), (s_k_sb, n_batch), (s_logit, 2 * n_batch))[b]
                    pe.wait_ge(read, value)
                    for k in range(KC):
                        mm = pe.transpose(cT_banks[b][:, k * 128:(k + 1) * 128],
                                          context[Item(0, j).par][:, b, k * 128:(k + 1) * 128], ident[:, :])
                    mm.then_inc(s_cT, 1)
                pe.wait_ge(s_pT_sb, n_batch)
                for b, j in enumerate(last_group):
                    pe.wait_ge(s_cT_lo, j + 1)
                    hi, lo = last_cT[b]
                    for k in range(KC):
                        mm = three_passes(pe, o_banks[b][:, 0:D], (hi[:, k, :], lo[:, k, :]),
                                          (wo_hi[:, k, :], wo_lo[:, k, :]), k == 0, k == KC - 1)
                    mm.then_inc(s_o, 1)


def phase_feed_forward(nc, ident, exponent, x_ring, s_x2_in, x2_stores, x1, x2, w1_split, b1, w2, rows_ff, out, n_batch, S, D, F):
    KC = D // 128
    FC = F // 128
    GB = 4
    NG = n_batch // GB
    NT = GB * S
    RMS_EPS = 1e-6
    LN_EPS = 1e-5
    T_STEP = {2: 0, 4: 1, 6: 2, 8: 3}

    with ExitStack() as ctx:
        def sb(name, shape, dt=F32):
            return ctx.enter_context(nc.sbuf_tensor(name, shape, dt))

        def sem(name):
            return ctx.enter_context(nc.semaphore(name))

        w1_hi, w1_lo = w1_split
        w_raw = [sb(f"c_w_raw{k}", [128, D * FC // KC]) for k in range(KC)]
        w2_hi = sb("c_w2_hi", [128, FC, D], F32R)
        w2_lo = sb("c_w2_lo", [128, FC, D], F32R)
        b1_col = sb("c_b1_col", [128, FC])
        rows = sb("c_rows", [128, 3, D])
        x2_in = [sb(f"c_x2_in{p}", [128, GB, D]) for p in range(2)]
        x1_in = [sb(f"c_x1_in{p}", [128, GB, D]) for p in range(2)]
        xT_hi = [sb(f"c_xT_hi{p}", [128, KC, NT], F32R) for p in range(2)]
        xT_lo = [sb(f"c_xT_lo{p}", [128, KC, NT], F32R) for p in range(2)]
        hid = sb("c_hid", [128, NT])
        hid_hi = [sb(f"c_hid_hi{p}", [128, NT], F32R) for p in range(2)]
        hid_lo = [sb(f"c_hid_lo{p}", [128, NT], F32R) for p in range(2)]
        y = [sb(f"c_y{b}", [128, D]) for b in range(GB)]
        square = sb("c_square", [128, D])
        sum_sq = [sb(f"c_sum_sq{b}", [128, 1]) for b in range(GB)]
        mean_sq = [sb(f"c_mean_sq{b}", [128, 1]) for b in range(GB)]
        r_rms = [sb(f"c_r_rms{b}", [128, 1]) for b in range(GB)]
        z = [sb(f"c_z{b}", [128, D]) for b in range(GB)]
        stats = sb("c_stats", [128, 6])
        mv = [sb(f"c_mv{b}", [128, 2]) for b in range(GB)]
        var_eps = [sb(f"c_var_eps{b}", [128, 1]) for b in range(GB)]
        rstd = [sb(f"c_rstd{b}", [128, 1]) for b in range(GB)]
        filler = sb("c_filler", [128, 1])
        o_out = [sb(f"c_o_out{b}", [128, D]) for b in range(GB)]

        def bank(name):
            return ctx.enter_context(nc.psum_tensor(name, [128, 512], F32))

        p_f1 = [bank("c_p_f1_0"), bank("c_p_f1_1")]
        p_f2 = [bank(f"c_p_f2_{b}") for b in range(GB)]
        p_T = bank("c_p_T")

        s_b1 = sem("c_s_b1")
        s_small = sem("c_s_small")
        s_wload = [sem(f"c_s_wload{k}") for k in range(KC)]
        s_whi = sem("c_s_whi")
        s_wlo = sem("c_s_wlo")
        s_wlo_pool = sem("c_s_wlo_pool")
        s_x2 = [sem(f"c_s_x2_{p}") for p in range(2)]
        s_x1 = [sem(f"c_s_x1_{p}") for p in range(2)]
        s_t = sem("c_s_t")
        s_t_hi = sem("c_s_t_hi")
        s_t_lo = sem("c_s_t_lo")
        s_f1 = sem("c_s_f1")
        s_silu = sem("c_s_silu")
        s_hid_hi = sem("c_s_hid_hi")
        s_hid_lo = sem("c_s_hid_lo")
        s_hid_used = sem("c_s_hid_used")
        s_f2 = [sem(f"c_s_f2_{b}") for b in range(GB)]
        s_xb = sem("c_s_xb")
        s_xg = sem("c_s_xg")
        s_y = sem("c_s_y")
        s_sq = sem("c_s_sq")
        s_ms = sem("c_s_ms")
        s_rms = sem("c_s_rms")
        s_z = sem("c_s_z")
        s_sum = sem("c_s_sum")
        s_stats = sem("c_s_stats")
        s_mv = sem("c_s_mv")
        s_var = sem("c_s_var")
        s_rstd = sem("c_s_rstd")
        s_o = sem("c_s_o")
        s_store = [sem(f"c_s_store{b}") for b in range(GB)]

        def wait(eng, s, value):
            if not isinstance(value, int) or value > 0:
                eng.wait_ge(s, value)

        def chunks(i, p, f):
            return i * (2 * FC) + (p * FC + f)

        def batches(i, p, b):
            return i * (2 * GB) + (p * GB + b)

        def groups(i, p):
            return i * 2 + p

        def is_last(i, p):
            return isinstance(i, int) and 2 * i + p == NG - 1

        def is_first(i, p):
            return isinstance(i, int) and 2 * i + p == 0

        def all_groups(eng, group):
            for p in range(2):
                group(0, p)
            with eng.Fori(1, NG // 2 - 1) as i:
                for p in range(2):
                    group(i, p)
            for p in range(2):
                group(NG // 2 - 1, p)

        x1_v = x1.rearrange("(g b) s d -> g s b d", b=GB)
        x2_v = x2.rearrange("(g b) s d -> g s b d", b=GB)
        W_PARTS = [tuple(half[:, k * (FC // KC):(k + 1) * (FC // KC), :].rearrange("p c n -> p (c n)")
                         for half in (w2_hi, w2_lo)) for k in range(KC)]

        def t_bank(b, first):
            return p_f2[b] if first else p_T

        with nc.Block() as block:

            @block.sync
            def _(sp):
                sp.dma_start(b1_col[:, :], b1).then_inc(s_b1, 16)
                for k in range(KC):
                    sp.dma_start(w_raw[k][:, :], w2[k]).then_inc(s_wload[k], 16)
                sp.dma_start(rows[:, :, :], rows_ff).then_inc(s_small, 16)
                for s, value in x2_stores:
                    sp.wait_ge(s, value)
                sp.dma_start(x2_in[0][:, :, :], x2_v[0]).then_inc(s_x2[0], 16)
                sp.dma_start(x1_in[0][:, :, :], x1_v[0]).then_inc(s_x1[0], 16)

                def group(i, p):
                    if not is_last(i, p):
                        wait(sp, s_y, batches(i, p, 0))
                        wait(sp, s_xb, batches(i, p, 0))
                        sp.dma_start(x2_in[1 - p][:, :, :], x2_v[groups(i, p) + 1]).then_inc(s_x2[1 - p], 16)
                        wait(sp, s_sum, batches(i, p, 0))
                        sp.dma_start(x1_in[1 - p][:, :, :], x1_v[groups(i, p) + 1]).then_inc(s_x1[1 - p], 16)
                    if not is_first(i, p):
                        for b in range(GB):
                            n = i * (2 * GB) + (p * GB + b - GB)
                            sp.wait_ge(s_o, n + 1)
                            sp.dma_start(out[n], o_out[b][:, :]).then_inc(s_store[b], 16)

                all_groups(sp, group)
                for b in range(GB):
                    n = n_batch - GB + b
                    sp.wait_ge(s_o, n + 1)
                    sp.dma_start(out[n], o_out[b][:, :]).then_inc(s_store[b], 16)
                for b in range(GB):
                    sp.wait_ge(s_store[b], 16 * NG)

            @block.gpsimd
            def _(pool):
                for k in range(1, KC):
                    hi, lo = W_PARTS[k]
                    pool.wait_ge(s_whi, k + 1)
                    pool.tensor_tensor(lo, w_raw[k][:, :], hi.bitcast(F32), ALU.subtract).then_inc(s_wlo_pool, 1)
                pool.wait_ge(s_small, 16)

                def finals(i, p):
                    for f in range(FC):
                        if 0 <= f - 1 < GB:
                            b = f - 1
                            pool.wait_ge(s_ms, batches(i, p, b) - GB + 1)
                            pool.tensor_tensor(r_rms[b][:, :], mean_sq[b][:, :], exponent[:, :],
                                               ALU.pow).then_inc(s_rms, 1)
                        if 0 <= f - 2 < GB:
                            b = f - 2
                            pool.wait_ge(s_z, batches(i, p, b) - GB + 1)
                            pool.wait_ge(s_xg, batches(i, p, b) - GB + 1)
                            pool.tensor_tensor(z[b][:, :], z[b][:, :], x1_in[1 - p][:, b, :], ALU.add).then_inc(s_sum, 1)
                        if 0 <= f - 4 < GB:
                            b = f - 4
                            pool.wait_ge(s_var, batches(i, p, b) - GB + 1)
                            pool.tensor_tensor(rstd[b][:, :], var_eps[b][:, :], exponent[:, :],
                                               ALU.pow).then_inc(s_rstd, 1)

                def group(i, p):
                    if not is_first(i, p):
                        finals(i, p)
                    for b in range(GB):
                        pool.wait_ge(s_x2[p], i * 16 + 16)
                        pool.wait_ge(s_t, batches(i, p, b) + 1)
                        pool.tensor_tensor(x2_in[p][:, b, :], x2_in[p][:, b, :], rows[:, 0, :], ALU.add).then_inc(s_xb, 1)
                    for b in range(GB):
                        pool.wait_ge(s_x1[p], i * 16 + 16)
                        pool.tensor_tensor(x1_in[p][:, b, :], x1_in[p][:, b, :], rows[:, 2, :], ALU.add).then_inc(s_xg, 1)

                all_groups(pool, group)
                finals(NG // 2, 0)

            @block.scalar
            def _(act):
                def transposed_hi(i, p, b, first=False):
                    act.wait_ge(s_t, batches(i, p, b) + 1)
                    act.activation(xT_hi[p % 2][:, :, b * S:(b + 1) * S],
                                   t_bank(b, first)[:, 0:D].rearrange("p (k n) -> p k n", k=KC),
                                   ACT.Copy).then_inc(s_t_hi, 1)

                for b in range(GB):
                    transposed_hi(0, 0, b, True)

                def weights_hi(k):
                    act.wait_ge(s_wload[k], 16)
                    act.activation(W_PARTS[k][0], w_raw[k][:, :], ACT.Copy).then_inc(s_whi, 1)

                weights_hi(0)

                def silu(n, par, f):
                    act.wait_ge(s_f1, n + 1)
                    wait(act, s_hid_lo, n)
                    act.activation(hid[:, :], p_f1[par][:, :], ACT.Silu, bias=b1_col[:, f:f + 1]).then_inc(s_silu, 1)

                def squares(i, p):
                    for b in range(GB):
                        n = batches(i, p, b)
                        act.wait_ge(s_y, n + 1)
                        wait(act, s_sq, n)
                        act.activation(square[:, :], y[b][:, :], ACT.Square,
                                       accum_out=sum_sq[b][:, 0:1]).then_inc(s_sq, 1)

                def group(i, p):
                    if is_first(i, p):
                        act.wait_ge(s_b1, 16)
                        silu(0, 0, 0)
                        weights_hi(1)
                        weights_hi(2)
                    for f in range(FC):
                        if not (is_last(i, p) and f == FC - 1):
                            silu(chunks(i, p, f) + 1, (f + 1) % 2, (f + 1) % FC)
                        if f in T_STEP and not is_last(i, p):
                            transposed_hi(i, p + 1, T_STEP[f])
                        if f == 0 and not is_first(i, p):
                            squares(i, p - 1)

                all_groups(act, group)
                squares(NG // 2, -1)

            @block.vector
            def _(dve):
                def transposed_lo(i, p, b, first=False):
                    dve.wait_ge(s_t_hi, batches(i, p, b) + 1)
                    dve.tensor_tensor(xT_lo[p % 2][:, :, b * S:(b + 1) * S],
                                      t_bank(b, first)[:, 0:D].rearrange("p (k n) -> p k n", k=KC),
                                      xT_hi[p % 2][:, :, b * S:(b + 1) * S].bitcast(F32), ALU.subtract).then_inc(s_t_lo, 1)

                for b in range(GB):
                    transposed_lo(0, 0, b, True)
                hi, lo = W_PARTS[0]
                dve.wait_ge(s_whi, 1)
                dve.tensor_tensor(lo, w_raw[0][:, :], hi.bitcast(F32), ALU.subtract).then_inc(s_wlo, 1)
                def hidden(n, par):
                    dve.wait_ge(s_silu, n + 1)
                    wait(dve, s_hid_used, n - 1)
                    dve.tensor_copy(hid_hi[par][:, :], hid[:, :]).then_inc(s_hid_hi, 1)
                    dve.wait_ge(s_hid_hi, n + 1)
                    dve.tensor_tensor(hid_lo[par][:, :], hid[:, :], hid_hi[par][:, :].bitcast(F32),
                                      ALU.subtract).then_inc(s_hid_lo, 1)

                def sums(i, p):
                    for b in range(GB):
                        n = batches(i, p, b)
                        dve.wait_ge(s_xb, n + 1)
                        if b < GB - 1:
                            dve.wait_ge(s_f2[b], groups(i, p) + 1)
                        else:
                            dve.wait_ge(s_hid_used, chunks(i, p, FC))
                        dve.tensor_tensor(y[b][:, :], p_f2[b][:, 0:D], x2_in[p][:, b, :], ALU.add).then_inc(s_y, 1)

                def mean_square(n, b):
                    dve.wait_ge(s_sq, n + 1)
                    dve.tensor_scalar(mean_sq[b][:, :], sum_sq[b][:, :], 1.0 / D, RMS_EPS,
                                      ALU.mult, ALU.add).then_inc(s_ms, 1)

                def scale_rms(n, b):
                    if isinstance(n, int) and n == 0:
                        dve.wait_ge(s_small, 16)
                    dve.wait_ge(s_rms, n + 1)
                    dve.scalar_tensor_tensor(out=z[b][:, :], in0=y[b][:, :], scalar=r_rms[b][:, 0:1],
                                             in1=rows[:, 1, :], op0=ALU.mult, op1=ALU.mult).then_inc(s_z, 1)

                def statistics(n, b):
                    dve.wait_ge(s_sum, n + 1)
                    dve.bn_stats(stats[:, :], z[b][:, :]).then_inc(s_stats, 1)
                    dve.wait_ge(s_stats, n + 1)
                    dve.memset(filler[:, :], 0.0)
                    dve.bn_aggr(mv[b][:, :], stats[:, :]).then_inc(s_mv, 1)
                    dve.wait_ge(s_mv, n + 1)
                    dve.tensor_scalar(var_eps[b][:, :], mv[b][:, 1:2], LN_EPS, None, ALU.add).then_inc(s_var, 1)

                def normalise(n, b, stores):
                    dve.wait_ge(s_rstd, n + 1)
                    wait(dve, s_store[b], stores)
                    dve.tensor_scalar(o_out[b][:, :], z[b][:, :], mv[b][:, 0:1], rstd[b][:, 0:1],
                                      ALU.subtract, ALU.mult).then_inc(s_o, 1)

                def finals(i, p, f):
                    for piece, lag in ((mean_square, 1), (scale_rms, 2), (statistics, 4)):
                        if 0 <= f - lag < GB:
                            piece(batches(i, p, f - lag) - GB, f - lag)
                    if 0 <= f - 6 < GB:
                        normalise(batches(i, p, f - 6) - GB, f - 6, i * 32 + 16 * (p - 1))

                def group(i, p):
                    if is_first(i, p):
                        hidden(0, 0)
                    for f in range(FC):
                        if not (is_last(i, p) and f == FC - 1):
                            hidden(chunks(i, p, f) + 1, (f + 1) % 2)
                        if f in T_STEP and not is_last(i, p):
                            transposed_lo(i, p + 1, T_STEP[f])
                        if not is_first(i, p):
                            finals(i, p, f)
                    sums(i, p)

                all_groups(dve, group)
                for f in range(FC):
                    finals(NG // 2, 0, f)

            @block.tensor
            def _(pe):
                def transposes(i, p, b, first=False):
                    if first:
                        pe.wait_ge(s_x2_in, 16 * GB)
                    else:
                        pe.wait_ge(s_x2[p % 2], i * 16 + 16 * (p // 2 + 1))
                        wait(pe, s_t_lo, batches(i, p, b))
                    src = x_ring[b][:, :] if first else x2_in[p % 2][:, b, :]
                    for k in range(KC):
                        mm = pe.transpose(t_bank(b, first)[:, k * 128:(k + 1) * 128],
                                          src[:, k * 128:(k + 1) * 128], ident[:, :])
                    mm.then_inc(s_t, 1)

                def hidden_product(n, p, par, f):
                    wait(pe, s_silu, n - 1)
                    c = slice(f * 128, (f + 1) * 128)
                    for k in range(KC):
                        pe.matmul(p_f1[par][:, :], w1_hi[:, k, c], xT_hi[p][:, k, :], start=(k == 0), stop=False)
                        pe.matmul(p_f1[par][:, :], w1_hi[:, k, c], xT_lo[p][:, k, :], start=False, stop=False)
                        mm = pe.matmul(p_f1[par][:, :], w1_lo[:, k, c], xT_hi[p][:, k, :], start=False, stop=(k == KC - 1))
                    mm.then_inc(s_f1, 1)

                def out_product(i, p, f):
                    n = chunks(i, p, f)
                    par = f % 2
                    pe.wait_ge(s_hid_lo, n + 1)
                    if is_first(i, p) and f % (FC // KC) == 0:
                        part = f // (FC // KC)
                        pe.wait_ge(s_wlo if part == 0 else s_wlo_pool, max(part, 1))
                    for b in range(GB):
                        if f == 0:
                            wait(pe, s_y, batches(i, p, b) - (GB - 1))
                        c = slice(b * S, (b + 1) * S)
                        pe.matmul(p_f2[b][:, 0:D], hid_hi[par][:, c], w2_hi[:, f, :], start=(f == 0), stop=False)
                        pe.matmul(p_f2[b][:, 0:D], hid_hi[par][:, c], w2_lo[:, f, :], start=False, stop=False)
                        mm = pe.matmul(p_f2[b][:, 0:D], hid_lo[par][:, c], w2_hi[:, f, :], start=False, stop=(f == FC - 1))
                        if b == GB - 1:
                            mm.then_inc(s_hid_used, 1)
                        elif f == FC - 1:
                            mm.then_inc(s_f2[b], 1)

                for b in range(GB):
                    transposes(0, 0, b, True)
                pe.wait_ge(s_t_lo, GB)

                def group(i, p):
                    if is_first(i, p):
                        hidden_product(0, 0, 0, 0)
                    for f in range(FC):
                        if f < FC - 1:
                            hidden_product(chunks(i, p, f) + 1, p, (f + 1) % 2, f + 1)
                        elif not is_last(i, p):
                            pe.wait_ge(s_t_lo, batches(i, p, GB) + GB)
                            hidden_product(chunks(i, p, f) + 1, 1 - p, 0, 0)
                        out_product(i, p, f)
                        if f in T_STEP and not is_last(i, p):
                            transposes(i, p + 1, T_STEP[f])

                all_groups(pe, group)


def make_constants(nc, ident, exponent):
    with nc.semaphore("k_s_const") as s_const, nc.Block() as block:

        @block.gpsimd
        def _(pool):
            pool.memset(ident[:, :], 0.0).then_inc(s_const, 1)
            pool.memset(exponent[:, :], -0.5)
            pool.wait_ge(s_const, 1)
            pool.affine_select(out=ident[:, :], in_=ident[:, :], compare_op=ALU.not_equal, fill=1.0,
                               base=0, pattern=[[-1, 128]], channel_multiplier=1)


def graph_stack_kernel(nc, x, x_T, adj, w_gcn, rows_gcn, w_attn, bqk, rows_at, w1, b1, w2, rows_ff, out):
    n_batch, S, D = x.shape
    F = b1.shape[0] * b1.shape[1]
    H = 2 * bqk.shape[3]
    KC = D // 128
    HP = 64
    x1 = nc.dram_tensor("x1_scratch", (n_batch, S, D), F32, kind="Internal").ap()
    x2 = nc.dram_tensor("x2_scratch", (n_batch, S, D), F32, kind="Internal").ap()
    with ExitStack() as ctx:
        def parts(name, cols, to):
            return [to.enter_context(nc.sbuf_tensor(f"{name}_{part}", [128, KC, cols], F32R)) for part in ("hi", "lo")]

        ident = ctx.enter_context(nc.sbuf_tensor("k_ident", [128, 128], F32))
        exponent = ctx.enter_context(nc.sbuf_tensor("k_exponent", [128, 1], F32))
        w1_split = parts("k_w1", F, ctx)
        make_constants(nc, ident, exponent)
        RING = 4
        x_ring = [ctx.enter_context(nc.sbuf_tensor(f"k_x_ring{s}", [128, D], F32)) for s in range(RING)]
        x_out = [ctx.enter_context(nc.sbuf_tensor(f"k_x_out{s}", [128, D], F32)) for s in range(2)]
        s_x1_in = [ctx.enter_context(nc.semaphore(f"s_x1_in{s}")) for s in range(RING)]
        s_x2_in = ctx.enter_context(nc.semaphore("s_x2_in"))
        s_x1_free = [ctx.enter_context(nc.semaphore(f"s_x1_free{s}")) for s in range(2)]
        s_x2_store = [ctx.enter_context(nc.semaphore(f"s_x2_store{s}")) for s in range(2)]
        x1_stores = [(s, 16 * (n_batch // 2 + 1)) for s in s_x1_free]
        x2_stores = [(s, 16 * (n_batch // 2)) for s in s_x2_store]
        with ExitStack() as attn:
            w_split = [parts(f"k_w{m}", cols, attn) for m, cols in (("q", H * HP), ("k", H * HP), ("v", D), ("o", D))]
            phase_graph_conv(nc, ident, exponent, x_ring, x_out, s_x1_free, s_x1_in, x, x_T, adj, w_gcn, rows_gcn, x1,
                             w_attn, w_split, n_batch, S, D, H)
            phase_attention(nc, ident, exponent, x_ring, x_out, s_x1_in, x1_stores, s_x2_in, s_x2_store, x1, adj,
                            w_split, bqk, rows_at, x2, w1, w1_split, n_batch, S, D, H)
        phase_feed_forward(nc, ident, exponent, x_ring, s_x2_in, x2_stores, x1, x2, w1_split, b1, w2, rows_ff, out,
                           n_batch, S, D, F)


_OUTS = [((64, 128, 384), 'float32')]


def _laid_out(t):
    import numpy as _np
    P, D, F, H, L = 128, 384, 1536, 8, 2
    KC, FC = D // P, F // P
    a = {n: _np.asarray(v) for n, v in t.items()}

    def every_partition(*rows):
        stacked = _np.stack(rows)
        return _np.broadcast_to(stacked, (P, *stacked.shape))

    w = _np.stack([a['L0_gnn_Wl'], a['L0_gnn_Wr'], a['L0_gnn_Ws']], 1)
    w_gcn = w.transpose(0, 1, 3, 2).reshape(L, 3, KC, P, D).transpose(0, 1, 3, 2, 4).reshape(L, 3, P, KC * D)
    rows_gcn = _np.stack([a['L0_gnn_bl'], a['L0_gnn_br'], a['L0_gnn_bs'], a['L0_gnn_ln_w'], a['L0_gnn_ln_b']], 1)
    return {
        'x': a['x'],
        'x_T': a['x'].reshape(-1, P, KC, P).transpose(0, 3, 2, 1),
        'adj': a['adj'],
        'w_gcn': w_gcn,
        'rows_gcn': _np.broadcast_to(rows_gcn[:, None], (L, P, 5, D)),
        'w_attn': _np.stack([a[f'L1_gnn_w{m}'] for m in 'qkvo']).reshape(4, KC, P, D).transpose(0, 2, 1, 3).reshape(4, P, KC * D),
        'bqk': _np.stack([a['L1_gnn_bq'], a['L1_gnn_bk']]).reshape(2, H // 2, 2, D // H).transpose(0, 2, 3, 1),
        'rows_at': every_partition(a['L1_gnn_bo'], a['L1_gnn_alpha1'], a['L1_gnn_gamma1'], a['L1_gnn_bv']),
        'w1': a['L1_gnn_w1'].reshape(KC, P, F),
        'b1': a['L1_gnn_b1'].reshape(FC, P).T,
        'w2': a['L1_gnn_w2'].reshape(KC, FC // KC, P, D).transpose(0, 2, 1, 3).reshape(KC, P, FC // KC * D),
        'rows_ff': every_partition(a['L1_gnn_b2'], a['L1_gnn_alpha2'], a['L1_gnn_gamma2']),
    }


def kernel(**inputs):
    import numpy as _np
    import concourse.bacc as _bacc
    from concourse import mybir as _mybir
    from concourse.bass_utils import run_bass_kernel_spmd as _run

    nc = _bacc.Bacc("TRN2", target_bir_lowering=False, num_devices=1)
    arrays, args = {}, []
    for name, a in _laid_out(inputs).items():
        a = _np.ascontiguousarray(a)
        arrays[f"in_{name}_dram"] = a
        args.append(nc.dram_tensor(f"in_{name}_dram", a.shape, _mybir.dt.from_np(a.dtype), kind="ExternalInput").ap())
    for i, (shape, dtype) in enumerate(_OUTS):
        dt = _mybir.dt.from_np(_np.dtype(dtype))
        args.append(nc.dram_tensor(f"out_{i}_dram", shape, dt, kind="ExternalOutput").ap())
    graph_stack_kernel(nc, *args)
    r = _run(nc, [arrays], core_ids=[0])
    got = tuple(r.results[0][f"out_{i}_dram"] for i in range(len(_OUTS)))
    return got[0]
```
